# Optimizing a Trainium2 kernel written in Bass

```python
import numpy as np
import jax
import jax.numpy as jnp

def _softmax(x, axis=-1):
    return jax.nn.softmax(x, axis=axis)

def _gelu(x):
    return jax.nn.gelu(x, approximate=True)

def _silu(x):
    return jax.nn.silu(x)

def _sigmoid(x):
    return jax.nn.sigmoid(x)

def _layernorm(x, axis=-1, eps=1e-05):
    m = jnp.mean(x, axis=axis, keepdims=True)
    v = jnp.var(x, axis=axis, keepdims=True)
    return (x - m) / jnp.sqrt(v + eps)

def _scatter_add(tgt, idx, src, axis=0):
    return tgt.at[idx].add(src)

def _segment_sum(src, seg, n):
    return jax.ops.segment_sum(src, seg, n)
kernel_name = 'mk_early_fusion_embed_d2_tok_img1024_r4_65f18f'

def setup_inputs(seed: int=0):
    np.random.seed(seed)
    _w = jnp.asarray

    def _rec_inputs():
        import jax
        import jax.numpy as jnp
        _rk = jax.random.key(seed)
        x = -0.00150118 + 0.499729 * jax.random.normal(jax.random.fold_in(_rk, 1), (8, 256, 64, 2), jnp.float32)
        x_txt = jax.random.randint(jax.random.fold_in(_rk, 51), (8, 77), 0, 12564, jnp.int32)
        return (x, x_txt)
    x, x_txt = _rec_inputs()

    def _L0_tok_setup():
        import jax, jax.numpy as jnp
        import numpy as np
        import math
        H = 256
        N = 64
        CH = 1
        SEQ_L = 256
        key = jax.random.key(seed)
        k1, k2, k3, k4 = jax.random.split(key, 4)
        log_dt = jax.random.uniform(k1, (H,), dtype=jnp.float32, minval=math.log(0.001), maxval=math.log(0.1))
        inv_A_real = jnp.log(0.5 * jnp.ones((H, N), jnp.float32)) + 0.1 * jax.random.normal(k2, (H, N), dtype=jnp.float32)
        A_imag = jnp.broadcast_to(math.pi * jnp.arange(N, dtype=jnp.float32), (H, N)).copy()
        B_ri = jax.random.normal(k3, (H, N, 2), dtype=jnp.float32) * 0.5
        C_ri = jax.random.normal(k4, (CH, H, N, 2), dtype=jnp.float32) * 0.5
        return {'log_dt': log_dt, 'inv_A_real': inv_A_real, 'A_imag': A_imag, 'B_ri': B_ri, 'C_ri': C_ri, 'L': SEQ_L}
    _L0_tok_all = _L0_tok_setup()
    _L0_tok_in = {k: v for k, v in _L0_tok_all.items() if k in ('log_dt', 'inv_A_real', 'A_imag', 'B_ri')}
    del _L0_tok_all

    def _L0_txt_setup():
        import jax, jax.numpy as jnp
        import numpy as np
        VOCAB = 50257
        CUTOFFS = [5000, 10000, 50257]
        BAND_DIMS = [256, 64, 64]
        OUT_DIM = 256
        PAD_IDX = 0
        key = jax.random.key(seed)
        ks = jax.random.split(key, 8)
        tokens = jax.random.randint(ks[0], (8, 1024), 0, VOCAB, dtype=jnp.int32)
        prev = 0
        params = {}
        for i, (c, d) in enumerate(zip(CUTOFFS, BAND_DIMS)):
            size = c - prev
            E = jax.random.normal(ks[1 + 2 * i], (size, d), dtype=jnp.float32) * d ** (-0.5)
            if i == 0:
                E = E.at[PAD_IDX].set(0.0)
            bound = float(np.sqrt(6.0 / (d + OUT_DIM)))
            W = jax.random.uniform(ks[2 + 2 * i], (d, OUT_DIM), dtype=jnp.float32, minval=-bound, maxval=bound)
            params[f'E{i}'] = E
            params[f'W{i}'] = W
            prev = c
        return {'tokens': tokens, **params}
    _L0_txt_all = _L0_txt_setup()
    _L0_txt_in = {k: v for k, v in _L0_txt_all.items() if k in ('E0', 'W0', 'E1', 'W1', 'E2', 'W2')}
    del _L0_txt_all

    def _L0_attn_setup():
        import jax, jax.numpy as jnp
        import numpy as np
        B, N, C, H = (4, 2048, 256, 16)
        D = C // H
        EPS = 1e-05
        key = jax.random.key(seed)
        ks = jax.random.split(key, 10)
        s = 1.0 / np.sqrt(C)
        return {'x': jax.random.normal(ks[0], (B, N, C), jnp.float32), 'Wq': jax.random.uniform(ks[1], (C, C), jnp.float32, -s, s), 'bq': jax.random.uniform(ks[2], (C,), jnp.float32, -s, s), 'Wk': jax.random.uniform(ks[3], (C, C), jnp.float32, -s, s), 'bk': jax.random.uniform(ks[4], (C,), jnp.float32, -s, s), 'Wv': jax.random.uniform(ks[5], (C, C), jnp.float32, -s, s), 'bv': jax.random.uniform(ks[6], (C,), jnp.float32, -s, s), 'Wo': jax.random.uniform(ks[7], (C, C), jnp.float32, -s, s), 'bo': jax.random.uniform(ks[8], (C,), jnp.float32, -s, s), 'ln_g': jnp.ones((C,), jnp.float32), 'ln_b': jnp.zeros((C,), jnp.float32)}
    _L0_attn_all = _L0_attn_setup()
    _L0_attn_in = {k: v for k, v in _L0_attn_all.items() if k in ('Wq', 'bq', 'Wk', 'bk', 'Wv', 'bv', 'Wo', 'bo', 'ln_g', 'ln_b')}
    del _L0_attn_all

    def _L0_ffn_setup():
        import jax, jax.numpy as jnp
        import numpy as np
        B, S, H, F, E, R, TOPK = (4, 512, 256, 1024, 4, 4, 2)

        def _more_forward(x, Wg, bg, W1, b1, W2, b2):
            b, s, h = x.shape
            cur = x
            for r in range(R):
                flat = cur.reshape(-1, h)
                logits = flat @ Wg[r] + bg[r]
                vals, idx = jax.lax.top_k(logits, TOPK)
                w = jax.nn.softmax(vals, axis=-1)
                cw = jnp.sum(jax.nn.one_hot(idx, E, dtype=flat.dtype) * w[..., None], axis=1)
                hmid = jax.nn.gelu(jnp.einsum('nh,ehf->enf', flat, W1) + b1[:, None, :])
                y = jnp.einsum('enf,efh->enh', hmid, W2) + b2[:, None, :]
                out = jnp.einsum('ne,enh->nh', cw, y)
                cur = cur + out.reshape(b, s, h)
            return cur
        key = jax.random.key(seed)
        ks = jax.random.split(key, 8)
        scale = 0.02
        return {'x': jax.random.normal(ks[0], (B, S, H), dtype=jnp.float32), 'Wg': jax.random.normal(ks[1], (R, H, E), dtype=jnp.float32) * scale, 'bg': jnp.zeros((R, E), dtype=jnp.float32), 'W1': jax.random.normal(ks[2], (E, H, F), dtype=jnp.float32) * scale, 'b1': jnp.zeros((E, F), dtype=jnp.float32), 'W2': jax.random.normal(ks[3], (E, F, H), dtype=jnp.float32) * scale, 'b2': jnp.zeros((E, H), dtype=jnp.float32)}
    _L0_ffn_all = _L0_ffn_setup()
    _L0_ffn_in = {k: v for k, v in _L0_ffn_all.items() if k in ('Wg', 'bg', 'W1', 'b1', 'W2', 'b2')}
    del _L0_ffn_all

    def _L1_attn_setup():
        import jax, jax.numpy as jnp
        import numpy as np
        import math
        D_MODEL = 256
        N_HEADS = 16
        D_HEAD = D_MODEL // N_HEADS
        DECAY_MAX = 0.99
        LN_EPS = 1e-05

        def _decay_mask(S):
            i = jnp.arange(S, dtype=jnp.float32)[:, None]
            j = jnp.arange(S, dtype=jnp.float32)[None, :]
            diff = i - j
            return jnp.where(diff >= 0, jnp.power(jnp.float32(DECAY_MAX), diff), 0.0)
        key = jax.random.key(seed)
        ks = jax.random.split(key, 12)
        B, S = (2, 512)
        x = jax.random.normal(ks[0], (B, S, D_MODEL), dtype=jnp.float32)

        def w(k):
            return jax.random.normal(k, (D_MODEL, D_MODEL), dtype=jnp.float32) * 0.02
        return {'x': x, 'Wq': w(ks[1]), 'bq': jnp.zeros((D_MODEL,), jnp.float32), 'Wk': w(ks[2]), 'bk': jnp.zeros((D_MODEL,), jnp.float32), 'Wv': w(ks[3]), 'bv': jnp.zeros((D_MODEL,), jnp.float32), 'Wg': w(ks[4]), 'bg': jnp.zeros((D_MODEL,), jnp.float32), 'Wo': w(ks[5]), 'bo': jnp.zeros((D_MODEL,), jnp.float32), 'gamma': jnp.ones((D_MODEL,), jnp.float32), 'beta': jnp.zeros((D_MODEL,), jnp.float32)}
    _L1_attn_all = _L1_attn_setup()
    _L1_attn_in = {k: v for k, v in _L1_attn_all.items() if k in ('Wq', 'bq', 'Wk', 'bk', 'Wv', 'bv', 'Wg', 'bg', 'Wo', 'bo', 'gamma', 'beta')}
    del _L1_attn_all

    def _L1_ffn_setup():
        import jax, jax.numpy as jnp
        import numpy as np
        B, S, H = (2, 512, 256)
        N, F, SF, K = (16, 256, 1024, 1)
        key = jax.random.key(seed)
        ks = jax.random.split(key, 7)
        std = 0.02
        return {'hidden_states': jax.random.normal(ks[0], (B, S, H), dtype=jnp.float32), 'router_w': jax.random.normal(ks[1], (N, H), dtype=jnp.float32) * std, 'gate_up_proj': jax.random.normal(ks[2], (N, H, 2 * F), dtype=jnp.float32) * std, 'down_proj': jax.random.normal(ks[3], (N, F, H), dtype=jnp.float32) * std, 'shared_gate_w': jax.random.normal(ks[4], (SF, H), dtype=jnp.float32) * std, 'shared_up_w': jax.random.normal(ks[5], (SF, H), dtype=jnp.float32) * std, 'shared_down_w': jax.random.normal(ks[6], (H, SF), dtype=jnp.float32) * std}
    _L1_ffn_all = _L1_ffn_setup()
    _L1_ffn_in = {k: v for k, v in _L1_ffn_all.items() if k in ('router_w', 'gate_up_proj', 'down_proj', 'shared_gate_w', 'shared_up_w', 'shared_down_w')}
    del _L1_ffn_all
    return {'x': x, 'x_txt': x_txt, 'L0_tok_log_dt': _L0_tok_in['log_dt'], 'L0_tok_inv_A_real': _L0_tok_in['inv_A_real'], 'L0_tok_A_imag': _L0_tok_in['A_imag'], 'L0_tok_B_ri': _L0_tok_in['B_ri'], 'L0_txt_E0': _L0_txt_in['E0'], 'L0_txt_W0': _L0_txt_in['W0'], 'L0_txt_E1': _L0_txt_in['E1'], 'L0_txt_W1': _L0_txt_in['W1'], 'L0_txt_E2': _L0_txt_in['E2'], 'L0_txt_W2': _L0_txt_in['W2'], 'L0_attn_Wq': _L0_attn_in['Wq'], 'L0_attn_bq': _L0_attn_in['bq'], 'L0_attn_Wk': _L0_attn_in['Wk'], 'L0_attn_bk': _L0_attn_in['bk'], 'L0_attn_Wv': _L0_attn_in['Wv'], 'L0_attn_bv': _L0_attn_in['bv'], 'L0_attn_Wo': _L0_attn_in['Wo'], 'L0_attn_bo': _L0_attn_in['bo'], 'L0_attn_ln_g': _L0_attn_in['ln_g'], 'L0_attn_ln_b': _L0_attn_in['ln_b'], 'L0_ffn_Wg': _L0_ffn_in['Wg'], 'L0_ffn_bg': _L0_ffn_in['bg'], 'L0_ffn_W1': _L0_ffn_in['W1'], 'L0_ffn_b1': _L0_ffn_in['b1'], 'L0_ffn_W2': _L0_ffn_in['W2'], 'L0_ffn_b2': _L0_ffn_in['b2'], 'L1_attn_Wq': _L1_attn_in['Wq'], 'L1_attn_bq': _L1_attn_in['bq'], 'L1_attn_Wk': _L1_attn_in['Wk'], 'L1_attn_bk': _L1_attn_in['bk'], 'L1_attn_Wv': _L1_attn_in['Wv'], 'L1_attn_bv': _L1_attn_in['bv'], 'L1_attn_Wg': _L1_attn_in['Wg'], 'L1_attn_bg': _L1_attn_in['bg'], 'L1_attn_Wo': _L1_attn_in['Wo'], 'L1_attn_bo': _L1_attn_in['bo'], 'L1_attn_gamma': _L1_attn_in['gamma'], 'L1_attn_beta': _L1_attn_in['beta'], 'L1_ffn_router_w': _L1_ffn_in['router_w'], 'L1_ffn_gate_up_proj': _L1_ffn_in['gate_up_proj'], 'L1_ffn_down_proj': _L1_ffn_in['down_proj'], 'L1_ffn_shared_gate_w': _L1_ffn_in['shared_gate_w'], 'L1_ffn_shared_up_w': _L1_ffn_in['shared_up_w'], 'L1_ffn_shared_down_w': _L1_ffn_in['shared_down_w']}

def reference(x, x_txt, L0_tok_log_dt, L0_tok_inv_A_real, L0_tok_A_imag, L0_tok_B_ri, L0_txt_E0, L0_txt_W0, L0_txt_E1, L0_txt_W1, L0_txt_E2, L0_txt_W2, L0_attn_Wq, L0_attn_bq, L0_attn_Wk, L0_attn_bk, L0_attn_Wv, L0_attn_bv, L0_attn_Wo, L0_attn_bo, L0_attn_ln_g, L0_attn_ln_b, L0_ffn_Wg, L0_ffn_bg, L0_ffn_W1, L0_ffn_b1, L0_ffn_W2, L0_ffn_b2, L1_attn_Wq, L1_attn_bq, L1_attn_Wk, L1_attn_bk, L1_attn_Wv, L1_attn_bv, L1_attn_Wg, L1_attn_bg, L1_attn_Wo, L1_attn_bo, L1_attn_gamma, L1_attn_beta, L1_ffn_router_w, L1_ffn_gate_up_proj, L1_ffn_down_proj, L1_ffn_shared_gate_w, L1_ffn_shared_up_w, L1_ffn_shared_down_w):
    import jax
    import jax.numpy as jnp

    def _L0_tok_ref(log_dt, inv_A_real, A_imag, B_ri, C_ri, L):
        import jax, jax.numpy as jnp
        import numpy as np
        import math
        H = 256
        N = 64
        CH = 1
        SEQ_L = 256
        dt = jnp.exp(log_dt)
        A = -jnp.exp(inv_A_real) + 1j * A_imag
        B = B_ri[..., 0] + 1j * B_ri[..., 1]
        C = C_ri[..., 0] + 1j * C_ri[..., 1]
        dtA = A * dt[:, None]
        dA = (1.0 + dtA / 2) / (1.0 - dtA / 2)
        C_term = C * B[None]
        log_dA = jnp.log(dA)
        V = jnp.exp(log_dA[:, :, None] * jnp.arange(L))
        K = 2.0 * jnp.einsum('chn,hnl->chl', C_term, V).real
        return K.astype(jnp.float32)

    def _L0_txt_ref(tokens, E0, W0, E1, W1, E2, W2):
        import jax, jax.numpy as jnp
        import numpy as np
        VOCAB = 50257
        CUTOFFS = [5000, 10000, 50257]
        BAND_DIMS = [256, 64, 64]
        OUT_DIM = 256
        PAD_IDX = 0
        Es = [E0, E1, E2]
        Ws = [W0, W1, W2]
        out = jnp.zeros(tokens.shape + (OUT_DIM,), dtype=jnp.float32)
        prev = 0
        for E, W, c in zip(Es, Ws, CUTOFFS):
            rel = jnp.clip(tokens - prev, 0, E.shape[0] - 1)
            emb = jnp.einsum('bsd,de->bse', E[rel], W)
            mask = (tokens >= prev) & (tokens < c)
            out = jnp.where(mask[..., None], emb, out)
            prev = c
        return out

    def _L0_attn_ref(x, Wq, bq, Wk, bk, Wv, bv, Wo, bo, ln_g, ln_b):
        import jax, jax.numpy as jnp
        import numpy as np
        B, N, C, H = (4, 2048, 256, 16)
        D = C // H
        EPS = 1e-05
        b, n, c = x.shape
        q = x @ Wq.T + bq
        k = x @ Wk.T + bk
        v = x @ Wv.T + bv
        split = lambda z: z.reshape(b, n, H, D).transpose(0, 2, 1, 3)
        q, k, v = (split(q), split(k), split(v))
        q = jax.nn.softmax(q, axis=-1)
        k = jax.nn.softmax(k, axis=-2)
        state = jnp.einsum('bhnd,bhne->bhde', k, v)
        out = jnp.einsum('bhnd,bhde->bhne', q, state)
        out = out.transpose(0, 2, 1, 3).reshape(b, n, c)
        mu = out.mean(-1, keepdims=True)
        var = out.var(-1, keepdims=True)
        out = (out - mu) * jax.lax.rsqrt(var + EPS) * ln_g + ln_b
        return out @ Wo.T + bo

    def _L0_ffn_ref(x, Wg, bg, W1, b1, W2, b2):
        import jax, jax.numpy as jnp
        import numpy as np
        B, S, H, F, E, R, TOPK = (4, 512, 256, 1024, 4, 4, 2)

        def _more_forward(x, Wg, bg, W1, b1, W2, b2):
            b, s, h = x.shape
            cur = x
            for r in range(R):
                flat = cur.reshape(-1, h)
                logits = flat @ Wg[r] + bg[r]
                vals, idx = jax.lax.top_k(logits, TOPK)
                w = jax.nn.softmax(vals, axis=-1)
                cw = jnp.sum(jax.nn.one_hot(idx, E, dtype=flat.dtype) * w[..., None], axis=1)
                hmid = jax.nn.gelu(jnp.einsum('nh,ehf->enf', flat, W1) + b1[:, None, :])
                y = jnp.einsum('enf,efh->enh', hmid, W2) + b2[:, None, :]
                out = jnp.einsum('ne,enh->nh', cw, y)
                cur = cur + out.reshape(b, s, h)
            return cur
        return _more_forward(x, Wg, bg, W1, b1, W2, b2)

    def _L1_attn_ref(x, Wq, bq, Wk, bk, Wv, bv, Wg, bg, Wo, bo, gamma, beta):
        import jax, jax.numpy as jnp
        import numpy as np
        import math
        D_MODEL = 256
        N_HEADS = 16
        D_HEAD = D_MODEL // N_HEADS
        DECAY_MAX = 0.99
        LN_EPS = 1e-05

        def _decay_mask(S):
            i = jnp.arange(S, dtype=jnp.float32)[:, None]
            j = jnp.arange(S, dtype=jnp.float32)[None, :]
            diff = i - j
            return jnp.where(diff >= 0, jnp.power(jnp.float32(DECAY_MAX), diff), 0.0)
        B, S, D = x.shape
        H, DH = (N_HEADS, D_HEAD)
        Q = (x @ Wq + bq).reshape(B, S, H, DH).transpose(0, 2, 1, 3)
        K = (x @ Wk + bk).reshape(B, S, H, DH).transpose(0, 2, 1, 3)
        V = (x @ Wv + bv).reshape(B, S, H, DH).transpose(0, 2, 1, 3)
        scores = jnp.einsum('bhsd,bhtd->bhst', Q, K) / math.sqrt(DH)
        mask = _decay_mask(S)
        retained = jnp.einsum('bhst,bhtd->bhsd', scores * mask, V)
        retained = retained.transpose(0, 2, 1, 3).reshape(B, S, D)
        mu = jnp.mean(retained, axis=-1, keepdims=True)
        var = jnp.var(retained, axis=-1, keepdims=True)
        normed = (retained - mu) * jax.lax.rsqrt(var + LN_EPS) * gamma + beta
        G = jax.nn.sigmoid(x @ Wg + bg)
        return normed * G @ Wo + bo

    def _L1_ffn_ref(hidden_states, router_w, gate_up_proj, down_proj, shared_gate_w, shared_up_w, shared_down_w):
        import jax, jax.numpy as jnp
        import numpy as np
        B, S, H = (2, 512, 256)
        N, F, SF, K = (16, 256, 1024, 1)
        b, s, h = hidden_states.shape
        hidden = hidden_states.reshape(-1, h)
        t = hidden.shape[0]
        logits = hidden @ router_w.T
        top_vals, top_idx = jax.lax.top_k(logits, K)
        scores = jnp.full_like(logits, -jnp.inf)
        scores = scores.at[jnp.arange(t)[:, None], top_idx].set(top_vals)
        scores = jax.nn.sigmoid(scores.astype(jnp.float32)).astype(hidden.dtype)
        routed_in = hidden[None, :, :] * scores.T[:, :, None]
        gate_up = jnp.einsum('nth,nhf->ntf', routed_in, gate_up_proj)
        gate, up = jnp.split(gate_up, 2, axis=-1)
        routed_out = jnp.einsum('ntf,nfh->nth', up * jax.nn.silu(gate), down_proj)
        expert_sum = routed_out.sum(axis=0)
        shared = jax.nn.silu(hidden @ shared_gate_w.T) * (hidden @ shared_up_w.T) @ shared_down_w.T
        return (shared + expert_sum).reshape(b, s, h)
    h = _L0_tok_ref(L0_tok_log_dt, L0_tok_inv_A_real, L0_tok_A_imag, L0_tok_B_ri, x, 256)
    h = jnp.concatenate([h, _L0_txt_ref(x_txt, L0_txt_E0, L0_txt_W0, L0_txt_E1, L0_txt_W1, L0_txt_E2, L0_txt_W2)], axis=1)
    h = h + _L0_attn_ref(_layernorm(h, axis=-1), L0_attn_Wq, L0_attn_bq, L0_attn_Wk, L0_attn_bk, L0_attn_Wv, L0_attn_bv, L0_attn_Wo, L0_attn_bo, L0_attn_ln_g, L0_attn_ln_b)
    h = h + _L0_ffn_ref(_layernorm(h, axis=-1), L0_ffn_Wg, L0_ffn_bg, L0_ffn_W1, L0_ffn_b1, L0_ffn_W2, L0_ffn_b2)
    h = h + _L1_attn_ref(_layernorm(h, axis=-1), L1_attn_Wq, L1_attn_bq, L1_attn_Wk, L1_attn_bk, L1_attn_Wv, L1_attn_bv, L1_attn_Wg, L1_attn_bg, L1_attn_Wo, L1_attn_bo, L1_attn_gamma, L1_attn_beta)
    h = h + _L1_ffn_ref(_layernorm(h, axis=-1), L1_ffn_router_w, L1_ffn_gate_up_proj, L1_ffn_down_proj, L1_ffn_shared_gate_w, L1_ffn_shared_up_w, L1_ffn_shared_down_w)
    return h

_drawn_inputs = setup_inputs


def setup_inputs(seed=0):
    import zlib

    import numpy as np

    out = dict(_drawn_inputs(seed))
    spreads = {'L0_attn_ln_g': (1.0, 0.2),
     'L0_attn_ln_b': (0.0, 0.381),
     'L0_ffn_bg': (0.0, 0.484),
     'L0_ffn_b1': (0.0, 0.422),
     'L0_ffn_b2': (0.0, 0.1),
     'L1_attn_bq': (0.0, 0.644),
     'L1_attn_bk': (0.0, 0.378),
     'L1_attn_bv': (0.0, 0.386),
     'L1_attn_bg': (0.0, 0.8),
     'L1_attn_bo': (0.0, 0.39),
     'L1_attn_gamma': (1.0, 0.6),
     'L1_attn_beta': (0.0, 0.8)}
    factors = {'L0_attn_bq': 8.0,
     'L0_attn_bk': 8.0,
     'L0_attn_bo': 3.986,
     'L1_attn_Wg': 8.0,
     'L1_ffn_router_w': 8.0,
     'L1_ffn_gate_up_proj': 8.0,
     'L1_ffn_down_proj': 8.0,
     'L1_ffn_shared_gate_w': 8.0,
     'L1_ffn_shared_up_w': 7.946,
     'L1_ffn_shared_down_w': 8.0}
    for name, (base, spread) in spreads.items():
        noise = np.random.default_rng([zlib.crc32(name.encode()), seed]).standard_normal(out[name].shape)
        drawn = base * np.exp(spread * noise) if base else spread * noise
        out[name] = jnp.asarray(drawn.astype(out[name].dtype))
    for name, factor in factors.items():
        out[name] = (out[name] * factor).astype(out[name].dtype)
    return out
```

```python
from contextlib import ExitStack, contextmanager

import concourse.bass as bass
from concourse import mybir

F32 = mybir.dt.float32
F32R = mybir.dt.float32r
I32 = mybir.dt.int32
U32 = mybir.dt.uint32
ALU = mybir.AluOpType
ACT = mybir.ActivationFunctionType
AX = mybir.AxisListType
ds = bass.ds

B, SSM_ROWS, TXT_ROWS, D = 8, 256, 77, 256
S = SSM_ROWS + TXT_ROWS
CHUNK = S // 3
NCH = S // CHUNK
NT = B * NCH
T = B * S
KC = D // 128
MODES = 64
NA, NB = 8, 32
CA = B * NA
HG = 16
CUT = (0, 5000, 10000, 50257)
TXT_AT = SSM_ROWS - (NCH - 1) * CHUNK
HEADS, DH = 16, 16
LN_EPS = 1e-05


class Chain:

    def __init__(self, eng, sem, start=0):
        self.eng, self.sem, self.start, self.n = eng, sem, start, 0

    def step(self, ins):
        ins.then_inc(self.sem, 1)
        self.n += 1

    def wait(self):
        self.eng.wait_ge(self.sem, self.start + self.n)


def exact_exp(c, out, x, power, rest):
    v = c.eng
    c.step(v.tensor_scalar(x, x, -87.0, 88.0, ALU.max, ALU.min))
    c.wait()
    c.step(v.tensor_scalar(power, x, 1.4426950408889634, 12582912.0, ALU.mult, ALU.add))
    c.wait()
    c.step(v.tensor_scalar(rest, power, 12582912.0, None, ALU.subtract))
    c.wait()
    c.step(v.scalar_tensor_tensor(x, rest, -0.693359375, x, ALU.mult, ALU.add))
    c.wait()
    c.step(v.scalar_tensor_tensor(x, rest, 2.12194440054690583e-4, x, ALU.mult, ALU.add))
    bits = power.bitcast(I32)
    c.step(v.tensor_scalar(bits, bits, 23, None, ALU.logical_shift_left))
    c.wait()
    c.step(v.tensor_scalar(bits, bits, 127 << 23, None, ALU.add))
    c.step(v.tensor_scalar(out, x, 1 / 5040, None, ALU.mult))
    for k in (720, 120, 24, 6, 2, 1):
        c.wait()
        c.step(v.scalar_tensor_tensor(out, out, 1 / k, x, ALU.add, ALU.mult))
    c.wait()
    c.step(v.scalar_tensor_tensor(out, out, 1.0, power, ALU.add, ALU.mult))
    c.wait()


@contextmanager
def cleared_semaphores(nc, prefix):
    sems = []

    def sem(name):
        sems.append(nc.alloc_semaphore(name=prefix + name))
        return sems[-1]

    yield sem
    nc.clear_and_free_semaphores(sems)
    nc.all_engine_barrier()


def embed_tokens(nc, io, h, ident, ident_ready):
    with ExitStack() as ctx:
        def sb(name, shape, dt=F32):
            return ctx.enter_context(nc.sbuf_tensor(name, shape, dt))

        def sem(name):
            return ctx.enter_context(nc.semaphore(name))

        pool_ram = sb("pool_ram", [128, 2 * B * D + NB // 2 * D])
        ssm_x = pool_ram[:, 0:2 * B * D].rearrange("p (s c h) -> p s c h", s=2, c=B)
        z_swap = pool_ram[:, 2 * B * D:].rearrange("p (b h) -> p b h", h=D)
        prod = pool_ram[0:CA].rearrange("p (h b) -> p h b", b=NB)
        left_h = sb("left_h", [128, 2, HG, CA])
        z_low = sb("z_low", [128, NB, D])
        left = sb("left", [128, B, NA, D])
        ct_im = sb("ct_im", [128, B, D])
        w_hi = sb("w_hi", [128, 2, NA, D])
        par = sb("par", [128, 5, D])
        tmp = sb("tmp", [128, 6, D])
        sq = sb("sq", [128, 5, 2, D])
        sign = sb("sign", [128, 1])
        loaded, params = sem("ssm_loaded"), sem("ssm_params")
        dve, pool = sem("ssm_dve"), sem("ssm_pool")
        left_done, low_done = sem("ssm_left"), sem("ssm_low")
        staged, multiplied, stored = sem("ssm_staged"), sem("ssm_multiplied"), sem("ssm_stored")
        turned, kept_even, kept_odd = sem("ssm_turned"), sem("ssm_kept_even"), sem("ssm_kept_odd")
        product = ctx.enter_context(nc.psum_tensor("ssm_product", [128, 2, HG, NB], F32))
        rows_ps = ctx.enter_context(nc.psum_tensor("ssm_rows", [128, 2, 8, CA], F32))
        block = ctx.enter_context(nc.Block())

        scratch = left[:].rearrange("p c a h -> p (c a) h")

        turns = [(j, g) for g in range(NB // 8) for j in range(NCH)]

        def rows_of(j):
            return min(CHUNK, D - j * CHUNK)

        def row_in(n, j):
            return rows_ps[0:rows_of(j), n % 2].rearrange("p b (c a) -> p c a b", a=NA)

        def row_out(j, g):
            out = h[0:rows_of(j)].rearrange("p (c j) (a b) -> p j c a b", j=NCH, b=NB)
            return out[:, j, :, :, 8 * g:8 * g + 8]

        @block.sync
        def _(sp):
            sp.dma_start(ident[:], io["ident"]).then_inc(ident_ready, 16)
            for half in range(2):
                rows = slice(64 * half, 64 * half + 64)
                sp.dma_start(par[rows, 0, :], io["log_dt"].rearrange("(o h) -> o h", o=1).broadcast_to([64, D])).then_inc(params, 16)
                sp.dma_start(par[rows, 1, :], io["inv_A_real"]).then_inc(params, 16)
                sp.dma_start(par[rows, 2, :], io["A_imag"]).then_inc(params, 16)
                sp.dma_start(par[rows, 3, :], io["B_ri"][0]).then_inc(params, 16)
                sp.dma_start(par[rows, 4, :], io["B_ri"][1]).then_inc(params, 16)
            sp.dma_start(sign[:], io["sign"]).then_inc(params, 16)
            sp.dma_start(ssm_x[:, 0], io["x"].rearrange("r n c h -> (r n) c h")).then_inc(loaded, 16)
            sp.dma_start(ssm_x[0:64, 1], io["x"][1]).then_inc(loaded, 16)
            sp.dma_start(ssm_x[64:128, 1], io["x"][0]).then_inc(loaded, 16)

        @block.scalar
        def _(act):
            act.wait_ge(left_done, NA)
            with act.Fori(0, D // HG // 2) as i:
                for p in range(2):
                    act.wait_ge(multiplied, i * 2 + p + 1)
                    nc.scalar.copy(left_h[:, p].rearrange("p h c -> p c h"),
                                   scratch[:, :, ds(i * 2 * HG + p * HG, HG)]).then_inc(staged, 1)
            for n, (j, g) in enumerate(turns):
                if n % 2:
                    act.wait_ge(turned, n + 1)
                    nc.scalar.copy(row_out(j, g), row_in(n, j)).then_inc(kept_odd, 1)

        @block.vector
        def _(v):
            c = Chain(v, dve)
            v.sem_inc(stored, 2)

            def tt(out, a, b, op):
                c.step(v.tensor_tensor(out, a, b, op))

            dt, ea, t2, t3, ur, ui = (tmp[:, k, :] for k in range(6))
            v.wait_ge(params, 16 * 11)
            exact_exp(c, tmp[:, 0:2, :], par[:, 0:2, :], tmp[:, 2:4, :], tmp[:, 4:6, :])
            c.step(v.scalar_tensor_tensor(ur, ea, -0.5, dt, ALU.mult, ALU.mult))
            c.step(v.scalar_tensor_tensor(ui, par[:, 2, :], 0.5, dt, ALU.mult, ALU.mult))
            c.wait()
            c.step(v.tensor_scalar(t2, ur, -1.0, 1.0, ALU.mult, ALU.add))
            tt(t3, ui, ui, ALU.mult)
            tt(ea, ur, ur, ALU.mult)
            c.wait()
            tt(t2, t2, t2, ALU.mult)
            tt(ea, ea, t3, ALU.add)
            c.wait()
            tt(t2, t2, t3, ALU.add)
            c.step(v.tensor_scalar(ea, ea, -1.0, 1.0, ALU.mult, ALU.add))
            c.wait()
            c.step(v.reciprocal(t2, t2))
            c.wait()
            tt(sq[:, 0, 0, :], ea, t2, ALU.mult)
            c.step(v.scalar_tensor_tensor(sq[:, 0, 1, :], ui, 2.0, t2, ALU.mult, ALU.mult))
            power = [(sq[:, k, 0, :], sq[:, k, 1, :]) for k in range(5)]
            power += [(w_hi[:, 0, a, :], w_hi[:, 1, a, :]) for a in (1, 2, 4)]
            for k in range(7):
                (re, im), (re2, im2) = power[k], power[k + 1]
                c.wait()
                tt(t2, re, re, ALU.mult)
                tt(t3, im, im, ALU.mult)
                c.step(v.scalar_tensor_tensor(im2, re, 2.0, im, ALU.mult, ALU.mult))
                c.wait()
                tt(re2, t2, t3, ALU.subtract)
            c.step(v.memset(w_hi[:, 0, 0, :], 1.0))
            c.step(v.memset(w_hi[:, 1, 0, :], 0.0))
            c.wait()
            for n, lo, by, to in ((1, 1, 2, 3), (3, 1, 4, 5)):
                ar, ai = w_hi[:, 0, lo:lo + n, :], w_hi[:, 1, lo:lo + n, :]
                br = w_hi[:, 0, by:by + 1, :].broadcast_to([128, n, D])
                bi = w_hi[:, 1, by:by + 1, :].broadcast_to([128, n, D])
                m = [scratch[:, 3 * k:3 * k + n, :] for k in range(4)]
                tt(m[0], ar, br, ALU.mult)
                tt(m[1], ai, bi, ALU.mult)
                tt(m[2], ar, bi, ALU.mult)
                tt(m[3], ai, br, ALU.mult)
                c.wait()
                tt(w_hi[:, 0, to:to + n, :], m[0], m[1], ALU.subtract)
                tt(w_hi[:, 1, to:to + n, :], m[2], m[3], ALU.add)
                c.wait()
            c.step(v.memset(z_low[0:64, 0, :], 1.0))
            c.step(v.memset(z_low[64:128, 0, :], 0.0))
            c.step(v.memset(z_swap[0:64, 0, :], 0.0))
            c.step(v.memset(z_swap[64:128, 0, :], 1.0))
            for k in range(5):
                n = 1 << k
                wr = sq[:, k, 0:1, :].broadcast_to([128, n, D])
                wi = sq[:, k, 1:2, :].broadcast_to([128, n, D])
                z0, s0 = z_low[:, 0:n, :], z_swap[:, 0:n, :]
                z1 = z_low[:, n:2 * n, :]
                ta, tb = scratch[:, 0:n, :], scratch[:, 16:16 + n, :]
                c.wait()
                tt(ta, s0, wi, ALU.mult)
                tt(z1, z0, wr, ALU.mult)
                if k < 4:
                    s1 = z_swap[:, n:2 * n, :]
                    tt(tb, z0, wi, ALU.mult)
                    tt(s1, s0, wr, ALU.mult)
                c.wait()
                tt(z1, z1, ta, ALU.add)
                if k < 4:
                    tt(s1, s1, tb, ALU.subtract)
            c.step(v.tensor_scalar(tmp[:, 0, :], par[:, 3, :], sign[:, 0:1], 2.0, ALU.mult, ALU.mult))
            c.step(v.tensor_scalar(tmp[:, 1, :], par[:, 4, :], 2.0, None, ALU.mult))
            c.step(v.tensor_scalar(tmp[:, 2, :], par[:, 3, :], -2.0, None, ALU.mult))
            c.step(v.tensor_scalar(tmp[:, 3, :], par[:, 4, :], sign[:, 0:1], -2.0, ALU.mult, ALU.mult))
            c.wait()
            v.wait_ge(loaded, 48)
            coef = [tmp[:, k:k + 1, :].broadcast_to([128, B, D]) for k in range(4)]
            x1, x2 = ssm_x[:, 0], ssm_x[:, 1]
            spare = left[:, :, 1, :]
            tt(left[:, :, 0, :], x1, coef[0], ALU.mult)
            tt(spare, x2, coef[1], ALU.mult)
            tt(ct_im[:], x2, coef[2], ALU.mult)
            c.wait()
            tt(left[:, :, 0, :], left[:, :, 0, :], spare, ALU.subtract)
            tt(left[:, :, 2, :], x1, coef[3], ALU.mult)
            c.wait()
            tt(ct_im[:], ct_im[:], left[:, :, 2, :], ALU.add)
            c.wait()
            for a in range(1, NA):
                wr = w_hi[:, 0, a:a + 1, :].broadcast_to([128, B, D])
                if a == 1:
                    v.sem_inc(left_done, 1)
                tt(left[:, :, a, :], left[:, :, 0, :], wr, ALU.mult)
                c.wait()
                v.wait_ge(pool, a)
                v.tensor_tensor(left[:, :, a, :], left[:, :, a, :], ssm_x[:, a % 2], ALU.add).then_inc(left_done, 1)
            v.wait_ge(left_done, NA)
            with v.Fori(0, D // HG // 2) as i:
                for p in range(2):
                    v.wait_ge(multiplied, i * 2 + p + 3)
                    v.tensor_copy(prod[:, ds(i * 2 * HG + p * HG, HG), :], product[0:CA, p]).then_inc(stored, 1)
            for n, (j, g) in enumerate(turns):
                if n % 2 == 0:
                    v.wait_ge(turned, n + 1)
                    v.tensor_copy(row_out(j, g), row_in(n, j)).then_inc(kept_even, 1)

        @block.tensor
        def _(pe):
            pe.sem_inc(multiplied, 2)
            with pe.Fori(0, D // HG // 2) as i:
                for p in range(2):
                    pe.wait_ge(staged, i * 2 + p + 1)
                    pe.wait_ge(stored, i * 2 + p + 1)
                    for k in range(HG):
                        mm = pe.matmul(product[0:CA, p, k, :], left_h[:, p, k, :],
                                       z_low[:, :, ds(i * 2 * HG + p * HG + k, 1)].rearrange("p b o -> p (b o)"),
                                       start=True, stop=True)
                    mm.then_inc(multiplied, 1)
            pe.wait_ge(stored, D // HG + 2)
            pe.wait_ge(ident_ready, 16)
            for n, (j, g) in enumerate(turns):
                if n >= 2:
                    pe.wait_ge(kept_odd if n % 2 else kept_even, n // 2)
                w = rows_of(j)
                for k in range(8):
                    mm = pe.transpose(rows_ps[0:w, n % 2, k, :], prod[:, j * CHUNK:j * CHUNK + w, 8 * g + k],
                                      ident[0:CA, 0:CA])
                mm.then_inc(turned, 1)

        @block.gpsimd
        def _(g):
            for a in range(1, NA):
                g.wait_ge(left_done, 1 if a < 3 else a - 1)
                wi = w_hi[:, 1, a:a + 1, :].broadcast_to([128, B, D])
                g.tensor_tensor(ssm_x[:, a % 2], ct_im[:], wi, ALU.mult).then_inc(pool, 1)


def embed_text(nc, io, h, ident, ident_ready):
    with ExitStack() as ctx:
        def sb(name, shape, dt=F32):
            return ctx.enter_context(nc.sbuf_tensor(name, shape, dt))

        def sem(name):
            return ctx.enter_context(nc.semaphore(name))

        NBAND = len(CUT) - 1
        col = (0, 256, 320, 384)
        KT = col[-1] // 128
        tokens = sb("txt_tokens", [TXT_ROWS, B], I32)
        row = sb("txt_row", [TXT_ROWS, NBAND, B], I32)
        inside = sb("txt_inside", [TXT_ROWS, NBAND, B])
        below = sb("txt_below", [TXT_ROWS, NBAND, B])
        emb = sb("txt_emb", [TXT_ROWS, B, col[-1]])
        masked = sb("txt_masked", [TXT_ROWS, 2, col[-1]])
        emb_t = sb("txt_emb_t", [128, 2, KT, TXT_ROWS])
        w = sb("txt_w", [128, KT, D])
        res = sb("txt_res", [TXT_ROWS, B, D])
        turn_ps = ctx.enter_context(nc.psum_tensor("txt_turn", [128, 2, 512], F32))
        out_ps = ctx.enter_context(nc.psum_tensor("txt_out", [128, 2, 512], F32))
        loaded, wloaded, dve, gathered = sem("txt_loaded"), sem("txt_wloaded"), sem("txt_dve"), sem("txt_gathered")
        masked_ok, turned, copied, multiplied = sem("txt_masked_ok"), sem("txt_turned"), sem("txt_copied"), sem("txt_mult")
        res_ok, placed = sem("txt_res_ok"), sem("txt_placed")
        block = ctx.enter_context(nc.Block())

        @block.sync
        def _(sp):
            sp.dma_start(tokens[:], io["x_txt"]).then_inc(loaded, 16)
            sp.dma_start(w[:], io["W_txt"]).then_inc(wloaded, 16)
            sp.wait_ge(res_ok, B)
            last = h[:].rearrange("p (c j) d -> p c j d", j=NCH)[TXT_AT:CHUNK, :, NCH - 1, :]
            sp.dma_start(last, res[:]).then_inc(placed, 16)
            sp.wait_ge(placed, 16)

        @block.gpsimd
        def _(g):
            g.wait_ge(dve, 3 * NBAND)
            for b in range(B):
                for k in range(NBAND):
                    g.indirect_dma_start(
                        emb[:, b, col[k]:col[k + 1]], None, io[f"E{k}"],
                        bass.IndirectOffsetOnAxis(ap=row[:, k, b:b + 1].bitcast(U32), axis=0)).then_inc(gathered, 16)

        @block.vector
        def _(v):
            c = Chain(v, dve)
            v.wait_ge(loaded, 16)
            for k in range(NBAND):
                c.step(v.tensor_scalar(row[:, k, :], tokens[:], -CUT[k], 0, ALU.add, ALU.max))
                c.step(v.tensor_scalar(inside[:, k, :], tokens[:], CUT[k], None, ALU.is_ge))
            c.wait()
            for k in range(NBAND):
                v.tensor_scalar(below[:, k, :], tokens[:], CUT[k + 1], None, ALU.is_lt)
                c.step(v.tensor_scalar(row[:, k, :], row[:, k, :], CUT[k + 1] - CUT[k] - 1, None, ALU.min))
            c.wait()
            c.step(v.tensor_tensor(inside[:], inside[:], below[:], ALU.mult))
            c.wait()
            v.wait_ge(gathered, 16 * NBAND * B)
            v.sem_inc(turned, 2)
            with v.Fori(0, B // 2) as i:
                for p in range(2):
                    v.wait_ge(turned, i * 2 + p + 1)
                    for k in range(NBAND):
                        ins = v.tensor_scalar(masked[:, p, col[k]:col[k + 1]],
                                              emb[:, ds(i * 2 + p, 1), col[k]:col[k + 1]].rearrange("p o d -> p (o d)"),
                                              inside[:, k, ds(i * 2 + p, 1)], None, ALU.mult)
                    ins.then_inc(masked_ok, 1)
                    v.wait_ge(multiplied, i * 2 + p + 1)
                    v.tensor_copy(res[:, ds(i * 2 + p, 1), :].rearrange("p o d -> p (o d)"),
                                  out_ps[0:TXT_ROWS, p, 0:D]).then_inc(res_ok, 1)

        @block.scalar
        def _(act):
            with act.Fori(0, B // 2) as i:
                for p in range(2):
                    act.wait_ge(turned, i * 2 + p + 3)
                    nc.scalar.copy(emb_t[:, p].rearrange("p k t -> p (k t)"),
                                   turn_ps[:, p, 0:KT * TXT_ROWS]).then_inc(copied, 1)

        @block.tensor
        def _(pe):
            pe.wait_ge(ident_ready, 16)
            pe.wait_ge(wloaded, 16)
            with pe.Fori(0, B // 2) as i:
                for p in range(2):
                    pe.wait_ge(masked_ok, i * 2 + p + 1)
                    for k in range(KT):
                        mm = pe.transpose(turn_ps[:, p, k * TXT_ROWS:(k + 1) * TXT_ROWS],
                                          masked[:, p, 128 * k:128 * k + 128], ident[0:TXT_ROWS, 0:TXT_ROWS])
                    mm.then_inc(turned, 1)
                    pe.wait_ge(copied, i * 2 + p + 1)
                    for k in range(KT):
                        mm = pe.matmul(out_ps[0:TXT_ROWS, p, 0:D], emb_t[:, p, k, :], w[:, k, :],
                                       start=(k == 0), stop=(k == KT - 1))
                    mm.then_inc(multiplied, 1)


def row_stats(c, src, stats, mv, n=NT):
    v = c.eng
    with v.Fori(0, n) as t:
        v.bn_stats(stats[:, ds(t, 1), :].rearrange("p o s -> p (o s)"),
                   src[:, ds(t, 1), :].rearrange("p o d -> p (o d)")).then_inc(c.sem, 1)
    c.n += n
    c.wait()
    mean, var = mv[:, :, 0], mv[:, :, 1]
    c.step(v.tensor_tensor(mean, stats[:, :, 1], stats[:, :, 4], ALU.add))
    c.step(v.tensor_tensor(var, stats[:, :, 1], stats[:, :, 4], ALU.subtract))
    c.step(v.tensor_tensor(stats[:, :, 0], stats[:, :, 2], stats[:, :, 5], ALU.add))
    c.wait()
    c.step(v.tensor_scalar(mean, mean, 0.5, None, ALU.mult))
    c.step(v.tensor_tensor(stats[:, :, 3], var, var, ALU.mult))
    c.step(v.tensor_scalar(stats[:, :, 0], stats[:, :, 0], 1 / D, None, ALU.mult))
    c.wait()
    c.step(v.scalar_tensor_tensor(var, stats[:, :, 3], 0.25, stats[:, :, 0], ALU.mult, ALU.add))
    c.wait()


def inverse_root(c, var_eps, root, inv, spare):
    v = c.eng
    c.step(v.reciprocal(inv, root))
    c.wait()
    c.step(v.tensor_tensor(spare, inv, inv, ALU.mult))
    c.wait()
    c.step(v.tensor_tensor(spare, spare, var_eps, ALU.mult))
    c.wait()
    c.step(v.tensor_scalar(spare, spare, -0.5, 1.5, ALU.mult, ALU.add))
    c.wait()
    c.step(v.tensor_tensor(inv, inv, spare, ALU.mult))
    c.wait()


def normalise(nc, name, src, dst_t, ident, ident_ready):
    with ExitStack() as ctx:
        def sb(what, shape, dt=F32):
            return ctx.enter_context(nc.sbuf_tensor(f"{name}_{what}", shape, dt))

        def sem(what):
            return ctx.enter_context(nc.semaphore(f"{name}_{what}"))

        stats = sb("stats", [CHUNK, NT, 6])
        mv = sb("mv", [CHUNK, NT, 2])
        small = sb("small", [CHUNK, 4, NT])
        rows = sb("rows", [CHUNK, 2, D])
        ps = ctx.enter_context(nc.psum_tensor(f"{name}_ps", [128, 2, 512], F32))
        dve, var_ready, root_done = sem("dve"), sem("var_ready"), sem("root_done")
        rows_ok, turned, copied = sem("rows_ok"), sem("turned"), sem("copied")
        block = ctx.enter_context(nc.Block())

        @block.vector
        def _(v):
            c = Chain(v, dve)
            row_stats(c, src, stats, mv)
            v.tensor_scalar(small[:, 0, :], mv[:, :, 1], LN_EPS, None, ALU.add).then_inc(var_ready, 1)
            v.wait_ge(root_done, 1)
            inverse_root(c, small[:, 0, :], small[:, 1, :], small[:, 2, :], small[:, 3, :])
            with v.Fori(0, NT // 2) as i:
                for p in range(2):
                    t = i * 2 + p
                    v.wait_ge(turned, t + 1)
                    v.tensor_scalar(rows[:, p, :], src[:, ds(t, 1), :].rearrange("p o d -> p (o d)"),
                                    mv[:, ds(t, 1), 0], small[:, 2, ds(t, 1)],
                                    ALU.subtract, ALU.mult).then_inc(rows_ok, 1)

        @block.scalar
        def _(act):
            act.wait_ge(var_ready, 1)
            nc.scalar.sqrt(small[:, 1, :], small[:, 0, :]).then_inc(root_done, 1)
            act.sem_inc(copied, 2)
            with act.Fori(0, NT // 2) as i:
                for p in range(2):
                    t = i * 2 + p
                    act.wait_ge(turned, t + 3)
                    nc.scalar.copy(dst_t[:, :, ds(t * CHUNK, CHUNK)],
                                   ps[:, p, 0:KC * CHUNK].rearrange("p (k t) -> p k t", k=KC)).then_inc(copied, 1)

        @block.tensor
        def _(pe):
            pe.wait_ge(ident_ready, 16)
            pe.sem_inc(turned, 2)
            with pe.Fori(0, NT // 2) as i:
                for p in range(2):
                    t = i * 2 + p
                    pe.wait_ge(rows_ok, t + 1)
                    pe.wait_ge(copied, t + 1)
                    for k in range(KC):
                        mm = pe.transpose(ps[:, p, k * CHUNK:(k + 1) * CHUNK], rows[:, p, 128 * k:128 * k + 128],
                                          ident[0:CHUNK, 0:CHUNK])
                    mm.then_inc(turned, 1)


def linear_attention(nc, io, h, x_t, ident, ident_ready):
    with ExitStack() as ctx:
        def sb(name, shape, dt=F32):
            return ctx.enter_context(nc.sbuf_tensor("la_" + name, shape, dt))

        sem = ctx.enter_context(cleared_semaphores(nc, "la_"))

        qv = sb("qv", [CHUNK, NT, 2 * D])
        k_t = sb("k_t", [128, KC, B, S])
        out = sb("out", [CHUNK, NT, D])
        w_qv = sb("w_qv", [128, KC, 2 * D])
        w_k = sb("w_k", [128, KC, D])
        w_o = sb("w_o", [128, KC, D])
        b_qv = sb("b_qv", [CHUNK, 2 * D])
        b_o = sb("b_o", [CHUNK, D])
        cols = sb("cols", [128, 3, KC])
        head_mask = sb("head_mask", [128, 128])
        x_s = sb("x_s", [128, 2, KC, CHUNK])
        k_max = sb("k_max", [128, KC, B])
        k_sum = sb("k_sum", [128, KC, B])
        k_inv = sb("k_inv", [128, KC, B])
        k_exp = sb("k_exp", [128, 2, S])
        k_rows = sb("k_rows", [CHUNK, 2, NCH, 128])
        q_rows = sb("q_rows", [CHUNK, 2, NCH, 128])
        q_t = sb("q_t", [128, 2, NCH, CHUNK])
        state = sb("state", [128, 2, 128])
        q_red = sb("q_red", [CHUNK, NT, HEADS])
        q_inv = sb("q_inv", [CHUNK, NT, HEADS])
        stats = sb("stats", [CHUNK, NT, 6])
        mv = sb("mv", [CHUNK, NT, 2])
        small = sb("small", [CHUNK, 4, NT])
        loaded, dve, x_copied, projected = sem("loaded"), sem("dve"), sem("x_copied"), sem("projected")
        qv_ok, k_mult, k_ok, k_max_ok = sem("qv_ok"), sem("k_mult"), sem("k_ok"), sem("k_max_ok")
        q_sub, q_exp, k_exp_ok, k_turned = sem("q_sub"), sem("q_exp"), sem("k_exp_ok"), sem("k_turned")
        k_rows_ok, q_rows_ok, q_turned, q_t_ok = sem("k_rows_ok"), sem("q_rows_ok"), sem("q_turned"), sem("q_t_ok")
        state_mult, state_ok, out_mult, out_ok = sem("state_mult"), sem("state_ok"), sem("out_mult"), sem("out_ok")
        var_ready, root_done, n_ok, n_turned = sem("var_ready"), sem("root_done"), sem("n_ok"), sem("n_turned")
        n_t_ok, o_mult, h_ok, bias_added = sem("n_t_ok"), sem("o_mult"), sem("h_ok"), sem("bias_added")
        k_inv_ok = sem("k_inv_ok")
        ps = ctx.enter_context(nc.psum_tensor("la_ps", [128, 8, 512], F32))
        block = ctx.enter_context(nc.Block())
        NQ = 4
        TQ = NT // NQ

        def heads(ap):
            return ap.rearrange("p t (g e) -> p t g e", e=DH)

        def q_part(n):
            return heads(qv[:, TQ * n:TQ * n + TQ, 0:D])

        @block.sync
        def _(sp):
            sp.dma_start(w_qv[:], io["la_w_qv"]).then_inc(loaded, 16)
            sp.dma_start(w_k[:], io["la_w_k"]).then_inc(loaded, 16)
            sp.dma_start(w_o[:], io["la_w_o"]).then_inc(loaded, 16)
            sp.dma_start(b_qv[:], io["la_b_qv"].broadcast_to([CHUNK, 2 * D])).then_inc(loaded, 16)
            sp.dma_start(b_o[:], io["la_b_o"].broadcast_to([CHUNK, D])).then_inc(loaded, 16)
            sp.dma_start(cols[:], io["la_cols"]).then_inc(loaded, 16)
            sp.dma_start(head_mask[:], io["head_mask"]).then_inc(loaded, 16)

        @block.gpsimd
        def _(g):
            with g.Fori(0, NT // 2) as i:
                for p in range(2):
                    t = i * 2 + p
                    g.wait_ge(projected, t + 1)
                    g.tensor_copy(x_s[:, p], x_t[:, :, ds(t * CHUNK, CHUNK)]).then_inc(x_copied, 1)
            g.wait_ge(loaded, 16 * 7)
            g.tensor_tensor(h[:], h[:], b_o[:].unsqueeze(1).broadcast_to([CHUNK, NT, D]), ALU.add).then_inc(bias_added, 1)

        @block.tensor
        def _(pe):
            for s in (projected, k_turned, state_mult, q_turned, out_mult, n_turned, o_mult):
                pe.sem_inc(s, 2)
            pe.wait_ge(loaded, 16 * 7)
            pe.wait_ge(ident_ready, 16)
            with pe.Fori(0, NT // 2) as i:
                for p in range(2):
                    t = i * 2 + p
                    pe.wait_ge(x_copied, t + 1)
                    pe.wait_ge(qv_ok, t + 1)
                    for k in range(KC):
                        mm = pe.matmul(ps[0:CHUNK, p, :], x_s[:, p, k, :], w_qv[:, k, :], start=(k == 0), stop=(k == KC - 1))
                    mm.then_inc(projected, 1)
            with pe.Fori(0, B) as b:
                for m in range(KC):
                    pe.wait_ge(k_ok, b * KC + m + 1)
                    for k in range(KC):
                        mm = pe.matmul(ps[:, 2 + m, 0:S], w_k[:, k, 128 * m:128 * m + 128],
                                       x_t[:, k, ds(b * S, S)], start=(k == 0), stop=(k == KC - 1))
                    mm.then_inc(k_mult, 1)
            pe.wait_ge(qv_ok, NT + 2)
            pe.wait_ge(k_ok, B * KC + 2)
            with pe.Fori(0, B) as b:
                for m in range(KC):
                    pe.wait_ge(k_exp_ok, b * KC + m + 1)
                    pe.wait_ge(k_rows_ok, b * KC + m + 1)
                    for j in range(NCH):
                        mm = pe.transpose(ps[0:CHUNK, m, 128 * j:128 * j + 128], k_exp[:, m, j * CHUNK:(j + 1) * CHUNK],
                                          ident[:])
                    mm.then_inc(k_turned, 1)
                for m in range(KC):
                    pe.wait_ge(q_rows_ok, b * KC + m + 1)
                    pe.wait_ge(q_t_ok, b * KC + m + 1)
                    for j in range(NCH):
                        mm = pe.transpose(ps[:, 2 + m, CHUNK * j:CHUNK * (j + 1)], q_rows[:, m, j, :],
                                          ident[0:CHUNK, 0:CHUNK])
                    mm.then_inc(q_turned, 1)
                for m in range(KC):
                    pe.wait_ge(k_rows_ok, b * KC + m + 3)
                    pe.wait_ge(state_ok, b * KC + m + 1)
                    for j in range(NCH):
                        mm = pe.matmul(ps[:, 4 + m, 0:128], k_rows[:, m, j, :],
                                       qv[:, ds(b * NCH + j, 1), D + 128 * m:D + 128 * m + 128].rearrange("p o d -> p (o d)"),
                                       start=(j == 0), stop=(j == NCH - 1))
                    mm.then_inc(state_mult, 1)
                for m in range(KC):
                    pe.wait_ge(state_ok, b * KC + m + 3)
                    pe.wait_ge(q_t_ok, b * KC + m + 3)
                    pe.wait_ge(out_ok, b * KC + m + 1)
                    for j in range(NCH):
                        mm = pe.matmul(ps[0:CHUNK, 6 + m, 128 * j:128 * j + 128], q_t[:, m, j, :], state[:, m, :],
                                       start=True, stop=True)
                    mm.then_inc(out_mult, 1)
            with pe.Fori(0, NT // 2) as i:
                for p in range(2):
                    t = i * 2 + p
                    pe.wait_ge(n_ok, t + 1)
                    pe.wait_ge(n_t_ok, t + 1)
                    for k in range(KC):
                        mm = pe.transpose(ps[:, p, k * CHUNK:(k + 1) * CHUNK], q_rows[:, p, k, :],
                                          ident[0:CHUNK, 0:CHUNK])
                    mm.then_inc(n_turned, 1)
                for p in range(2):
                    t = i * 2 + p
                    pe.wait_ge(n_t_ok, t + 3)
                    pe.wait_ge(h_ok, t + 1)
                    for k in range(KC):
                        mm = pe.matmul(ps[0:CHUNK, 2 + p, 0:D], x_s[:, p, k, :], w_o[:, k, :],
                                       start=(k == 0), stop=(k == KC - 1))
                    mm.then_inc(o_mult, 1)

        @block.scalar
        def _(act):
            for s in (k_ok, q_t_ok, out_ok, n_t_ok):
                act.sem_inc(s, 2)
            act.wait_ge(loaded, 16 * 7)
            with act.Fori(0, B) as b:
                for m in range(KC):
                    act.wait_ge(k_mult, b * KC + m + 1)
                    nc.scalar.activation(k_t[:, m, ds(b, 1), :].rearrange("p o s -> p (o s)"), ps[:, 2 + m, 0:S],
                                         ACT.Identity, bias=cols[:, 0, m:m + 1]).then_inc(k_ok, 1)
            for n in range(NQ):
                act.wait_ge(q_sub, n + 1)
                nc.scalar.activation(q_part(n), q_part(n), ACT.Exp).then_inc(q_exp, 1)
            act.wait_ge(k_max_ok, 1)
            with act.Fori(0, B) as b:
                for m in range(KC):
                    act.wait_ge(k_turned, b * KC + m + 1)
                    nc.scalar.activation(k_exp[:, m, :], k_t[:, m, ds(b, 1), :].rearrange("p o s -> p (o s)"),
                                         ACT.Exp, bias=k_max[:, m, ds(b, 1)],
                                         accum_out=k_sum[:, m, ds(b, 1)]).then_inc(k_exp_ok, 1)
                for m in range(KC):
                    act.wait_ge(q_turned, b * KC + m + 3)
                    act.wait_ge(out_mult, b * KC + m + 1)
                    nc.scalar.copy(q_t[:, m].rearrange("p j t -> p (j t)"), ps[:, 2 + m, 0:S]).then_inc(q_t_ok, 1)
                for m in range(KC):
                    act.wait_ge(out_mult, b * KC + m + 3)
                    nc.scalar.copy(out[:, ds(b * NCH, NCH), 128 * m:128 * m + 128],
                                   ps[0:CHUNK, 6 + m, 0:NCH * 128].rearrange("p (j e) -> p j e", j=NCH)).then_inc(out_ok, 1)
            act.wait_ge(var_ready, 1)
            nc.scalar.sqrt(small[:, 1, :], small[:, 0, :]).then_inc(root_done, 1)
            with act.Fori(0, NT // 2) as i:
                for p in range(2):
                    t = i * 2 + p
                    act.wait_ge(n_turned, t + 3)
                    act.wait_ge(o_mult, t + 1)
                    for k in range(KC):
                        ins = nc.scalar.activation(x_s[:, p, k, :], ps[:, p, k * CHUNK:(k + 1) * CHUNK], ACT.Identity,
                                                   bias=cols[:, 2, k:k + 1], scale=cols[:, 1, k:k + 1])
                    ins.then_inc(n_t_ok, 1)

        @block.vector
        def _(v):
            c = Chain(v, dve)
            for s in (qv_ok, k_rows_ok, state_ok, h_ok):
                v.sem_inc(s, 2)
            v.wait_ge(loaded, 16 * 7)
            with v.Fori(0, NT // 2) as i:
                for p in range(2):
                    t = i * 2 + p
                    v.wait_ge(projected, t + 3)
                    v.tensor_tensor(qv[:, ds(t, 1), :].rearrange("p o d -> p (o d)"), ps[0:CHUNK, p, :], b_qv[:],
                                    ALU.add).then_inc(qv_ok, 1)
            v.wait_ge(qv_ok, NT + 2)
            for n in range(NQ):
                red = q_red[:, TQ * n:TQ * n + TQ, :]
                c.step(v.tensor_reduce(red, q_part(n), AX.X, ALU.max))
                c.wait()
                v.tensor_tensor(q_part(n), q_part(n), red.unsqueeze(3).broadcast_to([CHUNK, TQ, HEADS, DH]),
                                ALU.subtract).then_inc(q_sub, 1)
            v.wait_ge(k_ok, B * KC + 2)
            c.step(v.tensor_reduce(k_max[:], k_t[:], AX.X, ALU.max))
            c.wait()
            v.tensor_scalar(k_max[:], k_max[:], -1.0, None, ALU.mult).then_inc(k_max_ok, 1)
            for n in range(NQ):
                v.wait_ge(q_exp, n + 1)
                c.step(v.tensor_reduce(q_red[:, TQ * n:TQ * n + TQ, :], q_part(n), AX.X, ALU.add))
            c.wait()
            c.step(v.reciprocal(q_inv[:], q_red[:]))
            c.wait()
            with v.Fori(0, B) as b:
                for m in range(KC):
                    v.wait_ge(q_turned, b * KC + m + 1)
                    v.tensor_tensor(q_rows[:, m].rearrange("p j (g e) -> p j g e", e=DH),
                                    heads(qv[:, ds(b * NCH, NCH), 128 * m:128 * m + 128]),
                                    q_inv[:, ds(b * NCH, NCH), 8 * m:8 * m + 8].unsqueeze(3).broadcast_to([CHUNK, NCH, 8, DH]),
                                    ALU.mult).then_inc(q_rows_ok, 1)
                for m in range(KC):
                    v.wait_ge(k_turned, b * KC + m + 3)
                    v.wait_ge(state_mult, b * KC + m + 1)
                    v.tensor_copy(k_rows[:, m].rearrange("p j e -> p (j e)"), ps[0:CHUNK, m, 0:NCH * 128]).then_inc(k_rows_ok, 1)
                    v.wait_ge(k_exp_ok, b * KC + m + 1)
                    v.reciprocal(k_inv[:, m, ds(b, 1)], k_sum[:, m, ds(b, 1)]).then_inc(k_inv_ok, 1)
                for m in range(KC):
                    v.wait_ge(state_mult, b * KC + m + 3)
                    v.wait_ge(out_mult, b * KC + m + 1)
                    v.wait_ge(k_inv_ok, b * KC + m + 1)
                    v.scalar_tensor_tensor(state[:, m, :], ps[:, 4 + m, 0:128], k_inv[:, m, ds(b, 1)], head_mask[:],
                                           ALU.mult, ALU.mult).then_inc(state_ok, 1)
            v.wait_ge(out_ok, B * KC + 2)
            row_stats(c, out, stats, mv)
            v.tensor_scalar(small[:, 0, :], mv[:, :, 1], LN_EPS, None, ALU.add).then_inc(var_ready, 1)
            v.wait_ge(root_done, 1)
            inverse_root(c, small[:, 0, :], small[:, 1, :], small[:, 2, :], small[:, 3, :])
            v.wait_ge(bias_added, 1)
            with v.Fori(0, NT // 2) as i:
                for p in range(2):
                    t = i * 2 + p
                    v.wait_ge(n_turned, t + 1)
                    v.tensor_scalar(q_rows[:, p, 0:KC, :].rearrange("p k e -> p (k e)"),
                                    out[:, ds(t, 1), :].rearrange("p o d -> p (o d)"),
                                    mv[:, ds(t, 1), 0], small[:, 2, ds(t, 1)],
                                    ALU.subtract, ALU.mult).then_inc(n_ok, 1)
                for p in range(2):
                    t = i * 2 + p
                    v.wait_ge(o_mult, t + 3)
                    row = h[:, ds(t, 1), :].rearrange("p o d -> p (o d)")
                    v.tensor_tensor(row, row, ps[0:CHUNK, 2 + p, 0:D], ALU.add).then_inc(h_ok, 1)


EXPERTS, ROUNDS, FF = 4, 4, 1024
FT = FF // 128
TW = 444
NP = T // TW // 2
TC = TW // CHUNK
WCHUNK = 1024
NW = 2 * EXPERTS * KC * FF // WCHUNK


def split_weights(nc, io, w_hi, w_lo, x_t, x_dram):
    with ExitStack() as ctx:
        stage = ctx.enter_context(nc.sbuf_tensor("mw_stage", [128, 2, WCHUNK], F32))
        loaded = [ctx.enter_context(nc.semaphore(f"mw_loaded{p}")) for p in range(2)]
        x_stored = ctx.enter_context(nc.semaphore("mw_x_stored"))
        hi_ok = ctx.enter_context(nc.semaphore("mw_hi_ok"))
        lo_ok = ctx.enter_context(nc.semaphore("mw_lo_ok"))
        block = ctx.enter_context(nc.Block())

        @block.gpsimd
        def _(g):
            g.dma_start(x_dram, x_t[:]).then_inc(x_stored, 16)
            g.wait_ge(x_stored, 16)

        @block.sync
        def _(sp):
            with sp.Fori(0, NW // 2) as i:
                for p in range(2):
                    sp.wait_ge(lo_ok, i * 2 + p + 1)
                    sp.dma_start(stage[:, p, :], io["mo_w"][:, ds((i * 2 + p) * WCHUNK, WCHUNK)]).then_inc(loaded[p], 16)

        @block.scalar
        def _(act):
            with act.Fori(0, NW // 2) as i:
                for p in range(2):
                    act.wait_ge(loaded[p], i * 16 + 16)
                    nc.scalar.copy(w_hi[:, ds((i * 2 + p) * WCHUNK, WCHUNK)], stage[:, p, :]).then_inc(hi_ok, 1)

        @block.vector
        def _(v):
            v.sem_inc(lo_ok, 2)
            with v.Fori(0, NW // 2) as i:
                for p in range(2):
                    v.wait_ge(hi_ok, i * 2 + p + 1)
                    v.tensor_tensor(w_lo[:, ds((i * 2 + p) * WCHUNK, WCHUNK)], stage[:, p, :],
                                    w_hi[:, ds((i * 2 + p) * WCHUNK, WCHUNK)].bitcast(F32),
                                    ALU.subtract).then_inc(lo_ok, 1)


def recursive_mixture(nc, io, h, x_dram, w_hi, w_lo, ident):
    with ExitStack() as ctx:
        def sb(name, shape, dt=F32):
            return ctx.enter_context(nc.sbuf_tensor("mo_" + name, shape, dt))

        def sem(name):
            return ctx.enter_context(nc.semaphore("mo_" + name))

        K = EXPERTS * FT
        LAG = 2
        cur = sb("cur", [128, 2, KC, TW])
        x_hi = sb("x_hi", [128, 2, KC, TW], F32R)
        x_lo = sb("x_lo", [128, 2, KC, TW], F32R)
        g = sb("g", [128, 2, TW])
        g_hi = sb("g_hi", [128, 2, TW], F32R)
        g_lo = sb("g_lo", [128, 2, TW], F32R)
        cw_t = sb("cw_t", [EXPERTS, 2, TW])
        w_g = sb("w_g", [128, KC, ROUNDS + 1, EXPERTS])
        b_g = sb("b_g", [CHUNK, ROUNDS + 1, EXPERTS])
        b_1 = sb("b_1", [128, K])
        b_2 = sb("b_2", [EXPERTS, D])
        one_row = sb("one_row", [EXPERTS, EXPERTS, 128])
        before = sb("before", [CHUNK, 2, EXPERTS, EXPERTS])
        lg = sb("lg", [CHUNK, TC, EXPERTS])
        cmp = sb("cmp", [CHUNK, 2, TC, EXPERTS, EXPERTS])
        rank = sb("rank", [CHUNK, 3, TC, EXPERTS])
        total = sb("total", [CHUNK, TC])
        cw = sb("cw", [CHUNK, TC, EXPERTS])
        ps = ctx.enter_context(nc.psum_tensor("mo_ps", [128, 8, 512], F32))
        HID, CWB, Y, GATE, TURN = 0, 2, 4, 6, 7
        loaded, gate_mult = sem("loaded"), sem("gate_mult")
        cur_loaded = [sem("cur_loaded0"), sem("cur_loaded1")]
        x_hi_ok, x_lo_ok, gate_dve = sem("x_hi_ok"), sem("x_lo_ok"), sem("gate_dve")
        arg_ok, tanh_ok, cw_ok, cw_turned, cw_t_ok = sem("arg_ok"), sem("tanh_ok"), sem("cw_ok"), sem("cw_turned"), sem("cw_t_ok")
        cw_spread, hid_mult, gelu_ok, s_ok = sem("cw_spread"), sem("hid_mult"), sem("gelu_ok"), sem("s_ok")
        hi_ok, lo_ok, y_mult, y_done, cur_ok = sem("hi_ok"), sem("lo_ok"), sem("y_mult"), sem("y_done"), sem("cur_ok")
        back_turned, h_ok = sem("back_turned"), sem("h_ok")
        block = ctx.enter_context(nc.Block())
        w1 = [w[:, 0:NW * WCHUNK // 2].rearrange("p (e k f) -> p e k f", e=EXPERTS, k=KC) for w in (w_hi, w_lo)]
        w2 = [w[:, NW * WCHUNK // 2:].rearrange("p (e f d) -> p e f d", e=EXPERTS, f=FT) for w in (w_hi, w_lo)]
        GATE_STEPS = 11
        PREPS = 2 * ROUNDS + 1
        S_FREE = 9

        @block.sync
        def _(sp):
            for dst, name in ((w_g, "mo_w_g"), (b_1, "mo_b_1"), (b_2, "mo_b_2"), (one_row, "one_row")):
                sp.dma_start(dst[:], io[name]).then_inc(loaded, 16)
            sp.dma_start(b_g[:], io["mo_b_g"].broadcast_to([CHUNK, ROUNDS + 1, EXPERTS])).then_inc(loaded, 16)
            sp.dma_start(before[:], io["before"].broadcast_to([CHUNK, 2, EXPERTS, EXPERTS])).then_inc(loaded, 16)
            with sp.Fori(0, NP) as i:
                for p in range(2):
                    sp.wait_ge(back_turned, i * 2 + p + 1)
                    sp.dma_start(cur[:, p], x_dram[:, :, ds(i * 2 * TW + p * TW, TW)]).then_inc(cur_loaded[p], 16)

        def cur_is(eng, i, r, p):
            if r is None:
                eng.wait_ge(cur_loaded[0], i * 16 + 16)
            elif p == 0:
                eng.wait_ge(cur_loaded[1], i * 16 + 16)
                eng.wait_ge(cur_ok, i * 8 + r * 2 + 1)
            else:
                eng.wait_ge(cur_ok, i * 8 + r * 2 + 2)

        @block.tensor
        def _(pe):
            for s, n in ((back_turned, 2), (y_mult, 2)):
                pe.sem_inc(s, n)
            pe.wait_ge(loaded, 16 * 6)

            def gate(i, r, p, prep, nxt, to):
                cur_is(pe, i, r, p)
                pe.wait_ge(cw_ok, prep + 1)
                pe.wait_ge(h_ok, i * 2 + 1)
                for c in range(TC):
                    for k in range(KC):
                        mm = pe.matmul(ps[0:CHUNK, GATE, 4 * c:4 * c + 4], cur[:, to, k, c * CHUNK:(c + 1) * CHUNK],
                                       w_g[:, k, ds(nxt, 1), :].rearrange("p o e -> p (o e)"),
                                       start=(k == 0), stop=(k == KC - 1))
                mm.then_inc(gate_mult, 1)

            def turn_cw(prep):
                pe.wait_ge(cw_ok, prep + 2)
                pe.wait_ge(cw_t_ok, prep + 1)
                for c in range(TC):
                    mm = pe.transpose(ps[0:EXPERTS, TURN, c * CHUNK:(c + 1) * CHUNK], cw[:, c, :], ident[0:CHUNK, 0:CHUNK])
                mm.then_inc(cw_turned, 1)

            with pe.Fori(0, NP) as i:
                gate(i, None, None, i * PREPS, 0, 0)
                turn_cw(i * PREPS)
                with pe.Fori(0, ROUNDS) as r:
                    for p in range(2):
                        n = i * 8 + r * 2 + p
                        prep = i * PREPS + r * 2 + p
                        pe.wait_ge(x_lo_ok, prep + 1)
                        pe.wait_ge(cw_t_ok, prep + 2)
                        for k in range(K + LAG):
                            if k < K:
                                e, f = divmod(k, FT)
                                if f == 0:
                                    pe.wait_ge(s_ok, n * K + FT * e + 1)
                                    pe.matmul(ps[:, CWB + e % 2, 0:TW], one_row[:, e, :], cw_t[:, p, :],
                                              start=True, stop=True).then_inc(cw_spread, 1)
                                pe.wait_ge(gelu_ok, n * K + k + 1)
                                for a in range(KC):
                                    for part, xs in ((0, x_hi), (0, x_lo), (1, x_hi)):
                                        mm = pe.matmul(ps[:, HID + k % 2, 0:TW], w1[part][:, e, a, 128 * f:128 * f + 128],
                                                       xs[:, p, a, :], start=(a == 0 and xs is x_hi and part == 0),
                                                       stop=(a == KC - 1 and part == 1))
                                mm.then_inc(hid_mult, 1)
                            if k == LAG:
                                pe.wait_ge(cur_ok, n + 1)
                                for m in range(KC):
                                    pe.matmul(ps[:, Y + m, 0:TW], b_2[:, 128 * m:128 * m + 128], cw_t[:, p, :],
                                              start=True, stop=False)
                            if k >= LAG:
                                q = k - LAG
                                e, f = divmod(q, FT)
                                pe.wait_ge(lo_ok, n * K + q + 3)
                                for m in range(KC):
                                    for part, gs in ((0, g_hi), (0, g_lo), (1, g_hi)):
                                        mm = pe.matmul(ps[:, Y + m, 0:TW], w2[part][:, e, f, 128 * m:128 * m + 128],
                                                       gs[:, q % 2, :], start=False, stop=(q == K - 1 and part == 1))
                                mm.then_inc(y_mult, 1)
                            if k == 8:
                                gate(i, r, p, prep + 1, r + 1 if p else r, 1 - p)
                            if k == 20:
                                turn_cw(prep + 1)
                for p in range(2):
                    pe.wait_ge(cur_ok, i * 8 + 2 * ROUNDS + p)
                    pe.wait_ge(cw_t_ok, (i + 1) * PREPS + 1)
                    pe.wait_ge(h_ok, i * 2 + p + 1)
                    for c in range(TC):
                        for m in range(KC):
                            at = 256 * (c % 2) + 128 * m
                            mm = pe.transpose(ps[0:CHUNK, GATE + c // 2, at:at + 128],
                                              cur[:, p, m, c * CHUNK:(c + 1) * CHUNK], ident[:])
                    mm.then_inc(back_turned, 1)

        @block.scalar
        def _(act):
            for s, n in ((gelu_ok, 2), (cw_t_ok, 1)):
                act.sem_inc(s, n)
            act.wait_ge(loaded, 16 * 6)

            def part_x(i, r, p, to):
                cur_is(act, i, r, p)
                nc.scalar.copy(x_hi[:, to], cur[:, to]).then_inc(x_hi_ok, 1)

            def tanh(prep):
                act.wait_ge(arg_ok, prep + 1)
                nc.scalar.activation(cw[:], cw[:], ACT.Tanh).then_inc(tanh_ok, 1)

            def keep_cw(prep, to):
                act.wait_ge(cw_turned, prep + 1)
                nc.scalar.copy(cw_t[:, to, :], ps[0:EXPERTS, TURN, 0:TW]).then_inc(cw_t_ok, 1)

            with act.Fori(0, NP) as i:
                part_x(i, None, None, 0)
                tanh(i * PREPS)
                keep_cw(i * PREPS, 0)
                with act.Fori(0, ROUNDS) as r:
                    for p in range(2):
                        n = i * 8 + r * 2 + p
                        prep = i * PREPS + r * 2 + p + 1
                        for k in range(K):
                            act.wait_ge(hid_mult, n * K + k + 1)
                            act.wait_ge(lo_ok, n * K + k + 1)
                            nc.scalar.activation(g[:, k % 2, :], ps[:, HID + k % 2, 0:TW], ACT.Gelu_apprx_tanh,
                                                 bias=b_1[:, k:k + 1]).then_inc(gelu_ok, 1)
                            act.wait_ge(s_ok, n * K + k + 1 + S_FREE)
                            act.wait_ge(y_mult, n * K + k + 1)
                            nc.scalar.copy(g_hi[:, k % 2, :], g[:, k % 2, :]).then_inc(hi_ok, 1)
                            if k == 8:
                                part_x(i, r, p, 1 - p)
                            if k == 14:
                                tanh(prep)
                            if k == 22:
                                keep_cw(prep, 1 - p)

        @block.vector
        def _(v):
            for s, n in ((s_ok, S_FREE), (lo_ok, 2), (cur_ok, 1), (cw_ok, 1), (h_ok, 1)):
                v.sem_inc(s, n)
            v.wait_ge(loaded, 16 * 6)
            by_e = [CHUNK, TC, EXPERTS, EXPERTS]

            def top_two(prep, nxt):
                c = Chain(v, gate_dve, prep * GATE_STEPS)
                v.wait_ge(gate_mult, prep + 1)
                c.step(v.tensor_tensor(lg[:], ps[0:CHUNK, GATE, 0:TC * EXPERTS].rearrange("p (c e) -> p c e", e=EXPERTS),
                                       b_g[:, ds(nxt, 1), :].broadcast_to([CHUNK, TC, EXPERTS]), ALU.add))
                c.wait()
                other = lg[:].unsqueeze(2).broadcast_to(by_e)
                own = lg[:].unsqueeze(3).broadcast_to(by_e)
                c.step(v.tensor_tensor(cmp[:, 0], other, own, ALU.is_ge))
                c.step(v.tensor_tensor(cmp[:, 1], other, own, ALU.is_gt))
                c.wait()
                for a in range(2):
                    c.step(v.tensor_tensor(cmp[:, a], cmp[:, a], before[:, a:a + 1].broadcast_to(by_e), ALU.mult))
                c.wait()
                c.step(v.tensor_tensor(cmp[:, 0], cmp[:, 0], cmp[:, 1], ALU.add))
                c.wait()
                c.step(v.tensor_reduce(rank[:, 0], cmp[:, 0], AX.X, ALU.add))
                c.wait()
                chosen, chosen_lg = rank[:, 1], rank[:, 2]
                c.step(v.tensor_scalar(chosen, rank[:, 0], 2.0, None, ALU.is_lt))
                c.wait()
                c.step(v.tensor_tensor(chosen_lg, chosen, lg[:], ALU.mult))
                c.wait()
                c.step(v.tensor_reduce(total[:], chosen_lg, AX.X, ALU.add))
                c.wait()
                v.scalar_tensor_tensor(cw[:], total[:].unsqueeze(2).broadcast_to([CHUNK, TC, EXPERTS]), -0.5, lg[:],
                                       ALU.mult, ALU.add).then_inc(arg_ok, 1)
                return c

            def weigh(c, prep):
                v.wait_ge(tanh_ok, prep + 1)
                c.step(v.tensor_scalar(cw[:], cw[:], 1.0, 0.5, ALU.add, ALU.mult))
                c.wait()
                v.tensor_tensor(cw[:], cw[:], rank[:, 1], ALU.mult).then_inc(cw_ok, 1)
                assert c.n == GATE_STEPS, c.n

            def rest_x(prep, to):
                v.wait_ge(x_hi_ok, prep + 1)
                v.tensor_tensor(x_lo[:, to], cur[:, to], x_hi[:, to].bitcast(F32), ALU.subtract).then_inc(x_lo_ok, 1)

            with v.Fori(0, NP) as i:
                rest_x(i * PREPS, 0)
                weigh(top_two(i * PREPS, 0), i * PREPS)
                with v.Fori(0, ROUNDS) as r:
                    for p in range(2):
                        n = i * 8 + r * 2 + p
                        prep = i * PREPS + r * 2 + p + 1
                        for k in range(K + 1):
                            if k < K:
                                e, f = divmod(k, FT)
                                if f == 0:
                                    v.wait_ge(cw_spread, n * EXPERTS + e + 1)
                                v.wait_ge(gelu_ok, n * K + k + 3)
                                v.tensor_tensor(g[:, k % 2, :], g[:, k % 2, :], ps[:, CWB + e % 2, 0:TW],
                                                ALU.mult).then_inc(s_ok, 1)
                            if k >= 1:
                                q = k - 1
                                v.wait_ge(hi_ok, n * K + q + 1)
                                v.wait_ge(y_mult, n * K + q + 1)
                                v.tensor_tensor(g_lo[:, q % 2, :], g[:, q % 2, :], g_hi[:, q % 2, :].bitcast(F32),
                                                ALU.subtract).then_inc(lo_ok, 1)
                            if k == 9:
                                rest_x(prep, 1 - p)
                            if k == 11:
                                c = top_two(prep, r + 1 if p else r)
                            if k == 16:
                                weigh(c, prep)
                        v.wait_ge(y_mult, n * K + K + 2)
                        v.tensor_tensor(cur[:, p], cur[:, p], ps[:, Y:Y + KC, 0:TW], ALU.add).then_inc(cur_ok, 1)
                for p in range(2):
                    v.wait_ge(back_turned, i * 2 + p + 3)
                    rows = h[:, ds(i * 2 * TC + p * TC, TC), :].rearrange("p (a b) d -> p a (b d)", a=2)
                    v.tensor_tensor(rows, rows, ps[0:CHUNK, GATE:GATE + 2, :], ALU.add).then_inc(h_ok, 1)


def retention(nc, io, h, x_t, ident):
    with ExitStack() as ctx:
        def sb(name, shape, dt=F32):
            return ctx.enter_context(nc.sbuf_tensor("re_" + name, shape, dt))

        def sem(name):
            return ctx.enter_context(nc.semaphore("re_" + name))

        U = 2 * NCH
        GH = 4
        NG = HEADS // GH
        vg = sb("vg", [CHUNK, NT, 2 * D])
        out = sb("out", [CHUNK, NT, D])
        w = sb("w", [128, KC, 4 * D])
        w_o = sb("w_o", [128, KC, D])
        bias = sb("bias", [CHUNK, 4 * D])
        b_qk = sb("b_qk", [CHUNK, NCH, 2 * D])
        rows3 = sb("rows3", [CHUNK, 3, D])
        decay = sb("decay", [CHUNK, NCH, 2])
        causal = sb("causal", [CHUNK, CHUNK])
        head_mask = sb("head_mask", [128, 128])
        head_of = sb("head_of", [128, 8])
        x_s = sb("x_s", [128, 2, KC, CHUNK])
        qk = sb("qk", [CHUNK, 2, 2 * D])
        qk_t = sb("qk_t", [128, 2, 2 * KC, CHUNK])
        q_h = sb("q_h", [128, 2, HEADS, CHUNK])
        sc = sb("sc", [CHUNK, HEADS, CHUNK])
        state = sb("state", [128, KC, 128])
        stats = sb("stats", [CHUNK, NT, 6])
        mv = sb("mv", [CHUNK, NT, 2])
        small = sb("small", [CHUNK, 4, NT])
        rows = sb("rows", [CHUNK, 2, D])
        ps = ctx.enter_context(nc.psum_tensor("re_ps", [128, 8, 512], F32))
        QK, VG, TURN, SC, OUT, ST = 0, 1, 2, 3, 5, 7
        loaded, dve, x_copied, projected = sem("loaded"), sem("dve"), sem("x_copied"), sem("projected")
        qkvg_ok, turned, qk_t_ok, q_h_ok = sem("qkvg_ok"), sem("turned"), sem("qk_t_ok"), sem("q_h_ok")
        sc_mult, sc_ok, st_ok, out_mult, out_ok = sem("sc_mult"), sem("sc_ok"), sem("st_ok"), sem("out_mult"), sem("out_ok")
        gate_ok, gates_ready, var_ready, root_done = sem("gate_ok"), sem("gates_ready"), sem("var_ready"), sem("root_done")
        n_ok, r_ok, n_turned, n_t_ok, o_mult, h_ok = sem("n_ok"), sem("r_ok"), sem("n_turned"), sem("n_t_ok"), sem("o_mult"), sem("h_ok")
        block = ctx.enter_context(nc.Block())

        @block.sync
        def _(sp):
            sp.dma_start(w[:], io["re_w"]).then_inc(loaded, 16)
            sp.dma_start(w_o[:], io["re_w_o"]).then_inc(loaded, 16)
            sp.dma_start(bias[:], io["re_bias"].broadcast_to([CHUNK, 4 * D])).then_inc(loaded, 16)
            sp.dma_start(rows3[:], io["re_rows3"].broadcast_to([CHUNK, 3, D])).then_inc(loaded, 16)
            sp.dma_start(decay[:], io["decay"]).then_inc(loaded, 16)
            sp.dma_start(causal[:], io["causal"]).then_inc(loaded, 16)
            sp.dma_start(head_mask[:], io["head_mask"]).then_inc(loaded, 16)
            sp.dma_start(head_of[:], io["head_of"]).then_inc(loaded, 16)

        LOADED = 16 * 8

        @block.gpsimd
        def _(g):
            g.wait_ge(loaded, LOADED)
            with g.Fori(0, NT // U) as i:
                for u in range(U + 1):
                    t = i * U + u
                    if u < U:
                        g.wait_ge(projected, t + 1)
                        g.tensor_copy(x_s[:, u % 2], x_t[:, :, ds(t * CHUNK, CHUNK)]).then_inc(x_copied, 1)
                    if u >= 1:
                        t, p = t - 1, (u - 1) % 2
                        g.wait_ge(qk_t_ok, t + 2)
                        g.wait_ge(sc_mult, t * NG + NG)
                        for m in range(KC):
                            ins = g.tensor_tensor(q_h[:, p, 8 * m:8 * m + 8, :],
                                                  qk_t[:, p, m:m + 1, :].broadcast_to([128, 8, CHUNK]),
                                                  head_of[:].unsqueeze(2).broadcast_to([128, 8, CHUNK]), ALU.mult)
                        ins.then_inc(q_h_ok, 1)
            g.tensor_tensor(h[:], h[:], rows3[:, 0:1, :].broadcast_to([CHUNK, NT, D]), ALU.add).then_inc(gate_ok, 1)
            g.wait_ge(gates_ready, 1)
            g.wait_ge(out_mult, NT + 2)
            v_at, g_at = vg[:, :, 0:D], vg[:, :, D:2 * D]
            g.tensor_tensor(v_at, g_at, rows3[:, 2:3, :].broadcast_to([CHUNK, NT, D]), ALU.mult).then_inc(gate_ok, 1)
            g.wait_ge(gate_ok, 2)
            g.tensor_tensor(g_at, g_at, rows3[:, 1:2, :].broadcast_to([CHUNK, NT, D]), ALU.mult).then_inc(gate_ok, 1)

        @block.tensor
        def _(pe):
            for s, n in ((projected, 2), (sc_mult, 2 * NG), (out_mult, 2), (n_turned, 2), (o_mult, 2)):
                pe.sem_inc(s, n)
            pe.wait_ge(loaded, LOADED)

            def project(t, u):
                pe.wait_ge(x_copied, t + 1)
                pe.wait_ge(qkvg_ok, t + 1)
                for bank in (QK, VG):
                    for k in range(KC):
                        mm = pe.matmul(ps[0:CHUNK, bank, :], x_s[:, u % 2, k, :], w[:, k, 512 * bank:512 * bank + 512],
                                       start=(k == 0), stop=(k == KC - 1))
                mm.then_inc(projected, 1)

            def turn(t, u):
                pe.wait_ge(qkvg_ok, t + 2)
                pe.wait_ge(qk_t_ok, t + 1)
                for k in range(2 * KC):
                    mm = pe.transpose(ps[:, TURN, k * CHUNK:(k + 1) * CHUNK], qk[:, u % 2, 128 * k:128 * k + 128],
                                      ident[0:CHUNK, 0:CHUNK])
                mm.then_inc(turned, 1)

            def scores(t, u):
                pe.wait_ge(q_h_ok, t + 1)
                for n in range(NG):
                    pe.wait_ge(sc_ok, t * NG + n + 1)
                    pe.matmul(ps[0:CHUNK, SC + n % 2, 0:GH * CHUNK], qk_t[:, u % 2, KC + n // 2, :],
                              q_h[:, u % 2, GH * n:GH * n + GH, :], start=True, stop=True).then_inc(sc_mult, 1)

            def outputs(i, t, u):
                j = u % NCH
                pe.wait_ge(sc_ok, t * NG + NG + 2)
                pe.wait_ge(out_ok, t + 1)
                if j > 0:
                    pe.wait_ge(st_ok, i * 4 + (u // NCH) * 2 + j)
                    for m in range(KC):
                        pe.matmul(ps[0:CHUNK, OUT + u % 2, 128 * m:128 * m + 128], qk_t[:, u % 2, m, :], state[:, m, :],
                                  start=(m == 0), stop=False, skip_group_check=True)
                for e in range(HEADS):
                    mm = pe.matmul(ps[0:CHUNK, OUT + u % 2, DH * e:DH * e + DH], sc[:, e, :],
                                   vg[:, ds(t, 1), DH * e:DH * e + DH].rearrange("p o d -> p (o d)"),
                                   start=(j == 0 and e == 0), stop=True, skip_group_check=True)
                if j < NCH - 1:
                    for m in range(KC):
                        mm = pe.matmul(ps[:, ST, 128 * m:128 * m + 128], qk[:, u % 2, D + 128 * m:D + 128 * m + 128],
                                       vg[:, ds(t, 1), 128 * m:128 * m + 128].rearrange("p o d -> p (o d)"),
                                       start=(j == 0 and m == 0), stop=True, skip_group_check=True)
                mm.then_inc(out_mult, 1)

            with pe.Fori(0, NT // U) as i:
                for u in range(U + 1):
                    t = i * U + u
                    if u < U:
                        project(t, u)
                    if u >= 1:
                        scores(t - 1, u - 1)
                    if u < U:
                        turn(t, u)
                    if u >= 1:
                        outputs(i, t - 1, u - 1)
            pe.wait_ge(out_ok, NT + 2)
            with pe.Fori(0, NT // 2) as i:
                for p in range(2):
                    t = i * 2 + p
                    pe.wait_ge(n_ok, t + 1)
                    pe.wait_ge(n_t_ok, t + 1)
                    for k in range(KC):
                        mm = pe.transpose(ps[:, p, k * CHUNK:(k + 1) * CHUNK], rows[:, p, 128 * k:128 * k + 128],
                                          ident[0:CHUNK, 0:CHUNK])
                    mm.then_inc(n_turned, 1)
                for p in range(2):
                    t = i * 2 + p
                    pe.wait_ge(n_t_ok, t + 3)
                    pe.wait_ge(h_ok, t + 1)
                    for k in range(KC):
                        mm = pe.matmul(ps[0:CHUNK, 2 + p, 0:D], x_s[:, p, k, :], w_o[:, k, :],
                                       start=(k == 0), stop=(k == KC - 1))
                    mm.then_inc(o_mult, 1)

        @block.scalar
        def _(act):
            for s, n in ((qk_t_ok, 1), (out_ok, 2), (n_t_ok, 2)):
                act.sem_inc(s, n)
            with act.Fori(0, NT // U) as i:
                for u in range(U + 1):
                    t = i * U + u
                    if u < U:
                        act.wait_ge(turned, t + 1)
                        act.wait_ge(out_mult, t + 1)
                        nc.scalar.copy(qk_t[:, u % 2].rearrange("p k t -> p (k t)"), ps[:, TURN, 0:2 * KC * CHUNK]).then_inc(qk_t_ok, 1)
                    if u >= 1:
                        act.wait_ge(out_mult, t - 1 + 3)
                        nc.scalar.copy(out[:, ds(t - 1, 1), :].rearrange("p o d -> p (o d)"),
                                       ps[0:CHUNK, OUT + (u - 1) % 2, 0:D]).then_inc(out_ok, 1)
            act.wait_ge(qkvg_ok, NT + 1)
            nc.scalar.activation(vg[:, :, D:2 * D], vg[:, :, D:2 * D], ACT.Sigmoid).then_inc(gates_ready, 1)
            act.wait_ge(var_ready, 1)
            nc.scalar.sqrt(small[:, 1, :], small[:, 0, :]).then_inc(root_done, 1)
            with act.Fori(0, NT // 2) as i:
                for p in range(2):
                    t = i * 2 + p
                    act.wait_ge(n_turned, t + 3)
                    act.wait_ge(o_mult, t + 1)
                    nc.scalar.copy(x_s[:, p].rearrange("p k t -> p (k t)"), ps[:, p, 0:KC * CHUNK]).then_inc(n_t_ok, 1)

        @block.vector
        def _(v):
            for s, n in ((qkvg_ok, 1), (sc_ok, 2), (h_ok, 2)):
                v.sem_inc(s, n)
            c = Chain(v, dve)
            v.wait_ge(loaded, LOADED)
            for j in range(NCH):
                for a in range(2):
                    c.step(v.tensor_scalar(b_qk[:, j, a * D:a * D + D], bias[:, a * D:a * D + D], decay[:, j, a:a + 1],
                                           None, ALU.mult))
            c.wait()
            with v.Fori(0, NT // U) as i:
                for u in range(U + 1):
                    t = i * U + u
                    if u < U:
                        j = u % NCH
                        v.wait_ge(projected, t + 3)
                        v.wait_ge(out_mult, t + 1)
                        for a in range(2):
                            v.scalar_tensor_tensor(qk[:, u % 2, a * D:a * D + D], ps[0:CHUNK, QK, a * D:a * D + D],
                                                   decay[:, j, a:a + 1], b_qk[:, j, a * D:a * D + D], ALU.mult, ALU.add)
                        v.tensor_tensor(vg[:, ds(t, 1), :].rearrange("p o d -> p (o d)"), ps[0:CHUNK, VG, :],
                                        bias[:, 2 * D:4 * D], ALU.add).then_inc(qkvg_ok, 1)
                    if u >= 1:
                        t, j = t - 1, (u - 1) % NCH
                        if j > 0:
                            v.wait_ge(out_mult, t + 2)
                            v.tensor_tensor(state[:], ps[:, ST, 0:D].rearrange("p (m e) -> p m e", m=KC),
                                            head_mask[:].unsqueeze(1).broadcast_to([128, KC, 128]), ALU.mult).then_inc(st_ok, 1)
                        v.wait_ge(out_mult, t + 2)
                        for n in range(NG):
                            v.wait_ge(sc_mult, t * NG + n + 1 + 2 * NG)
                            v.tensor_tensor(sc[:, GH * n:GH * n + GH, :],
                                            ps[0:CHUNK, SC + n % 2, 0:GH * CHUNK].rearrange("p (g i) -> p g i", g=GH),
                                            causal[:].unsqueeze(1).broadcast_to([CHUNK, GH, CHUNK]), ALU.mult).then_inc(sc_ok, 1)
            v.wait_ge(out_ok, NT + 2)
            row_stats(c, out, stats, mv)
            v.tensor_scalar(small[:, 0, :], mv[:, :, 1], LN_EPS, None, ALU.add).then_inc(var_ready, 1)
            v.wait_ge(root_done, 1)
            inverse_root(c, small[:, 0, :], small[:, 1, :], small[:, 2, :], small[:, 3, :])
            v.wait_ge(gate_ok, 3)
            with v.Fori(0, NT // 2) as i:
                for p in range(2):
                    t = i * 2 + p
                    v.wait_ge(n_turned, t + 1)
                    v.tensor_scalar(rows[:, p, :], out[:, ds(t, 1), :].rearrange("p o d -> p (o d)"),
                                    mv[:, ds(t, 1), 0], small[:, 2, ds(t, 1)], ALU.subtract, ALU.mult).then_inc(r_ok, 1)
                    v.wait_ge(r_ok, t * 2 + 1)
                    v.tensor_tensor(rows[:, p, :], rows[:, p, :], vg[:, ds(t, 1), D:2 * D].rearrange("p o d -> p (o d)"),
                                    ALU.mult).then_inc(r_ok, 1)
                    v.wait_ge(r_ok, t * 2 + 2)
                    v.tensor_tensor(rows[:, p, :], rows[:, p, :], vg[:, ds(t, 1), 0:D].rearrange("p o d -> p (o d)"),
                                    ALU.add).then_inc(n_ok, 1)
                for p in range(2):
                    t = i * 2 + p
                    v.wait_ge(o_mult, t + 3)
                    row = h[:, ds(t, 1), :].rearrange("p o d -> p (o d)")
                    v.tensor_tensor(row, row, ps[0:CHUNK, 2 + p, 0:D], ALU.add).then_inc(h_ok, 1)


NEXP, EF, SF = 16, 256, 1024
ST = SF // 128
ROWS = 128
G_TILES = (T + NEXP * (ROWS - 1)) // ROWS
SHW = ST * (2 * KC * 128 + D)


def route_and_share(nc, io, h, x_sorted, place, tile_expert, w_gu, ident):
    with ExitStack() as ctx:
        def sb(name, shape, dt=F32):
            return ctx.enter_context(nc.sbuf_tensor("sh_" + name, shape, dt))

        def sem(name):
            return ctx.enter_context(nc.semaphore("sh_" + name))

        w_hi, w_lo = sb("w_hi", [128, SHW], F32R), sb("w_lo", [128, SHW], F32R)
        stats = sb("stats", [CHUNK, NT, 6])
        mv = sb("mv", [CHUNK, NT, 2])
        small = sb("small", [CHUNK, 6, NT])
        x_rows = sb("x_rows", [CHUNK, NT, D])
        x_f = sb("x_f", [128, KC, TW])
        x_hi, x_lo = sb("x_hi", [128, 2, KC, TW], F32R), sb("x_lo", [128, 2, KC, TW], F32R)
        router = sb("router", [128, KC, NEXP])
        lg = sb("lg", [CHUNK, NT, NEXP])
        hot = sb("hot", [CHUNK, NT, NEXP])
        early = sb("early", [CHUNK, CHUNK])
        ones = sb("ones", [CHUNK, CHUNK])
        numbers = sb("numbers", [CHUNK, NEXP + G_TILES])
        keep = sb("keep", [CHUNK, NEXP * NT])
        ends = sb("ends", [CHUNK, 4, NEXP])
        ends_i = sb("ends_i", [CHUNK, NEXP], I32)
        zeros = sb("zeros", [128, D])
        big = sb("big", [128, 6 * TW])
        g = big[:, 0:2 * TW].rearrange("p (s t) -> p s t", s=2)
        pr = big[:, 2 * TW:4 * TW].rearrange("p (s t) -> p s t", s=2)
        g_hi, g_lo = sb("g_hi", [128, 2, TW], F32R), sb("g_lo", [128, 2, TW], F32R)
        rows = sb("rows", [CHUNK, 2, D])
        y_f = big[:, 4 * TW:6 * TW].rearrange("p (m t) -> p m t", m=KC)
        stage = big[:, 0:2 * 1024].rearrange("p (s n) -> p s n", s=2)
        ps = ctx.enter_context(nc.psum_tensor("sh_ps", [128, 8, 512], F32))
        GATE, UP, Y, XT = 0, 2, 4, 6
        loaded, gu_loaded, zero_ok, zeroed, lo_ok_w, hi_ok_w = (sem("loaded"), sem("gu_loaded"), sem("zero_ok"), sem("zeroed"),
                                                                sem("lo_ok_w"), sem("hi_ok_w"))
        staged = [sem("staged0"), sem("staged1")]
        dve, var_ready, root_done, rows_ok, r_turned, r_t_ok = (sem("dve"), sem("var_ready"), sem("root_done"), sem("rows_ok"),
                                                                sem("r_turned"), sem("r_t_ok"))
        lg_mult, lg_ok, hot_ok, counted, score_arg, score_ok = (sem("lg_mult"), sem("lg_ok"), sem("hot_ok"), sem("counted"),
                                                                sem("score_arg"), sem("score_ok"))
        scale_ok, x_rows_ok, scattered = sem("scale_ok"), sem("x_rows_ok"), sem("scattered")
        rows2_ok, turned, x_f_ok, x_hi_ok, x_lo_ok = sem("rows2_ok"), sem("turned"), sem("x_f_ok"), sem("x_hi_ok"), sem("x_lo_ok")
        hid_mult, silu_ok, prod_ok, hi_ok, lo_ok = sem("hid_mult"), sem("silu_ok"), sem("prod_ok"), sem("hi_ok"), sem("lo_ok")
        y_mult, y_f_ok, back_turned, h_ok = sem("y_mult"), sem("y_f_ok"), sem("back_turned"), sem("h_ok")
        block = ctx.enter_context(nc.Block())
        NPIECE = SHW // 1024
        Y_FREE = ST + 1
        w1 = [w[:, 0:ST * 2 * KC * 128].rearrange("p (f u k c) -> p f u k c", f=ST, u=2, k=KC) for w in (w_hi, w_lo)]
        w2 = [w[:, ST * 2 * KC * 128:].rearrange("p (f d) -> p f d", f=ST) for w in (w_hi, w_lo)]

        @block.sync
        def _(sp):
            for dst, name in ((router, "router"), (early, "early"), (keep, "keep"), (numbers, "numbers")):
                src = io[name]
                sp.dma_start(dst[:], src if src.shape[0] > 1 else src.broadcast_to([CHUNK, src.shape[1]])).then_inc(loaded, 16)
            with sp.Fori(0, NPIECE // 2) as i:
                for p in range(2):
                    sp.wait_ge(lo_ok_w, i * 2 + p + 1)
                    sp.dma_start(stage[:, p, :], io["sh_w"][:, ds((i * 2 + p) * 1024, 1024)]).then_inc(staged[p], 16)
            sp.wait_ge(zero_ok, 1)
            sp.dma_start(x_sorted.rearrange("(p n) d -> p n d", p=128), zeros[:].unsqueeze(1).broadcast_to([128, G_TILES, D])).then_inc(zeroed, 16)
            sp.dma_start(w_gu[:], io["ex_gu"]).then_inc(gu_loaded, 16)
            sp.wait_ge(gu_loaded, 16)

        @block.gpsimd
        def _(gp):
            gp.memset(zeros[:], 0.0).then_inc(zero_ok, 1)
            gp.wait_ge(zeroed, 16)
            gp.wait_ge(scale_ok, 2)
            for t in range(NT):
                gp.wait_ge(x_rows_ok, t + 1)
                gp.indirect_dma_start(x_sorted, bass.IndirectOffsetOnAxis(ap=place[:, t:t + 1].bitcast(U32), axis=0),
                                      x_rows[:, t, :], None).then_inc(scattered, 16)
            gp.wait_ge(scattered, 16 * NT)

        @block.tensor
        def _(pe):
            for s, n in ((r_turned, 2), (lg_mult, 2), (turned, 2), (y_mult, Y_FREE), (back_turned, 1)):
                pe.sem_inc(s, n)
            pe.wait_ge(loaded, 16 * 4)
            with pe.Fori(0, NT // 2) as i:
                for p in range(2):
                    t = i * 2 + p
                    pe.wait_ge(rows_ok, t + 1)
                    pe.wait_ge(r_t_ok, t + 1)
                    for k in range(KC):
                        mm = pe.transpose(ps[:, p, k * CHUNK:(k + 1) * CHUNK], rows[:, p, 128 * k:128 * k + 128],
                                          ident[0:CHUNK, 0:CHUNK])
                    mm.then_inc(r_turned, 1)
                for p in range(2):
                    t = i * 2 + p
                    pe.wait_ge(r_t_ok, t + 3)
                    pe.wait_ge(lg_ok, t + 1)
                    for k in range(KC):
                        mm = pe.matmul(ps[0:CHUNK, 2 + p, 0:NEXP], x_f[:, p, k * CHUNK:(k + 1) * CHUNK], router[:, k, :],
                                       start=(k == 0), stop=(k == KC - 1))
                    mm.then_inc(lg_mult, 1)
            pe.wait_ge(hot_ok, 1)
            all_hot = hot[:].rearrange("p t e -> p (t e)")
            pe.matmul(ps[0:CHUNK, 4, 0:NT * NEXP], early[:], all_hot, start=True, stop=True)
            pe.matmul(ps[0:CHUNK, 5, 0:NT * NEXP], ones[:], all_hot, start=True, stop=True).then_inc(counted, 1)
            pe.wait_ge(scale_ok, 2)

            def back(j, p):
                pe.wait_ge(y_f_ok, j + 2)
                pe.wait_ge(h_ok, j + 1)
                pe.wait_ge(x_f_ok, (j - p) * TC + 2 * TC + 2)
                for c in range(TC):
                    for m in range(KC):
                        at = 256 * (c % 2) + 128 * m
                        mm = pe.transpose(ps[0:CHUNK, XT + c // 2, at:at + 128], y_f[:, m, c * CHUNK:(c + 1) * CHUNK], ident[:])
                mm.then_inc(back_turned, 1)

            with pe.Fori(0, NP) as i:
                for p in range(2):
                    j = i * 2 + p
                    for c in range(TC):
                        pe.wait_ge(rows2_ok, j * TC + c + 1)
                        pe.wait_ge(x_f_ok, j * TC + c + 1)
                        pe.wait_ge(h_ok, i * 2 + 1)
                        for k in range(KC):
                            mm = pe.transpose(ps[:, XT + c % 2, k * CHUNK:(k + 1) * CHUNK], rows[:, c % 2, 128 * k:128 * k + 128],
                                              ident[0:CHUNK, 0:CHUNK])
                        mm.then_inc(turned, 1)
                for p in range(2):
                    j = i * 2 + p
                    pe.wait_ge(x_lo_ok, j + 2)
                    for k in range(ST + 2):
                        if k < ST:
                            q = j * ST + k
                            pe.wait_ge(prod_ok, q + 1)
                            for u, bank in ((0, GATE), (1, UP)):
                                for a in range(KC):
                                    for part, xs in ((0, x_hi), (0, x_lo), (1, x_hi)):
                                        mm = pe.matmul(ps[:, bank + k % 2, 0:TW], w1[part][:, k, u, a, :], xs[:, p, a, :],
                                                       start=(a == 0 and part == 0 and xs is x_hi), stop=(a == KC - 1 and part == 1))
                            mm.then_inc(hid_mult, 1)
                        if k == 2:
                            pe.wait_ge(y_f_ok, j + 1)
                        if k >= 2:
                            f = k - 2
                            pe.wait_ge(lo_ok, j * ST + f + 3)
                            for m in range(KC):
                                for part, gs in ((0, g_hi), (0, g_lo), (1, g_hi)):
                                    mm = pe.matmul(ps[:, Y + m, 0:TW], w2[part][:, f, 128 * m:128 * m + 128], gs[:, f % 2, :],
                                                   start=(f == 0 and part == 0 and gs is g_hi), stop=(f == ST - 1 and part == 1))
                            mm.then_inc(y_mult, 1)
                        if k == 1 and p == 1:
                            back(j - 1, 0)
                back(i * 2 + 1, 1)

        @block.scalar
        def _(act):
            for s, n in ((r_t_ok, 2), (x_f_ok, 2), (y_f_ok, 1)):
                act.sem_inc(s, n)
            with act.Fori(0, NPIECE // 2) as i:
                for p in range(2):
                    act.wait_ge(staged[p], i * 16 + 16)
                    nc.scalar.copy(w_hi[:, ds((i * 2 + p) * 1024, 1024)], stage[:, p, :]).then_inc(hi_ok_w, 1)
            act.wait_ge(var_ready, 1)
            nc.scalar.sqrt(small[:, 1, :], small[:, 0, :]).then_inc(root_done, 1)
            with act.Fori(0, NT // 2) as i:
                for p in range(2):
                    t = i * 2 + p
                    act.wait_ge(r_turned, t + 3)
                    act.wait_ge(lg_mult, t + 1)
                    nc.scalar.copy(x_f[:, p, 0:KC * CHUNK], ps[:, p, 0:KC * CHUNK]).then_inc(r_t_ok, 1)
            act.wait_ge(score_arg, 1)
            nc.scalar.activation(small[:, 4, :], small[:, 3, :], ACT.Sigmoid).then_inc(score_ok, 1)
            act.wait_ge(scale_ok, 2)
            with act.Fori(0, NT) as t:
                nc.scalar.activation(x_rows[:, ds(t, 1), :].rearrange("p o d -> p (o d)"),
                                     h[:, ds(t, 1), :].rearrange("p o d -> p (o d)"), ACT.Identity,
                                     bias=small[:, 5, ds(t, 1)], scale=small[:, 4, ds(t, 1)]).then_inc(x_rows_ok, 1)

            def silu(j, k):
                q = j * ST + k
                act.wait_ge(hid_mult, q + 1)
                nc.scalar.activation(g[:, k % 2, :], ps[:, GATE + k % 2, 0:TW], ACT.Silu).then_inc(silu_ok, 1)
                act.wait_ge(prod_ok, q + 3)
                act.wait_ge(y_mult, q + ST)
                nc.scalar.copy(g_hi[:, k % 2, :], pr[:, k % 2, :]).then_inc(hi_ok, 1)

            with act.Fori(0, NP) as i:
                for p in range(2):
                    j = i * 2 + p
                    act.wait_ge(x_lo_ok, j + 1)
                    for c in range(TC):
                        act.wait_ge(turned, j * TC + c + 3)
                        nc.scalar.copy(x_f[:, :, c * CHUNK:(c + 1) * CHUNK],
                                       ps[:, XT + c % 2, 0:KC * CHUNK].rearrange("p (k t) -> p k t", k=KC)).then_inc(x_f_ok, 1)
                    act.wait_ge(x_f_ok, j * TC + TC + 2)
                    act.wait_ge(y_mult, j * ST + 1)
                    nc.scalar.copy(x_hi[:, p], x_f[:]).then_inc(x_hi_ok, 1)
                for p in range(2):
                    j = i * 2 + p
                    for k in range(ST):
                        silu(j, k)
                    act.wait_ge(y_mult, j * ST + ST + Y_FREE)
                    act.wait_ge(back_turned, j + 1)
                    nc.scalar.copy(y_f[:], ps[:, Y:Y + KC, 0:TW]).then_inc(y_f_ok, 1)

        @block.vector
        def _(v):
            for s, n in ((lo_ok_w, 2), (lg_ok, 2), (x_lo_ok, 1), (prod_ok, 2), (lo_ok, 2), (h_ok, 1)):
                v.sem_inc(s, n)
            c = Chain(v, dve)
            with v.Fori(0, NPIECE // 2) as i:
                for p in range(2):
                    v.wait_ge(hi_ok_w, i * 2 + p + 1)
                    at = ds((i * 2 + p) * 1024, 1024)
                    v.tensor_tensor(w_lo[:, at], stage[:, p, :], w_hi[:, at].bitcast(F32), ALU.subtract).then_inc(lo_ok_w, 1)
            c.step(v.memset(ones[:], 1.0))
            row_stats(c, h, stats, mv)
            v.tensor_scalar(small[:, 0, :], mv[:, :, 1], LN_EPS, None, ALU.add).then_inc(var_ready, 1)
            v.wait_ge(root_done, 1)
            inverse_root(c, small[:, 0, :], small[:, 1, :], small[:, 2, :], small[:, 3, :])

            def row_tile(t, slot):
                return v.tensor_scalar(rows[:, slot, :], h[:, ds(t, 1), :].rearrange("p o d -> p (o d)"),
                                       mv[:, ds(t, 1), 0], small[:, 2, ds(t, 1)], ALU.subtract, ALU.mult)

            with v.Fori(0, NT // 2) as i:
                for p in range(2):
                    v.wait_ge(r_turned, i * 2 + p + 1)
                    row_tile(i * 2 + p, p).then_inc(rows_ok, 1)
                for p in range(2):
                    v.wait_ge(lg_mult, i * 2 + p + 3)
                    v.tensor_copy(lg[:, ds(i * 2 + p, 1), :].rearrange("p o e -> p (o e)"),
                                  ps[0:CHUNK, 2 + p, 0:NEXP]).then_inc(lg_ok, 1)
            v.wait_ge(lg_ok, NT + 2)
            v.wait_ge(loaded, 16 * 4)
            by_e = [CHUNK, NT, NEXP]
            tables = big[0:CHUNK, 0:4 * NT * NEXP].rearrange("p (a n) -> p a n", a=4)
            v.tensor_reduce(small[:, 3, :], lg[:], AX.X, ALU.max).then_inc(score_arg, 1)
            v.wait_ge(score_arg, 1)
            number = numbers[:, 0:NEXP].unsqueeze(1).broadcast_to(by_e)
            c.step(v.tensor_tensor(hot[:], lg[:], small[:, 3, :].unsqueeze(2).broadcast_to(by_e), ALU.is_ge))
            c.wait()
            c.step(v.tensor_tensor(lg[:], hot[:], number, ALU.mult))
            c.wait()
            c.step(v.tensor_reduce(small[:, 5, :], lg[:], AX.X, ALU.min))
            c.wait()
            v.tensor_tensor(hot[:], number, small[:, 5, :].unsqueeze(2).broadcast_to(by_e), ALU.is_equal).then_inc(hot_ok, 1)
            v.wait_ge(counted, 1)
            before, total, running = tables[:, 0, :], tables[:, 1, :], tables[:, 2, :]

            def expert_first(ap):
                return ap.rearrange("p (t e) -> p e t", e=NEXP)

            c.step(v.tensor_copy(before.rearrange("p (e t) -> p e t", e=NEXP), expert_first(ps[0:CHUNK, 4, 0:NT * NEXP])))
            c.step(v.tensor_copy(total.rearrange("p (e t) -> p e t", e=NEXP), expert_first(ps[0:CHUNK, 5, 0:NT * NEXP])))
            c.wait()
            c.step(v.tensor_tensor_scan(running, keep[:], total, 0.0, ALU.mult, ALU.add))
            c.wait()
            count = running.rearrange("p (e t) -> p e t", e=NEXP)[:, :, NT - 1]
            tiles, end = ends[:, 0, :], ends[:, 1, :]
            c.step(v.tensor_scalar(ends_i[:], count, ROWS - 1, None, ALU.add))
            c.step(v.memset(ends[:, 3, :], 1.0))
            c.wait()
            c.step(v.tensor_scalar(ends_i[:], ends_i[:], 7, None, ALU.arith_shift_right))
            c.wait()
            c.step(v.tensor_copy(tiles, ends_i[:]))
            c.wait()
            c.step(v.tensor_tensor_scan(end, ends[:, 3, :], tiles, 0.0, ALU.mult, ALU.add))
            c.step(v.tensor_tensor(before, before, running, ALU.add))
            c.wait()
            c.step(v.tensor_tensor(ends[:, 2, :], end, tiles, ALU.subtract))
            c.step(v.tensor_tensor(before, before, total, ALU.subtract))
            c.wait()
            c.step(v.tensor_scalar(ends[:, 2, :], ends[:, 2, :], float(ROWS), None, ALU.mult))
            c.wait()
            c.step(v.tensor_tensor(before.rearrange("p (e t) -> p e t", e=NEXP), before.rearrange("p (e t) -> p e t", e=NEXP),
                                   ends[:, 2, :].unsqueeze(2).broadcast_to([CHUNK, NEXP, NT]), ALU.add))
            c.wait()
            c.step(v.tensor_tensor(lg[:], before.rearrange("p (e t) -> p t e", e=NEXP), hot[:], ALU.mult))
            c.wait()
            v.wait_ge(score_ok, 1)
            c.step(v.tensor_reduce(small[:, 3, :], lg[:], AX.X, ALU.add))
            c.wait()
            v.tensor_copy(place[:], small[:, 3, :]).then_inc(scale_ok, 1)
            cmp = big[0:CHUNK, 4 * NT * NEXP:4 * NT * NEXP + G_TILES * NEXP].rearrange("p (g e) -> p g e", e=NEXP)
            c.step(v.tensor_tensor(cmp, numbers[:, NEXP:].unsqueeze(2).broadcast_to([CHUNK, G_TILES, NEXP]),
                                   end.unsqueeze(1).broadcast_to([CHUNK, G_TILES, NEXP]), ALU.is_ge))
            c.wait()
            c.step(v.tensor_reduce(tables[:, 3, 0:G_TILES], cmp, AX.X, ALU.add))
            c.wait()
            c.step(v.tensor_scalar(tile_expert[:], tables[:, 3, 0:G_TILES], float(NEXP - 1), None, ALU.min))
            c.step(v.tensor_tensor(small[:, 4, :], small[:, 4, :], small[:, 2, :], ALU.mult))
            c.wait()
            v.scalar_tensor_tensor(small[:, 5, :], mv[:, :, 0], -1.0, small[:, 4, :], ALU.mult, ALU.mult).then_inc(scale_ok, 1)
            v.wait_ge(x_rows_ok, NT)
            with v.Fori(0, NP) as i:
                for p in range(2):
                    j = i * 2 + p
                    for cc in range(TC):
                        v.wait_ge(turned, j * TC + cc + 1)
                        row_tile(j * TC + cc, cc % 2).then_inc(rows2_ok, 1)
                    v.wait_ge(x_hi_ok, j + 1)
                    v.tensor_tensor(x_lo[:, p], x_f[:], x_hi[:, p].bitcast(F32), ALU.subtract).then_inc(x_lo_ok, 1)

                def add_back(j):
                    v.wait_ge(back_turned, j + 2)
                    out = h[:, ds(j * TC, TC), :].rearrange("p (a b) d -> p a (b d)", a=2)
                    v.tensor_tensor(out, out, ps[0:CHUNK, XT:XT + 2, :], ALU.add).then_inc(h_ok, 1)

                for p in range(2):
                    j = i * 2 + p
                    for k in range(ST + 1):
                        if k < ST:
                            q = j * ST + k
                            v.wait_ge(silu_ok, q + 1)
                            v.wait_ge(lo_ok, q + 1)
                            v.tensor_tensor(pr[:, k % 2, :], g[:, k % 2, :], ps[:, UP + k % 2, 0:TW], ALU.mult).then_inc(prod_ok, 1)
                        if k >= 1:
                            q = j * ST + k - 1
                            v.wait_ge(hi_ok, q + 1)
                            v.wait_ge(y_mult, q + ST)
                            v.tensor_tensor(g_lo[:, (k - 1) % 2, :], pr[:, (k - 1) % 2, :], g_hi[:, (k - 1) % 2, :].bitcast(F32),
                                            ALU.subtract).then_inc(lo_ok, 1)
                        if k == 4 and p == 1:
                            add_back(j - 1)
                add_back(i * 2 + 1)


def routed_experts(nc, io, h, out, x_sorted, y_sorted, place, tile_expert, w_gu, ident):
    with ExitStack() as ctx:
        def sb(name, shape, dt=F32):
            return ctx.enter_context(nc.sbuf_tensor("ex_" + name, shape, dt))

        def sem(name):
            return ctx.enter_context(nc.semaphore("ex_" + name))

        U = 4
        NGATHER = 4
        TG = NT // NGATHER
        w_d = sb("w_d", [128, NEXP, EF // 128, D])
        x = sb("x", [ROWS, U, D])
        x_t = sb("x_t", [128, 2, KC, ROWS])
        g = sb("g", [ROWS, 2, EF])
        pr = sb("pr", [ROWS, 2, EF])
        pr_t = sb("pr_t", [128, 2, EF // 128, ROWS])
        y = sb("y", [ROWS, G_TILES, D])
        y_rows = sb("y_rows", [CHUNK, NT, D])
        ps = ctx.enter_context(nc.psum_tensor("ex_ps", [128, 8, 512], F32))
        XT, GU, PT, Y = 0, 2, 4, 6
        w_loaded, x_turned, x_t_ok, gu_mult, silu_ok = sem("w_loaded"), sem("x_turned"), sem("x_t_ok"), sem("gu_mult"), sem("silu_ok")
        x_loaded = [sem(f"x_loaded{u}") for u in range(U)]
        prod_ok, p_turned, p_t_ok, y_mult, y_ok, y_stored = (sem("prod_ok"), sem("p_turned"), sem("p_t_ok"), sem("y_mult"),
                                                             sem("y_ok"), sem("y_stored"))
        gathered = [sem(f"gathered{n}") for n in range(NGATHER)]
        h_ok, out_stored = sem("h_ok"), sem("out_stored")
        block = ctx.enter_context(nc.Block())

        @block.sync
        def _(sp):
            with sp.Fori(0, G_TILES // U) as i:
                for u in range(U):
                    q = i * U + u
                    sp.wait_ge(x_turned, q + 1)
                    sp.dma_start(x[:, u, :], x_sorted[ds(q * ROWS, ROWS), :]).then_inc(x_loaded[u], 16)
            for n in range(NGATHER):
                sp.wait_ge(h_ok, n + 1)
                sp.dma_start(out.rearrange("c (j p) d -> p (c j) d", p=CHUNK)[:, TG * n:TG * n + TG, :],
                             h[:, TG * n:TG * n + TG, :]).then_inc(out_stored, 16)
            sp.wait_ge(out_stored, 16 * NGATHER)

        @block.gpsimd
        def _(gp):
            gp.dma_start(w_d[:], io["ex_d"]).then_inc(w_loaded, 16)
            with gp.Fori(0, G_TILES // U) as i:
                for u in range(U):
                    q = i * U + u
                    gp.wait_ge(y_ok, q + 3)
                    gp.dma_start(y_sorted[ds(q * ROWS, ROWS), :], y[:, ds(q, 1), :].rearrange("p o d -> p (o d)")).then_inc(y_stored, 16)
            gp.wait_ge(y_stored, 16 * G_TILES)
            for t in range(NT):
                gp.indirect_dma_start(y_rows[:, t, :], None, y_sorted,
                                      bass.IndirectOffsetOnAxis(ap=place[:, t:t + 1].bitcast(U32), axis=0)).then_inc(gathered[t // TG], 16)

        @block.tensor
        def _(pe):
            for s, n in ((x_turned, U), (gu_mult, 2), (p_turned, 2), (y_mult, 2)):
                pe.sem_inc(s, n)
            with pe.Fori(0, G_TILES // U) as i:
                for s in range(U + 1):
                    if s < U:
                        q, b = i * U + s, s % 2
                        pe.wait_ge(x_loaded[s], i * 16 + 16)
                        pe.wait_ge(x_t_ok, q + 1)
                        for k in range(KC):
                            mm = pe.transpose(ps[:, XT + b, ROWS * k:ROWS * k + ROWS], x[:, s, 128 * k:128 * k + 128], ident[:])
                        mm.then_inc(x_turned, 1)
                    if s >= 1:
                        q, b = i * U + s - 1, (s - 1) % 2
                        pe.wait_ge(prod_ok, q + 3)
                        pe.wait_ge(p_t_ok, q + 1)
                        for k in range(EF // 128):
                            mm = pe.transpose(ps[:, PT + b, ROWS * k:ROWS * k + ROWS], pr[:, b, 128 * k:128 * k + 128], ident[:])
                        mm.then_inc(p_turned, 1)
                    if s < U:
                        q, b = i * U + s, s % 2
                        e = pe.value_load(tile_expert[0:1, ds(q, 1)], min_val=0, max_val=NEXP - 1)
                        pe.wait_ge(x_t_ok, q + 3)
                        pe.wait_ge(prod_ok, q + 1)
                        for k in range(KC):
                            mm = pe.matmul(ps[0:ROWS, GU + b, :], x_t[:, b, k, :],
                                           w_gu[:, ds(e, 1), k, :].rearrange("p o f -> p (o f)"), start=(k == 0), stop=(k == KC - 1))
                        mm.then_inc(gu_mult, 1)
                    if s >= 1:
                        q, b = i * U + s - 1, (s - 1) % 2
                        if s == 1:
                            pe.wait_ge(w_loaded, 16)
                        e = pe.value_load(tile_expert[0:1, ds(q, 1)], min_val=0, max_val=NEXP - 1)
                        pe.wait_ge(p_t_ok, q + 3)
                        pe.wait_ge(y_ok, q + 1)
                        for k in range(EF // 128):
                            mm = pe.matmul(ps[0:ROWS, Y + b, 0:D], pr_t[:, b, k, :],
                                           w_d[:, ds(e, 1), k, :].rearrange("p o d -> p (o d)"), start=(k == 0), stop=(k == EF // 128 - 1))
                        mm.then_inc(y_mult, 1)

        @block.scalar
        def _(act):
            for s, n in ((x_t_ok, 2), (p_t_ok, 2)):
                act.sem_inc(s, n)
            with act.Fori(0, G_TILES // U) as i:
                for s in range(U + 1):
                    if s < U:
                        q, b = i * U + s, s % 2
                        act.wait_ge(x_turned, q + 1 + U)
                        act.wait_ge(gu_mult, q + 1)
                        nc.scalar.copy(x_t[:, b].rearrange("p k t -> p (k t)"), ps[:, XT + b, 0:KC * ROWS]).then_inc(x_t_ok, 1)
                    if s >= 1:
                        q, b = i * U + s - 1, (s - 1) % 2
                        act.wait_ge(p_turned, q + 3)
                        act.wait_ge(y_mult, q + 1)
                        nc.scalar.copy(pr_t[:, b].rearrange("p k t -> p (k t)"), ps[:, PT + b, 0:EF]).then_inc(p_t_ok, 1)
                    if s < U:
                        q, b = i * U + s, s % 2
                        act.wait_ge(gu_mult, q + 3)
                        act.wait_ge(prod_ok, q + 1)
                        nc.scalar.activation(g[:, b, :], ps[0:ROWS, GU + b, 0:EF], ACT.Silu).then_inc(silu_ok, 1)

        @block.vector
        def _(v):
            for s, n in ((prod_ok, 2), (y_ok, 2)):
                v.sem_inc(s, n)
            with v.Fori(0, G_TILES // U) as i:
                for s in range(U + 1):
                    if s < U:
                        q, b = i * U + s, s % 2
                        v.wait_ge(silu_ok, q + 1)
                        v.wait_ge(p_turned, q + 1)
                        v.tensor_tensor(pr[:, b, :], g[:, b, :], ps[0:ROWS, GU + b, EF:2 * EF], ALU.mult).then_inc(prod_ok, 1)
                    if s >= 1:
                        q, b = i * U + s - 1, (s - 1) % 2
                        v.wait_ge(y_mult, q + 3)
                        v.tensor_copy(y[:, ds(q, 1), :].rearrange("p o d -> p (o d)"), ps[0:ROWS, Y + b, 0:D]).then_inc(y_ok, 1)
            for n in range(NGATHER):
                v.wait_ge(gathered[n], 16 * TG)
                part = h[:, TG * n:TG * n + TG, :]
                v.tensor_tensor(part, part, y_rows[:, TG * n:TG * n + TG, :], ALU.add).then_inc(h_ok, 1)


def build(nc, io, out):
    with ExitStack() as ctx:
        h = ctx.enter_context(nc.sbuf_tensor("h", [CHUNK, NT, D], F32))
        ident = ctx.enter_context(nc.sbuf_tensor("ident", [128, 128], F32))
        ident_ready = ctx.enter_context(nc.semaphore("ident_ready"))
        embed_tokens(nc, io, h, ident, ident_ready)
        embed_text(nc, io, h, ident, ident_ready)
        with nc.sbuf_tensor("x0_t", [128, KC, T], F32) as x_t:
            normalise(nc, "n0", h, x_t, ident, ident_ready)
            linear_attention(nc, io, h, x_t, ident, ident_ready)
        x_dram = nc.dram_tensor("x1_rows", (128, KC, T), F32, kind="Internal").ap()
        with ExitStack() as inner:
            w_hi = inner.enter_context(nc.sbuf_tensor("mo_w_hi", [128, NW * WCHUNK], F32R))
            w_lo = inner.enter_context(nc.sbuf_tensor("mo_w_lo", [128, NW * WCHUNK], F32R))
            with nc.sbuf_tensor("x1_t", [128, KC, T], F32) as x_t:
                normalise(nc, "n1", h, x_t, ident, ident_ready)
                split_weights(nc, io, w_hi, w_lo, x_t, x_dram)
            recursive_mixture(nc, io, h, x_dram, w_hi, w_lo, ident)
        with nc.sbuf_tensor("x2_t", [128, KC, T], F32) as x_t:
            normalise(nc, "n2", h, x_t, ident, ident_ready)
            retention(nc, io, h, x_t, ident)
        x_sorted = nc.dram_tensor("x_sorted", (G_TILES * ROWS, D), F32, kind="Internal").ap()
        y_sorted = nc.dram_tensor("y_sorted", (G_TILES * ROWS, D), F32, kind="Internal").ap()
        place = ctx.enter_context(nc.sbuf_tensor("place", [CHUNK, NT], I32))
        tile_expert = ctx.enter_context(nc.sbuf_tensor("tile_expert", [CHUNK, G_TILES], I32))
        w_gu = ctx.enter_context(nc.sbuf_tensor("ex_w_gu", [128, NEXP, KC, 2 * EF], F32))
        route_and_share(nc, io, h, x_sorted, place, tile_expert, w_gu, ident)
        routed_experts(nc, io, h, out, x_sorted, y_sorted, place, tile_expert, w_gu, ident)


def host_arrays(inputs):
    import numpy as np
    f = lambda n: np.asarray(inputs[n])

    def pairs(w):
        return w.reshape(w.shape[0] // 128, 128, -1).transpose(1, 0, 2)

    io = {
        "x": f("x").transpose(3, 2, 0, 1), "log_dt": f("L0_tok_log_dt"), "inv_A_real": f("L0_tok_inv_A_real").T,
        "A_imag": f("L0_tok_A_imag").T, "B_ri": f("L0_tok_B_ri").transpose(2, 1, 0),
        "sign": np.repeat(np.array([[1.0], [-1.0]], np.float32), MODES, axis=0),
        "x_txt": f("x_txt").T, "W_txt": np.concatenate([f("L0_txt_W0"), f("L0_txt_W1"), f("L0_txt_W2")]).reshape(3, 128, D).transpose(1, 0, 2),
        "E0": f("L0_txt_E0"), "E1": f("L0_txt_E1"), "E2": f("L0_txt_E2"),
        "la_w_qv": pairs(np.concatenate([f("L0_attn_Wq").T, f("L0_attn_Wv").T], axis=1)),
        "la_w_k": pairs(f("L0_attn_Wk").T), "la_w_o": pairs(f("L0_attn_Wo").T),
        "la_b_qv": np.concatenate([f("L0_attn_bq"), f("L0_attn_bv")])[None], "la_b_o": f("L0_attn_bo")[None],
        "la_cols": np.stack([f("L0_attn_bk"), f("L0_attn_ln_g"), f("L0_attn_ln_b")]).reshape(3, KC, 128).transpose(2, 0, 1),
        "head_mask": np.kron(np.eye(8, dtype=np.float32), np.ones((16, 16), np.float32)),
        "mo_w": np.concatenate([
            f("L0_ffn_W1").reshape(EXPERTS, KC, 128, FF).transpose(2, 0, 1, 3).reshape(128, -1),
            f("L0_ffn_W2").reshape(EXPERTS, FT, 128, D).transpose(2, 0, 1, 3).reshape(128, -1)], axis=1),
        "mo_w_g": f("L0_ffn_Wg")[[0, 1, 2, 3, 0]].reshape(ROUNDS + 1, KC, 128, EXPERTS).transpose(2, 1, 0, 3),
        "mo_b_g": f("L0_ffn_bg")[[0, 1, 2, 3, 0]][None],
        "mo_b_1": f("L0_ffn_b1").reshape(EXPERTS * FT, 128).T, "mo_b_2": f("L0_ffn_b2"),
        "one_row": np.repeat(np.eye(EXPERTS, dtype=np.float32)[:, :, None], 128, axis=2),
        "before": np.stack([np.tri(EXPERTS, k=-1), np.tri(EXPERTS, k=-1).T]).astype(np.float32)[None],
        "re_w": pairs(np.concatenate([f("L1_attn_W" + n) for n in "qkvg"], axis=1)), "re_w_o": pairs(f("L1_attn_Wo")),
        "re_bias": np.concatenate([f("L1_attn_b" + n) for n in "qkvg"])[None],
        "re_rows3": np.stack([f("L1_attn_bo"), f("L1_attn_gamma"), f("L1_attn_beta")])[None],
        "decay": np.stack([0.25 * 0.99 ** np.arange(S), 0.99 ** -np.arange(S).astype(np.float64)], axis=1)
        .astype(np.float32).reshape(NCH, CHUNK, 2).transpose(1, 0, 2),
        "causal": np.tri(CHUNK, dtype=np.float32).T, "head_of": np.kron(np.eye(8, dtype=np.float32), np.ones((16, 1), np.float32)),
        "router": pairs(f("L1_ffn_router_w").T), "early": np.tri(CHUNK, k=-1, dtype=np.float32).T,
        "keep": (np.arange(NEXP * NT) % NT != 0).astype(np.float32)[None],
        "numbers": np.concatenate([np.arange(NEXP) - NEXP, np.arange(G_TILES)]).astype(np.float32)[None],
        "sh_w": np.concatenate([
            np.stack([f("L1_ffn_shared_gate_w"), f("L1_ffn_shared_up_w")]).reshape(2, ST, 128, KC, 128)
            .transpose(4, 1, 0, 3, 2).reshape(128, -1),
            f("L1_ffn_shared_down_w").T.reshape(ST, 128, D).transpose(1, 0, 2).reshape(128, -1)], axis=1),
        "ex_gu": f("L1_ffn_gate_up_proj").reshape(NEXP, KC, 128, 2 * EF).transpose(2, 0, 1, 3),
        "ex_d": f("L1_ffn_down_proj").reshape(NEXP, EF // 128, 128, D).transpose(2, 0, 1, 3),
        "ident": np.eye(128, dtype=np.float32),
    }
    return {k: np.ascontiguousarray(v) for k, v in io.items()}


def kernel(**inputs):
    import concourse.bacc as _bacc
    from concourse.bass_utils import run_bass_kernel_spmd as _run

    nc = _bacc.Bacc("TRN2", target_bir_lowering=False, num_devices=1)
    arrays, io = {}, {}
    for name, a in host_arrays(inputs).items():
        arrays[f"in_{name}_dram"] = a
        io[name] = nc.dram_tensor(f"in_{name}_dram", a.shape, mybir.dt.from_np(a.dtype), kind="ExternalInput").ap()
    out = nc.dram_tensor("out_0_dram", (B, S, D), F32, kind="ExternalOutput").ap()
    build(nc, io, out)
    r = _run(nc, [arrays], core_ids=[0])
    return r.results[0]["out_0_dram"]
```

```python
from contextlib import ExitStack, contextmanager

import concourse.bass as bass
from concourse import mybir

F32 = mybir.dt.float32
F32R = mybir.dt.float32r
I32 = mybir.dt.int32
U32 = mybir.dt.uint32
ALU = mybir.AluOpType
ACT = mybir.ActivationFunctionType
AX = mybir.AxisListType
ds = bass.ds

B, SSM_ROWS, TXT_ROWS, D = 8, 256, 77, 256
S = SSM_ROWS + TXT_ROWS
CHUNK = S // 3
NCH = S // CHUNK
NT = B * NCH
T = B * S
KC = D // 128
MODES = 64
NA, NB = 8, 32
CA = B * NA
HG = 16
CUT = (0, 5000, 10000, 50257)
TXT_AT = SSM_ROWS - (NCH - 1) * CHUNK
HEADS, DH = 16, 16
LN_EPS = 1e-05


class Chain:

    def __init__(self, eng, sem, start=0):
        self.eng, self.sem, self.start, self.n = eng, sem, start, 0

    def step(self, ins):
        ins.then_inc(self.sem, 1)
        self.n += 1

    def wait(self):
        self.eng.wait_ge(self.sem, self.start + self.n)


def exact_exp(c, out, x, power, rest):
    v = c.eng
    c.step(v.tensor_scalar(x, x, -87.0, 88.0, ALU.max, ALU.min))
    c.wait()
    c.step(v.tensor_scalar(power, x, 1.4426950408889634, 12582912.0, ALU.mult, ALU.add))
    c.wait()
    c.step(v.tensor_scalar(rest, power, 12582912.0, None, ALU.subtract))
    c.wait()
    c.step(v.scalar_tensor_tensor(x, rest, -0.693359375, x, ALU.mult, ALU.add))
    c.wait()
    c.step(v.scalar_tensor_tensor(x, rest, 2.12194440054690583e-4, x, ALU.mult, ALU.add))
    bits = power.bitcast(I32)
    c.step(v.tensor_scalar(bits, bits, 23, None, ALU.logical_shift_left))
    c.wait()
    c.step(v.tensor_scalar(bits, bits, 127 << 23, None, ALU.add))
    c.step(v.tensor_scalar(out, x, 1 / 5040, None, ALU.mult))
    for k in (720, 120, 24, 6, 2, 1):
        c.wait()
        c.step(v.scalar_tensor_tensor(out, out, 1 / k, x, ALU.add, ALU.mult))
    c.wait()
    c.step(v.scalar_tensor_tensor(out, out, 1.0, power, ALU.add, ALU.mult))
    c.wait()


@contextmanager
def cleared_semaphores(nc, prefix):
    sems = []

    def sem(name):
        sems.append(nc.alloc_semaphore(name=prefix + name))
        return sems[-1]

    yield sem
    nc.clear_and_free_semaphores(sems)
    nc.all_engine_barrier()


def embed_tokens(nc, io, h, ident, ident_ready):
    with ExitStack() as ctx:
        def sb(name, shape, dt=F32):
            return ctx.enter_context(nc.sbuf_tensor(name, shape, dt))

        def sem(name):
            return ctx.enter_context(nc.semaphore(name))

        pool_ram = sb("pool_ram", [128, 2 * B * D + NB // 2 * D])
        ssm_x = pool_ram[:, 0:2 * B * D].rearrange("p (s c h) -> p s c h", s=2, c=B)
        z_swap = pool_ram[:, 2 * B * D:].rearrange("p (b h) -> p b h", h=D)
        prod = pool_ram[0:CA].rearrange("p (h b) -> p h b", b=NB)
        left_h = sb("left_h", [128, 2, HG, CA])
        z_low = sb("z_low", [128, NB, D])
        left = sb("left", [128, B, NA, D])
        ct_im = sb("ct_im", [128, B, D])
        w_hi = sb("w_hi", [128, 2, NA, D])
        par = sb("par", [128, 5, D])
        tmp = sb("tmp", [128, 6, D])
        sq = sb("sq", [128, 5, 2, D])
        sign = sb("sign", [128, 1])
        loaded, params = sem("ssm_loaded"), sem("ssm_params")
        dve, pool = sem("ssm_dve"), sem("ssm_pool")
        left_done, low_done = sem("ssm_left"), sem("ssm_low")
        staged, multiplied, stored = sem("ssm_staged"), sem("ssm_multiplied"), sem("ssm_stored")
        turned, kept_even, kept_odd = sem("ssm_turned"), sem("ssm_kept_even"), sem("ssm_kept_odd")
        product = ctx.enter_context(nc.psum_tensor("ssm_product", [128, 2, HG, NB], F32))
        rows_ps = ctx.enter_context(nc.psum_tensor("ssm_rows", [128, 2, 8, CA], F32))
        block = ctx.enter_context(nc.Block())

        scratch = left[:].rearrange("p c a h -> p (c a) h")

        turns = [(j, g) for g in range(NB // 8) for j in range(NCH)]

        def rows_of(j):
            return min(CHUNK, D - j * CHUNK)

        def row_in(n, j):
            return rows_ps[0:rows_of(j), n % 2].rearrange("p b (c a) -> p c a b", a=NA)

        def row_out(j, g):
            out = h[0:rows_of(j)].rearrange("p (c j) (a b) -> p j c a b", j=NCH, b=NB)
            return out[:, j, :, :, 8 * g:8 * g + 8]

        @block.sync
        def _(sp):
            sp.dma_start(ident[:], io["ident"]).then_inc(ident_ready, 16)
            for half in range(2):
                rows = slice(64 * half, 64 * half + 64)
                sp.dma_start(par[rows, 0, :], io["log_dt"].rearrange("(o h) -> o h", o=1).broadcast_to([64, D])).then_inc(params, 16)
                sp.dma_start(par[rows, 1, :], io["inv_A_real"]).then_inc(params, 16)
                sp.dma_start(par[rows, 2, :], io["A_imag"]).then_inc(params, 16)
                sp.dma_start(par[rows, 3, :], io["B_ri"][0]).then_inc(params, 16)
                sp.dma_start(par[rows, 4, :], io["B_ri"][1]).then_inc(params, 16)
            sp.dma_start(sign[:], io["sign"]).then_inc(params, 16)
            sp.dma_start(ssm_x[:, 0], io["x"].rearrange("r n c h -> (r n) c h")).then_inc(loaded, 16)
            sp.dma_start(ssm_x[0:64, 1], io["x"][1]).then_inc(loaded, 16)
            sp.dma_start(ssm_x[64:128, 1], io["x"][0]).then_inc(loaded, 16)

        @block.scalar
        def _(act):
            act.wait_ge(left_done, NA)
            with act.Fori(0, D // HG // 2) as i:
                for p in range(2):
                    act.wait_ge(multiplied, i * 2 + p + 1)
                    nc.scalar.copy(left_h[:, p].rearrange("p h c -> p c h"),
                                   scratch[:, :, ds(i * 2 * HG + p * HG, HG)]).then_inc(staged, 1)
            for n, (j, g) in enumerate(turns):
                if n % 2:
                    act.wait_ge(turned, n + 1)
                    nc.scalar.copy(row_out(j, g), row_in(n, j)).then_inc(kept_odd, 1)

        @block.vector
        def _(v):
            c = Chain(v, dve)
            v.sem_inc(stored, 2)

            def tt(out, a, b, op):
                c.step(v.tensor_tensor(out, a, b, op))

            dt, ea, t2, t3, ur, ui = (tmp[:, k, :] for k in range(6))
            v.wait_ge(params, 16 * 11)
            exact_exp(c, tmp[:, 0:2, :], par[:, 0:2, :], tmp[:, 2:4, :], tmp[:, 4:6, :])
            c.step(v.scalar_tensor_tensor(ur, ea, -0.5, dt, ALU.mult, ALU.mult))
            c.step(v.scalar_tensor_tensor(ui, par[:, 2, :], 0.5, dt, ALU.mult, ALU.mult))
            c.wait()
            c.step(v.tensor_scalar(t2, ur, -1.0, 1.0, ALU.mult, ALU.add))
            tt(t3, ui, ui, ALU.mult)
            tt(ea, ur, ur, ALU.mult)
            c.wait()
            tt(t2, t2, t2, ALU.mult)
            tt(ea, ea, t3, ALU.add)
            c.wait()
            tt(t2, t2, t3, ALU.add)
            c.step(v.tensor_scalar(ea, ea, -1.0, 1.0, ALU.mult, ALU.add))
            c.wait()
            c.step(v.reciprocal(t2, t2))
            c.wait()
            tt(sq[:, 0, 0, :], ea, t2, ALU.mult)
            c.step(v.scalar_tensor_tensor(sq[:, 0, 1, :], ui, 2.0, t2, ALU.mult, ALU.mult))
            power = [(sq[:, k, 0, :], sq[:, k, 1, :]) for k in range(5)]
            power += [(w_hi[:, 0, a, :], w_hi[:, 1, a, :]) for a in (1, 2, 4)]
            for k in range(7):
                (re, im), (re2, im2) = power[k], power[k + 1]
                c.wait()
                tt(t2, re, re, ALU.mult)
                tt(t3, im, im, ALU.mult)
                c.step(v.scalar_tensor_tensor(im2, re, 2.0, im, ALU.mult, ALU.mult))
                c.wait()
                tt(re2, t2, t3, ALU.subtract)
            c.step(v.memset(w_hi[:, 0, 0, :], 1.0))
            c.step(v.memset(w_hi[:, 1, 0, :], 0.0))
            c.wait()
            for n, lo, by, to in ((1, 1, 2, 3), (3, 1, 4, 5)):
                ar, ai = w_hi[:, 0, lo:lo + n, :], w_hi[:, 1, lo:lo + n, :]
                br = w_hi[:, 0, by:by + 1, :].broadcast_to([128, n, D])
                bi = w_hi[:, 1, by:by + 1, :].broadcast_to([128, n, D])
                m = [scratch[:, 3 * k:3 * k + n, :] for k in range(4)]
                tt(m[0], ar, br, ALU.mult)
                tt(m[1], ai, bi, ALU.mult)
                tt(m[2], ar, bi, ALU.mult)
                tt(m[3], ai, br, ALU.mult)
                c.wait()
                tt(w_hi[:, 0, to:to + n, :], m[0], m[1], ALU.subtract)
                tt(w_hi[:, 1, to:to + n, :], m[2], m[3], ALU.add)
                c.wait()
            c.step(v.memset(z_low[0:64, 0, :], 1.0))
            c.step(v.memset(z_low[64:128, 0, :], 0.0))
            c.step(v.memset(z_swap[0:64, 0, :], 0.0))
            c.step(v.memset(z_swap[64:128, 0, :], 1.0))
            for k in range(5):
                n = 1 << k
                wr = sq[:, k, 0:1, :].broadcast_to([128, n, D])
                wi = sq[:, k, 1:2, :].broadcast_to([128, n, D])
                z0, s0 = z_low[:, 0:n, :], z_swap[:, 0:n, :]
                z1 = z_low[:, n:2 * n, :]
                ta, tb = scratch[:, 0:n, :], scratch[:, 16:16 + n, :]
                c.wait()
                tt(ta, s0, wi, ALU.mult)
                tt(z1, z0, wr, ALU.mult)
                if k < 4:
                    s1 = z_swap[:, n:2 * n, :]
                    tt(tb, z0, wi, ALU.mult)
                    tt(s1, s0, wr, ALU.mult)
                c.wait()
                tt(z1, z1, ta, ALU.add)
                if k < 4:
                    tt(s1, s1, tb, ALU.subtract)
            c.step(v.tensor_scalar(tmp[:, 0, :], par[:, 3, :], sign[:, 0:1], 2.0, ALU.mult, ALU.mult))
            c.step(v.tensor_scalar(tmp[:, 1, :], par[:, 4, :], 2.0, None, ALU.mult))
            c.step(v.tensor_scalar(tmp[:, 2, :], par[:, 3, :], -2.0, None, ALU.mult))
            c.step(v.tensor_scalar(tmp[:, 3, :], par[:, 4, :], sign[:, 0:1], -2.0, ALU.mult, ALU.mult))
            c.wait()
            v.wait_ge(loaded, 48)
            coef = [tmp[:, k:k + 1, :].broadcast_to([128, B, D]) for k in range(4)]
            x1, x2 = ssm_x[:, 0], ssm_x[:, 1]
            spare = left[:, :, 1, :]
            tt(left[:, :, 0, :], x1, coef[0], ALU.mult)
            tt(spare, x2, coef[1], ALU.mult)
            tt(ct_im[:], x2, coef[2], ALU.mult)
            c.wait()
            tt(left[:, :, 0, :], left[:, :, 0, :], spare, ALU.subtract)
            tt(left[:, :, 2, :], x1, coef[3], ALU.mult)
            c.wait()
            tt(ct_im[:], ct_im[:], left[:, :, 2, :], ALU.add)
            c.wait()
            for a in range(1, NA):
                wr = w_hi[:, 0, a:a + 1, :].broadcast_to([128, B, D])
                if a == 1:
                    v.sem_inc(left_done, 1)
                tt(left[:, :, a, :], left[:, :, 0, :], wr, ALU.mult)
                c.wait()
                v.wait_ge(pool, a)
                v.tensor_tensor(left[:, :, a, :], left[:, :, a, :], ssm_x[:, a % 2], ALU.add).then_inc(left_done, 1)
            v.wait_ge(left_done, NA)
            with v.Fori(0, D // HG // 2) as i:
                for p in range(2):
                    v.wait_ge(multiplied, i * 2 + p + 3)
                    v.tensor_copy(prod[:, ds(i * 2 * HG + p * HG, HG), :], product[0:CA, p]).then_inc(stored, 1)
            for n, (j, g) in enumerate(turns):
                if n % 2 == 0:
                    v.wait_ge(turned, n + 1)
                    v.tensor_copy(row_out(j, g), row_in(n, j)).then_inc(kept_even, 1)

        @block.tensor
        def _(pe):
            pe.sem_inc(multiplied, 2)
            with pe.Fori(0, D // HG // 2) as i:
                for p in range(2):
                    pe.wait_ge(staged, i * 2 + p + 1)
                    pe.wait_ge(stored, i * 2 + p + 1)
                    for k in range(HG):
                        mm = pe.matmul(product[0:CA, p, k, :], left_h[:, p, k, :],
                                       z_low[:, :, ds(i * 2 * HG + p * HG + k, 1)].rearrange("p b o -> p (b o)"),
                                       start=True, stop=True)
                    mm.then_inc(multiplied, 1)
            pe.wait_ge(stored, D // HG + 2)
            pe.wait_ge(ident_ready, 16)
            for n, (j, g) in enumerate(turns):
                if n >= 2:
                    pe.wait_ge(kept_odd if n % 2 else kept_even, n // 2)
                w = rows_of(j)
                for k in range(8):
                    mm = pe.transpose(rows_ps[0:w, n % 2, k, :], prod[:, j * CHUNK:j * CHUNK + w, 8 * g + k],
                                      ident[0:CA, 0:CA])
                mm.then_inc(turned, 1)

        @block.gpsimd
        def _(g):
            for a in range(1, NA):
                g.wait_ge(left_done, 1 if a < 3 else a - 1)
                wi = w_hi[:, 1, a:a + 1, :].broadcast_to([128, B, D])
                g.tensor_tensor(ssm_x[:, a % 2], ct_im[:], wi, ALU.mult).then_inc(pool, 1)


def embed_text(nc, io, h, ident, ident_ready):
    with ExitStack() as ctx:
        def sb(name, shape, dt=F32):
            return ctx.enter_context(nc.sbuf_tensor(name, shape, dt))

        def sem(name):
            return ctx.enter_context(nc.semaphore(name))

        NBAND = len(CUT) - 1
        col = (0, 256, 320, 384)
        KT = col[-1] // 128
        tokens = sb("txt_tokens", [TXT_ROWS, B], I32)
        row = sb("txt_row", [TXT_ROWS, NBAND, B], I32)
        inside = sb("txt_inside", [TXT_ROWS, NBAND, B])
        below = sb("txt_below", [TXT_ROWS, NBAND, B])
        emb = sb("txt_emb", [TXT_ROWS, B, col[-1]])
        masked = sb("txt_masked", [TXT_ROWS, 2, col[-1]])
        emb_t = sb("txt_emb_t", [128, 2, KT, TXT_ROWS])
        w = sb("txt_w", [128, KT, D])
        res = sb("txt_res", [TXT_ROWS, B, D])
        turn_ps = ctx.enter_context(nc.psum_tensor("txt_turn", [128, 2, 512], F32))
        out_ps = ctx.enter_context(nc.psum_tensor("txt_out", [128, 2, 512], F32))
        loaded, wloaded, dve, gathered = sem("txt_loaded"), sem("txt_wloaded"), sem("txt_dve"), sem("txt_gathered")
        masked_ok, turned, copied, multiplied = sem("txt_masked_ok"), sem("txt_turned"), sem("txt_copied"), sem("txt_mult")
        res_ok, placed = sem("txt_res_ok"), sem("txt_placed")
        block = ctx.enter_context(nc.Block())

        @block.sync
        def _(sp):
            sp.dma_start(tokens[:], io["x_txt"]).then_inc(loaded, 16)
            sp.dma_start(w[:], io["W_txt"]).then_inc(wloaded, 16)
            sp.wait_ge(res_ok, B)
            last = h[:].rearrange("p (c j) d -> p c j d", j=NCH)[TXT_AT:CHUNK, :, NCH - 1, :]
            sp.dma_start(last, res[:]).then_inc(placed, 16)
            sp.wait_ge(placed, 16)

        @block.gpsimd
        def _(g):
            g.wait_ge(dve, 3 * NBAND)
            for b in range(B):
                for k in range(NBAND):
                    g.indirect_dma_start(
                        emb[:, b, col[k]:col[k + 1]], None, io[f"E{k}"],
                        bass.IndirectOffsetOnAxis(ap=row[:, k, b:b + 1].bitcast(U32), axis=0)).then_inc(gathered, 16)

        @block.vector
        def _(v):
            c = Chain(v, dve)
            v.wait_ge(loaded, 16)
            for k in range(NBAND):
                c.step(v.tensor_scalar(row[:, k, :], tokens[:], -CUT[k], 0, ALU.add, ALU.max))
                c.step(v.tensor_scalar(inside[:, k, :], tokens[:], CUT[k], None, ALU.is_ge))
            c.wait()
            for k in range(NBAND):
                v.tensor_scalar(below[:, k, :], tokens[:], CUT[k + 1], None, ALU.is_lt)
                c.step(v.tensor_scalar(row[:, k, :], row[:, k, :], CUT[k + 1] - CUT[k] - 1, None, ALU.min))
            c.wait()
            c.step(v.tensor_tensor(inside[:], inside[:], below[:], ALU.mult))
            c.wait()
            v.wait_ge(gathered, 16 * NBAND * B)
            v.sem_inc(turned, 2)
            with v.Fori(0, B // 2) as i:
                for p in range(2):
                    v.wait_ge(turned, i * 2 + p + 1)
                    for k in range(NBAND):
                        ins = v.tensor_scalar(masked[:, p, col[k]:col[k + 1]],
                                              emb[:, ds(i * 2 + p, 1), col[k]:col[k + 1]].rearrange("p o d -> p (o d)"),
                                              inside[:, k, ds(i * 2 + p, 1)], None, ALU.mult)
                    ins.then_inc(masked_ok, 1)
                    v.wait_ge(multiplied, i * 2 + p + 1)
                    v.tensor_copy(res[:, ds(i * 2 + p, 1), :].rearrange("p o d -> p (o d)"),
                                  out_ps[0:TXT_ROWS, p, 0:D]).then_inc(res_ok, 1)

        @block.scalar
        def _(act):
            with act.Fori(0, B // 2) as i:
                for p in range(2):
                    act.wait_ge(turned, i * 2 + p + 3)
                    nc.scalar.copy(emb_t[:, p].rearrange("p k t -> p (k t)"),
                                   turn_ps[:, p, 0:KT * TXT_ROWS]).then_inc(copied, 1)

        @block.tensor
        def _(pe):
            pe.wait_ge(ident_ready, 16)
            pe.wait_ge(wloaded, 16)
            with pe.Fori(0, B // 2) as i:
                for p in range(2):
                    pe.wait_ge(masked_ok, i * 2 + p + 1)
                    for k in range(KT):
                        mm = pe.transpose(turn_ps[:, p, k * TXT_ROWS:(k + 1) * TXT_ROWS],
                                          masked[:, p, 128 * k:128 * k + 128], ident[0:TXT_ROWS, 0:TXT_ROWS])
                    mm.then_inc(turned, 1)
                    pe.wait_ge(copied, i * 2 + p + 1)
                    for k in range(KT):
                        mm = pe.matmul(out_ps[0:TXT_ROWS, p, 0:D], emb_t[:, p, k, :], w[:, k, :],
                                       start=(k == 0), stop=(k == KT - 1))
                    mm.then_inc(multiplied, 1)


def row_stats(c, src, stats, mv, n=NT):
    v = c.eng
    with v.Fori(0, n) as t:
        v.bn_stats(stats[:, ds(t, 1), :].rearrange("p o s -> p (o s)"),
                   src[:, ds(t, 1), :].rearrange("p o d -> p (o d)")).then_inc(c.sem, 1)
    c.n += n
    c.wait()
    moments(c, stats, mv)


def moments(c, stats, mv):
    v = c.eng
    mean, var = mv[:, :, 0], mv[:, :, 1]
    c.step(v.tensor_tensor(mean, stats[:, :, 1], stats[:, :, 4], ALU.add))
    c.step(v.tensor_tensor(var, stats[:, :, 1], stats[:, :, 4], ALU.subtract))
    c.step(v.tensor_tensor(stats[:, :, 0], stats[:, :, 2], stats[:, :, 5], ALU.add))
    c.wait()
    c.step(v.tensor_scalar(mean, mean, 0.5, None, ALU.mult))
    c.step(v.tensor_tensor(stats[:, :, 3], var, var, ALU.mult))
    c.step(v.tensor_scalar(stats[:, :, 0], stats[:, :, 0], 1 / D, None, ALU.mult))
    c.wait()
    c.step(v.scalar_tensor_tensor(var, stats[:, :, 3], 0.25, stats[:, :, 0], ALU.mult, ALU.add))
    c.wait()


def inverse_root(c, var_eps, root, inv, spare):
    v = c.eng
    c.step(v.reciprocal(inv, root))
    c.wait()
    c.step(v.tensor_tensor(spare, inv, inv, ALU.mult))
    c.wait()
    c.step(v.tensor_tensor(spare, spare, var_eps, ALU.mult))
    c.wait()
    c.step(v.tensor_scalar(spare, spare, -0.5, 1.5, ALU.mult, ALU.add))
    c.wait()
    c.step(v.tensor_tensor(inv, inv, spare, ALU.mult))
    c.wait()


def normalise(nc, name, src, dst_t, ident, ident_ready):
    with ExitStack() as ctx:
        def sb(what, shape, dt=F32):
            return ctx.enter_context(nc.sbuf_tensor(f"{name}_{what}", shape, dt))

        def sem(what):
            return ctx.enter_context(nc.semaphore(f"{name}_{what}"))

        stats = sb("stats", [CHUNK, NT, 6])
        mv = sb("mv", [CHUNK, NT, 2])
        small = sb("small", [CHUNK, 4, NT])
        rows = sb("rows", [CHUNK, 2, D])
        ps = ctx.enter_context(nc.psum_tensor(f"{name}_ps", [128, 2, 512], F32))
        dve, var_ready, root_done = sem("dve"), sem("var_ready"), sem("root_done")
        rows_ok, turned, copied = sem("rows_ok"), sem("turned"), sem("copied")
        block = ctx.enter_context(nc.Block())

        @block.vector
        def _(v):
            c = Chain(v, dve)
            row_stats(c, src, stats, mv)
            v.tensor_scalar(small[:, 0, :], mv[:, :, 1], LN_EPS, None, ALU.add).then_inc(var_ready, 1)
            v.wait_ge(root_done, 1)
            inverse_root(c, small[:, 0, :], small[:, 1, :], small[:, 2, :], small[:, 3, :])
            with v.Fori(0, NT // 2) as i:
                for p in range(2):
                    t = i * 2 + p
                    v.wait_ge(turned, t + 1)
                    v.tensor_scalar(rows[:, p, :], src[:, ds(t, 1), :].rearrange("p o d -> p (o d)"),
                                    mv[:, ds(t, 1), 0], small[:, 2, ds(t, 1)],
                                    ALU.subtract, ALU.mult).then_inc(rows_ok, 1)

        @block.scalar
        def _(act):
            act.wait_ge(var_ready, 1)
            nc.scalar.sqrt(small[:, 1, :], small[:, 0, :]).then_inc(root_done, 1)
            act.sem_inc(copied, 2)
            with act.Fori(0, NT // 2) as i:
                for p in range(2):
                    t = i * 2 + p
                    act.wait_ge(turned, t + 3)
                    nc.scalar.copy(dst_t[:, :, ds(t * CHUNK, CHUNK)],
                                   ps[:, p, 0:KC * CHUNK].rearrange("p (k t) -> p k t", k=KC)).then_inc(copied, 1)

        @block.tensor
        def _(pe):
            pe.wait_ge(ident_ready, 16)
            pe.sem_inc(turned, 2)
            with pe.Fori(0, NT // 2) as i:
                for p in range(2):
                    t = i * 2 + p
                    pe.wait_ge(rows_ok, t + 1)
                    pe.wait_ge(copied, t + 1)
                    for k in range(KC):
                        mm = pe.transpose(ps[:, p, k * CHUNK:(k + 1) * CHUNK], rows[:, p, 128 * k:128 * k + 128],
                                          ident[0:CHUNK, 0:CHUNK])
                    mm.then_inc(turned, 1)


def linear_attention(nc, io, h, x_t, to_zero, ident, ident_ready):
    with ExitStack() as ctx:
        def sb(name, shape, dt=F32):
            return ctx.enter_context(nc.sbuf_tensor("la_" + name, shape, dt))

        sem = ctx.enter_context(cleared_semaphores(nc, "la_"))

        qv = sb("qv", [CHUNK, NT, 2 * D])
        k_t = sb("k_t", [128, KC, B, S])
        out = sb("out", [CHUNK, NT, D])
        w_qv = sb("w_qv", [128, KC, 2 * D])
        w_k = sb("w_k", [128, KC, D])
        w_o = sb("w_o", [128, KC, D])
        b_qv = sb("b_qv", [CHUNK, 2 * D])
        b_o = sb("b_o", [CHUNK, D])
        cols = sb("cols", [128, 3, KC])
        head_mask = sb("head_mask", [128, 128])
        x_s = sb("x_s", [128, 2, KC, CHUNK])
        k_max = sb("k_max", [128, KC, B])
        k_sum = sb("k_sum", [128, KC, B])
        k_inv = sb("k_inv", [128, KC, B])
        k_exp = sb("k_exp", [128, 2, S])
        k_rows = sb("k_rows", [CHUNK, 2, NCH, 128])
        q_rows = sb("q_rows", [CHUNK, 2, NCH, 128])
        q_t = sb("q_t", [128, 2, NCH, CHUNK])
        state = sb("state", [128, 2, 128])
        q_red = sb("q_red", [CHUNK, NT, HEADS])
        q_inv = sb("q_inv", [CHUNK, NT, HEADS])
        stats = sb("stats", [CHUNK, NT, 6])
        mv = sb("mv", [CHUNK, NT, 2])
        small = sb("small", [CHUNK, 4, NT])
        loaded, dve, x_copied, projected = sem("loaded"), sem("dve"), sem("x_copied"), sem("projected")
        qv_ok, k_mult, k_ok, k_max_ok = sem("qv_ok"), sem("k_mult"), sem("k_ok"), sem("k_max_ok")
        q_sub, q_exp, k_exp_ok, k_turned = sem("q_sub"), sem("q_exp"), sem("k_exp_ok"), sem("k_turned")
        k_rows_ok, q_rows_ok, q_turned, q_t_ok = sem("k_rows_ok"), sem("q_rows_ok"), sem("q_turned"), sem("q_t_ok")
        state_mult, state_ok, out_mult, out_ok = sem("state_mult"), sem("state_ok"), sem("out_mult"), sem("out_ok")
        var_ready, root_done, n_ok, n_turned = sem("var_ready"), sem("root_done"), sem("n_ok"), sem("n_turned")
        n_t_ok, o_mult, h_ok, bias_added = sem("n_t_ok"), sem("o_mult"), sem("h_ok"), sem("bias_added")
        k_inv_ok, zero_ok, zeroed = sem("k_inv_ok"), sem("zero_ok"), sem("zeroed")
        zeros = sb("zeros", [128, D])
        ps = ctx.enter_context(nc.psum_tensor("la_ps", [128, 8, 512], F32))
        block = ctx.enter_context(nc.Block())
        NQ = 4
        TQ = NT // NQ

        def heads(ap):
            return ap.rearrange("p t (g e) -> p t g e", e=DH)

        def q_part(n):
            return heads(qv[:, TQ * n:TQ * n + TQ, 0:D])

        @block.sync
        def _(sp):
            sp.dma_start(w_qv[:], io["la_w_qv"]).then_inc(loaded, 16)
            sp.dma_start(w_k[:], io["la_w_k"]).then_inc(loaded, 16)
            sp.dma_start(w_o[:], io["la_w_o"]).then_inc(loaded, 16)
            sp.dma_start(b_qv[:], io["la_b_qv"].broadcast_to([CHUNK, 2 * D])).then_inc(loaded, 16)
            sp.dma_start(b_o[:], io["la_b_o"].broadcast_to([CHUNK, D])).then_inc(loaded, 16)
            sp.dma_start(cols[:], io["la_cols"]).then_inc(loaded, 16)
            sp.dma_start(head_mask[:], io["head_mask"]).then_inc(loaded, 16)
            sp.wait_ge(zero_ok, 1)
            for ap in to_zero:
                sp.dma_start(ap.rearrange("(p n) d -> p n d", p=128),
                             zeros[:].unsqueeze(1).broadcast_to([128, ap.shape[0] // 128, D])).then_inc(zeroed, 16)
            sp.wait_ge(zeroed, 16 * len(to_zero))

        @block.gpsimd
        def _(g):
            g.memset(zeros[:], 0.0).then_inc(zero_ok, 1)
            with g.Fori(0, NT // 2) as i:
                for p in range(2):
                    t = i * 2 + p
                    g.wait_ge(projected, t + 1)
                    g.tensor_copy(x_s[:, p], x_t[:, :, ds(t * CHUNK, CHUNK)]).then_inc(x_copied, 1)
            g.wait_ge(loaded, 16 * 7)
            g.tensor_tensor(h[:], h[:], b_o[:].unsqueeze(1).broadcast_to([CHUNK, NT, D]), ALU.add).then_inc(bias_added, 1)

        @block.tensor
        def _(pe):
            for s in (projected, k_turned, state_mult, q_turned, out_mult, n_turned, o_mult):
                pe.sem_inc(s, 2)
            pe.wait_ge(loaded, 16 * 7)
            pe.wait_ge(ident_ready, 16)
            with pe.Fori(0, NT // 2) as i:
                for p in range(2):
                    t = i * 2 + p
                    pe.wait_ge(x_copied, t + 1)
                    pe.wait_ge(qv_ok, t + 1)
                    for k in range(KC):
                        mm = pe.matmul(ps[0:CHUNK, p, :], x_s[:, p, k, :], w_qv[:, k, :], start=(k == 0), stop=(k == KC - 1))
                    mm.then_inc(projected, 1)
            with pe.Fori(0, B) as b:
                for m in range(KC):
                    pe.wait_ge(k_ok, b * KC + m + 1)
                    for k in range(KC):
                        mm = pe.matmul(ps[:, 2 + m, 0:S], w_k[:, k, 128 * m:128 * m + 128],
                                       x_t[:, k, ds(b * S, S)], start=(k == 0), stop=(k == KC - 1))
                    mm.then_inc(k_mult, 1)
            pe.wait_ge(qv_ok, NT + 2)
            pe.wait_ge(k_ok, B * KC + 2)
            def turn_parts(b):
                for m in range(KC):
                    pe.wait_ge(k_exp_ok, b * KC + m + 1)
                    pe.wait_ge(k_rows_ok, b * KC + m + 1)
                    for j in range(NCH):
                        mm = pe.transpose(ps[0:CHUNK, m, 128 * j:128 * j + 128], k_exp[:, m, j * CHUNK:(j + 1) * CHUNK],
                                          ident[:])
                    mm.then_inc(k_turned, 1)
                for m in range(KC):
                    pe.wait_ge(q_rows_ok, b * KC + m + 1)
                    pe.wait_ge(q_t_ok, b * KC + m + 1)
                    for j in range(NCH):
                        mm = pe.transpose(ps[:, 2 + m, CHUNK * j:CHUNK * (j + 1)], q_rows[:, m, j, :],
                                          ident[0:CHUNK, 0:CHUNK])
                    mm.then_inc(q_turned, 1)

            def state_and_output(b):
                for m in range(KC):
                    pe.wait_ge(k_rows_ok, b * KC + m + 3)
                    pe.wait_ge(state_ok, b * KC + m + 1)
                    for j in range(NCH):
                        mm = pe.matmul(ps[:, 4 + m, 0:128], k_rows[:, m, j, :],
                                       qv[:, ds(b * NCH + j, 1), D + 128 * m:D + 128 * m + 128].rearrange("p o d -> p (o d)"),
                                       start=(j == 0), stop=(j == NCH - 1))
                    mm.then_inc(state_mult, 1)
                for m in range(KC):
                    pe.wait_ge(state_ok, b * KC + m + 3)
                    pe.wait_ge(q_t_ok, b * KC + m + 3)
                    pe.wait_ge(out_ok, b * KC + m + 1)
                    for j in range(NCH):
                        mm = pe.matmul(ps[0:CHUNK, 6 + m, 128 * j:128 * j + 128], q_t[:, m, j, :], state[:, m, :],
                                       start=True, stop=True)
                    mm.then_inc(out_mult, 1)

            turn_parts(0)
            with pe.Fori(0, B - 1) as b:
                turn_parts(b + 1)
                state_and_output(b)
            state_and_output(B - 1)
            def turn_pair(i):
                for p in range(2):
                    t = i * 2 + p
                    pe.wait_ge(n_ok, t + 1)
                    pe.wait_ge(n_t_ok, t + 1)
                    for k in range(KC):
                        mm = pe.transpose(ps[:, p, k * CHUNK:(k + 1) * CHUNK], q_rows[:, p, k, :],
                                          ident[0:CHUNK, 0:CHUNK])
                    mm.then_inc(n_turned, 1)

            def project_pair(i):
                for p in range(2):
                    t = i * 2 + p
                    pe.wait_ge(n_t_ok, t + 3)
                    pe.wait_ge(h_ok, t + 1)
                    for k in range(KC):
                        mm = pe.matmul(ps[0:CHUNK, 2 + p, 0:D], x_s[:, p, k, :], w_o[:, k, :],
                                       start=(k == 0), stop=(k == KC - 1))
                    mm.then_inc(o_mult, 1)

            turn_pair(0)
            with pe.Fori(0, NT // 2 - 1) as i:
                project_pair(i)
                turn_pair(i + 1)
            project_pair(NT // 2 - 1)

        @block.scalar
        def _(act):
            for s in (k_ok, q_t_ok, out_ok, n_t_ok):
                act.sem_inc(s, 2)
            act.wait_ge(loaded, 16 * 7)
            with act.Fori(0, B) as b:
                for m in range(KC):
                    act.wait_ge(k_mult, b * KC + m + 1)
                    nc.scalar.activation(k_t[:, m, ds(b, 1), :].rearrange("p o s -> p (o s)"), ps[:, 2 + m, 0:S],
                                         ACT.Identity, bias=cols[:, 0, m:m + 1]).then_inc(k_ok, 1)
            for n in range(NQ):
                act.wait_ge(q_sub, n + 1)
                nc.scalar.activation(q_part(n), q_part(n), ACT.Exp).then_inc(q_exp, 1)
            act.wait_ge(k_max_ok, 1)
            def exp_k(b):
                for m in range(KC):
                    act.wait_ge(k_turned, b * KC + m + 1)
                    nc.scalar.activation(k_exp[:, m, :], k_t[:, m, ds(b, 1), :].rearrange("p o s -> p (o s)"),
                                         ACT.Exp, bias=k_max[:, m, ds(b, 1)],
                                         accum_out=k_sum[:, m, ds(b, 1)]).then_inc(k_exp_ok, 1)

            def keep_q(b):
                for m in range(KC):
                    act.wait_ge(q_turned, b * KC + m + 3)
                    act.wait_ge(out_mult, b * KC + m + 1)
                    nc.scalar.copy(q_t[:, m].rearrange("p j t -> p (j t)"), ps[:, 2 + m, 0:S]).then_inc(q_t_ok, 1)

            def keep_out(b):
                for m in range(KC):
                    act.wait_ge(out_mult, b * KC + m + 3)
                    nc.scalar.copy(out[:, ds(b * NCH, NCH), 128 * m:128 * m + 128],
                                   ps[0:CHUNK, 6 + m, 0:NCH * 128].rearrange("p (j e) -> p j e", j=NCH)).then_inc(out_ok, 1)

            exp_k(0)
            keep_q(0)
            with act.Fori(0, B - 1) as b:
                exp_k(b + 1)
                keep_out(b)
                keep_q(b + 1)
            keep_out(B - 1)
            act.wait_ge(var_ready, 1)
            nc.scalar.sqrt(small[:, 1, :], small[:, 0, :]).then_inc(root_done, 1)
            with act.Fori(0, NT // 2) as i:
                for p in range(2):
                    t = i * 2 + p
                    act.wait_ge(n_turned, t + 3)
                    act.wait_ge(o_mult, t + 1)
                    for k in range(KC):
                        ins = nc.scalar.activation(x_s[:, p, k, :], ps[:, p, k * CHUNK:(k + 1) * CHUNK], ACT.Identity,
                                                   bias=cols[:, 2, k:k + 1], scale=cols[:, 1, k:k + 1])
                    ins.then_inc(n_t_ok, 1)

        @block.vector
        def _(v):
            c = Chain(v, dve)
            for s in (qv_ok, k_rows_ok, state_ok, h_ok):
                v.sem_inc(s, 2)
            v.wait_ge(loaded, 16 * 7)
            with v.Fori(0, NT // 2) as i:
                for p in range(2):
                    t = i * 2 + p
                    v.wait_ge(projected, t + 3)
                    v.tensor_tensor(qv[:, ds(t, 1), :].rearrange("p o d -> p (o d)"), ps[0:CHUNK, p, :], b_qv[:],
                                    ALU.add).then_inc(qv_ok, 1)
            v.wait_ge(qv_ok, NT + 2)
            for n in range(NQ):
                red = q_red[:, TQ * n:TQ * n + TQ, :]
                c.step(v.tensor_reduce(red, q_part(n), AX.X, ALU.max))
                c.wait()
                v.tensor_tensor(q_part(n), q_part(n), red.unsqueeze(3).broadcast_to([CHUNK, TQ, HEADS, DH]),
                                ALU.subtract).then_inc(q_sub, 1)
            v.wait_ge(k_ok, B * KC + 2)
            c.step(v.tensor_reduce(k_max[:], k_t[:], AX.X, ALU.max))
            c.wait()
            v.tensor_scalar(k_max[:], k_max[:], -1.0, None, ALU.mult).then_inc(k_max_ok, 1)
            for n in range(NQ):
                v.wait_ge(q_exp, n + 1)
                c.step(v.tensor_reduce(q_red[:, TQ * n:TQ * n + TQ, :], q_part(n), AX.X, ALU.add))
            c.wait()
            c.step(v.reciprocal(q_inv[:], q_red[:]))
            c.wait()
            def place_q(b):
                for m in range(KC):
                    v.wait_ge(q_turned, b * KC + m + 1)
                    v.tensor_tensor(q_rows[:, m].rearrange("p j (g e) -> p j g e", e=DH),
                                    heads(qv[:, ds(b * NCH, NCH), 128 * m:128 * m + 128]),
                                    q_inv[:, ds(b * NCH, NCH), 8 * m:8 * m + 8].unsqueeze(3).broadcast_to([CHUNK, NCH, 8, DH]),
                                    ALU.mult).then_inc(q_rows_ok, 1)

            def place_k(b):
                for m in range(KC):
                    v.wait_ge(k_turned, b * KC + m + 3)
                    v.wait_ge(state_mult, b * KC + m + 1)
                    v.tensor_copy(k_rows[:, m].rearrange("p j e -> p (j e)"), ps[0:CHUNK, m, 0:NCH * 128]).then_inc(k_rows_ok, 1)
                    v.wait_ge(k_exp_ok, b * KC + m + 1)
                    v.reciprocal(k_inv[:, m, ds(b, 1)], k_sum[:, m, ds(b, 1)]).then_inc(k_inv_ok, 1)

            def place_state(b):
                for m in range(KC):
                    v.wait_ge(state_mult, b * KC + m + 3)
                    v.wait_ge(out_mult, b * KC + m + 1)
                    v.wait_ge(k_inv_ok, b * KC + m + 1)
                    v.scalar_tensor_tensor(state[:, m, :], ps[:, 4 + m, 0:128], k_inv[:, m, ds(b, 1)], head_mask[:],
                                           ALU.mult, ALU.mult).then_inc(state_ok, 1)

            place_q(0)
            place_k(0)
            with v.Fori(0, B - 1) as b:
                place_q(b + 1)
                place_state(b)
                place_k(b + 1)
            place_state(B - 1)
            v.wait_ge(out_ok, B * KC + 2)
            row_stats(c, out, stats, mv)
            v.tensor_scalar(small[:, 0, :], mv[:, :, 1], LN_EPS, None, ALU.add).then_inc(var_ready, 1)
            v.wait_ge(root_done, 1)
            inverse_root(c, small[:, 0, :], small[:, 1, :], small[:, 2, :], small[:, 3, :])
            v.wait_ge(bias_added, 1)
            def rows_pair(i):
                for p in range(2):
                    t = i * 2 + p
                    v.wait_ge(n_turned, t + 1)
                    v.tensor_scalar(q_rows[:, p, 0:KC, :].rearrange("p k e -> p (k e)"),
                                    out[:, ds(t, 1), :].rearrange("p o d -> p (o d)"),
                                    mv[:, ds(t, 1), 0], small[:, 2, ds(t, 1)],
                                    ALU.subtract, ALU.mult).then_inc(n_ok, 1)

            def add_pair(i):
                for p in range(2):
                    t = i * 2 + p
                    v.wait_ge(o_mult, t + 3)
                    row = h[:, ds(t, 1), :].rearrange("p o d -> p (o d)")
                    v.tensor_tensor(row, row, ps[0:CHUNK, 2 + p, 0:D], ALU.add).then_inc(h_ok, 1)

            rows_pair(0)
            with v.Fori(0, NT // 2 - 1) as i:
                rows_pair(i + 1)
                add_pair(i)
            add_pair(NT // 2 - 1)


EXPERTS, ROUNDS, FF = 4, 4, 1024
FT = FF // 128
NG2 = 2
GT = NT // NG2
MROWS = 128
MT = (2 * GT * CHUNK + EXPERTS * (MROWS - 1)) // MROWS
SORTED = MT * MROWS
W1N, W2N = EXPERTS * KC * FF, EXPERTS * FT * D
TW = 444
NP = T // TW // 2
TC = TW // CHUNK


def wait_if(eng, sem, count):
    if not isinstance(count, int) or count >= 1:
        eng.wait_ge(sem, count)


def recursive_mixture(nc, io, h, x_sorted, y_sorted, h_dram, bias_dram, ident):
    with ExitStack() as ctx:
        def sb(name, shape, dt=F32):
            return ctx.enter_context(nc.sbuf_tensor("mo_" + name, shape, dt))

        sem = ctx.enter_context(cleared_semaphores(nc, "mo_"))
        PHASES = NG2 * ROUNDS
        BODIES = MT // 2
        GU = 3
        GB = GT // GU
        G_FIRST = 2
        CHOOSE, PLACE = G_FIRST + GB, G_FIRST + GB + 1
        HALF = FF // 2
        BN = FF + D

        w_hi, w_lo = sb("w_hi", [128, W1N + W2N], F32R), sb("w_lo", [128, W1N + W2N], F32R)
        bias = sb("bias", [2, EXPERTS, BN], F32R)
        ones_r = sb("ones_r", [2, MROWS], F32R)
        x = sb("x", [MROWS, 2, D])
        x_hi, x_lo = sb("x_hi", [128, 2, KC, MROWS], F32R), sb("x_lo", [128, 2, KC, MROWS], F32R)
        room = sb("room", [MROWS, 2 * HALF + 2 * D])
        g = room[:, 0:2 * HALF].rearrange("p (s f) -> p s f", s=2)
        y = room[:, 2 * HALF:].rearrange("p (s d) -> p s d", s=2)
        bias_raw = sb("bias_raw", [128, EXPERTS * BN // 128])
        bias_hi, bias_lo = (sb(name, [128, EXPERTS * BN // 128], F32R) for name in ("bias_hi", "bias_lo"))
        g_hi, g_lo = sb("g_hi", [128, 2, HALF], F32R), sb("g_lo", [128, 2, HALF], F32R)
        y_rows = sb("y_rows", [CHUNK, GU, 2, D])
        rows = y_rows[:, :, 1, :]
        x_f = sb("x_f", [128, GU, KC, CHUNK])
        w_g = sb("w_g", [128, KC, ROUNDS, EXPERTS])
        b_g = sb("b_g", [CHUNK, ROUNDS, EXPERTS])
        before = sb("before", [CHUNK, 2, EXPERTS, EXPERTS])
        early = sb("early", [CHUNK, CHUNK])
        ones = sb("ones", [CHUNK, CHUNK])
        numbers = sb("numbers", [CHUNK, MT])
        keep = sb("keep", [CHUNK, EXPERTS * GT])
        lg = sb("lg", [CHUNK, GT, EXPERTS])
        rank = sb("rank", [CHUNK, 4, GT, EXPERTS])
        cw = sb("cw", [CHUNK, GT, EXPERTS])
        total = sb("total", [CHUNK, GT])
        tables = sb("tables", [CHUNK, 3, EXPERTS * GT])
        ends = sb("ends", [CHUNK, 4, EXPERTS])
        ends_i = sb("ends_i", [CHUNK, EXPERTS], I32)
        place_f = sb("place_f", [CHUNK, 2, GT])
        place = sb("place", [CHUNK, NG2, 2, GT], I32)
        weight = sb("weight", [CHUNK, NG2, 2, GT])
        tile_expert = sb("tile_expert", [CHUNK, 1 + NG2 * MT], I32)
        stats = sb("stats", [CHUNK, NT, 6])
        mv = sb("mv", [CHUNK, NT, 2])
        small = sb("small", [CHUNK, 4, NT])
        cmp = y_rows[:, 0:2].rearrange("p a b d -> p a (b d)")[:, :, 0:GT * EXPERTS * EXPERTS].rearrange(
            "p a (t e f) -> p a t e f", e=EXPERTS, f=EXPERTS)
        tile_cmp = y_rows[:, 0, 0, 0:MT * EXPERTS].rearrange("p (g e) -> p g e", e=EXPERTS)
        ps = ctx.enter_context(nc.psum_tensor("mo_ps", [128, 8, 512], F32))
        HID, TURN, XT, Y, GA, GL = 0, 2, 4, 5, 6, 7

        loaded, w_loaded, h_stored, bias_loaded = sem("loaded"), [sem(f"w_loaded{n}") for n in range(4)], [sem("h_stored0"), sem("h_stored1")], sem("bias_loaded")
        ones_ok, dve, var_ready, root_done = sem("ones_ok"), sem("dve"), sem("var_ready"), sem("root_done")
        bias_split, bias_stored, kept_loaded, bias_ok, w_hi_ok, w_lo_ok = sem("bias_split"), sem("bias_stored"), [sem("kept_loaded0"), sem("kept_loaded1")], sem("bias_ok"), sem("w_hi_ok"), sem("w_lo_ok")
        half_added, row_ok, gate_turned, x_f_ok, h_ok, gate_mult = (sem("half_added"), sem("row_ok"), sem("gate_turned"),
                                                                    sem("x_f_ok"), sem("h_ok"), sem("gate_mult"))
        gate_dve, arg_ok, tanh_ok, hot_ok, counted, place_ok = (sem("gate_dve"), sem("arg_ok"), sem("tanh_ok"), sem("hot_ok"),
                                                                sem("counted"), sem("place_ok"))
        pool_step, weigh_dve, weight_ok = sem("pool_step"), sem("weigh_dve"), sem("weight_ok")
        scattered, gathered = sem("scattered"), [sem(f"gathered{j}") for j in range(GU)]
        x_loaded = [sem("x_loaded0"), sem("x_loaded1")]
        y_stored = [sem("y_stored0"), sem("y_stored1")]
        x_turned, x_hi_ok, x_lo_ok, hid_mult, gelu_ok = sem("x_turned"), sem("x_hi_ok"), sem("x_lo_ok"), sem("hid_mult"), sem("gelu_ok")
        g_turned, hi_ok, lo_ok, y_mult, y_ok = sem("g_turned"), sem("hi_ok"), sem("lo_ok"), sem("y_mult"), sem("y_ok")
        block = ctx.enter_context(nc.Block())
        w1 = [w[:, 0:W1N].rearrange("p (e k f) -> p e k f", e=EXPERTS, k=KC) for w in (w_hi, w_lo)]
        w2 = [w[:, W1N:].rearrange("p (e f d) -> p e f d", e=EXPERTS, f=FT) for w in (w_hi, w_lo)]
        WQ = (W1N + W2N) // 4

        def kept(grp):
            return w_hi[0:CHUNK, grp * GT * D:(grp + 1) * GT * D].bitcast(F32).rearrange("p (t d) -> p t d", d=D)



        def gate_slot(j):
            return ps[:, (GA, GL)[j % 2], 0:KC * CHUNK]

        LG_AT, COUNT_AT, SUM_AT = 256, 256 + EXPERTS * GT, 256 + 2 * EXPERTS * GT

        def row_of(grp, t):
            return h[:, ds(grp * GT + t, 1), :].rearrange("p o d -> p (o d)")

        def bodies(eng, body, ph, grp, rnd):
            if isinstance(ph, int) and ph == 0:
                for i in range(G_FIRST):
                    body(ph, grp, i, None)
            else:
                with eng.Fori(0, G_FIRST) as i:
                    body(ph, grp, i, None)
            with eng.Fori(0, GB) as b:
                body(ph, grp, b + G_FIRST, ("rows", b, rnd))
            body(ph, grp, CHOOSE, ("choose", None, rnd) if rnd is not None else None)
            body(ph, grp, PLACE, ("place", None, rnd) if rnd is not None else None)
            last = isinstance(ph, int) and ph == PHASES - 1
            with eng.Fori(PLACE + 1, BODIES - last) as i:
                body(ph, grp, i, None)
            if last:
                body(ph, grp, BODIES - 1, None)

        def all_phases(eng, body):
            bodies(eng, body, 0, 0, 0)
            with eng.Fori(0, ROUNDS - 1) as r:
                bodies(eng, body, r * 2 + 1, 1, r + 1)
                bodies(eng, body, r * 2 + 2, 0, r + 1)
            bodies(eng, body, PHASES - 1, 1, None)

        @block.sync
        def _(sp):
            for dst, name in ((w_g, "mo_w_g"), (b_g, "mo_b_g"), (before, "before"), (early, "early"), (numbers, "mo_numbers"),
                              (keep, "mo_keep")):
                src = io[name]
                if src.shape[0] == 1:
                    src = src.broadcast_to([CHUNK] + list(src.shape[1:]))
                sp.dma_start(dst[:], src).then_inc(loaded, 16)
            sp.dma_start(bias_raw[:], io["mo_b"]).then_inc(bias_loaded, 16)
            for grp in range(NG2):
                part = slice(grp * GT, (grp + 1) * GT)
                sp.dma_start(h_dram[:, part, :], h[:, part, :]).then_inc(h_stored[grp], 16)
            for n in range(4):
                sp.dma_start(w_lo[:, WQ * n:WQ * n + WQ].bitcast(F32), io["mo_w"][:, WQ * n:WQ * n + WQ]).then_inc(w_loaded[n], 16)
            for n, part in enumerate((bias_hi, bias_lo)):
                sp.wait_ge(bias_split, n + 1)
                sp.dma_start(bias_dram[n].rearrange("(p n) -> p n", p=128), part[:].bitcast(F32)).then_inc(bias_stored, 16)
            sp.wait_ge(bias_stored, 32)
            sp.dma_start(bias[:].bitcast(F32).rearrange("o e n -> o (e n)"), bias_dram).then_inc(bias_ok, 16)

            def tile(halves, grp, n):
                if isinstance(n, int) and not 0 <= n < MT:
                    grp, n = 1 - grp, n % MT
                return halves[grp][ds(n * MROWS, MROWS), :]

            def load(s, q, grp, n):
                sp.wait_ge(x_turned, q + 1)
                sp.dma_start(x[:, s, :], tile(x_sorted, grp, n)).then_inc(x_loaded[s], 16)

            def store(s, q, grp, n):
                sp.wait_ge(y_ok, q + 3)
                sp.dma_start(tile(y_sorted, grp, n), y[:, s, :]).then_inc(y_stored[s], 16)

            def tiles(ph, grp, i):
                for s in range(2):
                    q, n = (ph * BODIES + i) * 2 + s, i * 2 + s
                    if isinstance(i, int) and i == BODIES - 1 and s == 0 and not (isinstance(ph, int) and ph == PHASES - 1):
                        sp.wait_ge(scattered, (ph + 2) * 16 * 2 * GT)
                    if not (isinstance(q, int) and q + 2 >= PHASES * MT):
                        load(s, q + 2, grp, n + 2)
                    if not (isinstance(q, int) and q == 0):
                        store(1 - s, q - 1, grp, n - 1)

            def phase(ph, grp):
                tiles(ph, grp, 0)
                with sp.Fori(1, BODIES - 1) as i:
                    tiles(ph, grp, i)
                tiles(ph, grp, BODIES - 1)

            sp.wait_ge(scattered, 16 * 2 * GT)
            load(0, 0, 0, 0)
            load(1, 1, 0, 1)
            phase(0, 0)
            with sp.Fori(0, ROUNDS - 1) as r:
                phase(r * 2 + 1, 1)
                phase(r * 2 + 2, 0)
            phase(PHASES - 1, 1)
            store(1, PHASES * MT - 1, 1, MT - 1)
            for grp in range(NG2):
                sp.dma_start(kept(grp), h_dram[:, grp * GT:(grp + 1) * GT, :]).then_inc(kept_loaded[grp], 16)

        @block.gpsimd
        def _(gp):
            def arrived(*waits):
                for s, n in waits:
                    gp.wait_ge(s, n)
                gp.sem_inc(pool_step, 1)

            def scatter(ex, grp):
                arrived((place_ok, ex + 1), (h_ok, ex * GT + GT + GU))
                for t in range(GT):
                    for k in range(2):
                        gp.indirect_dma_start(x_sorted[grp], bass.IndirectOffsetOnAxis(ap=place[:, grp, k, t:t + 1].bitcast(U32), axis=0),
                                              h[:, grp * GT + t, :], None).then_inc(scattered, 16)

            def gather(ex, grp, to_rows=True, first_after_gates=False):
                arrived(*((stored, (ex - 1) * 16 * BODIES) for stored in y_stored))
                for t in range(GT):
                    n = ex * GT + t
                    if to_rows or (first_after_gates and t < GU):
                        arrived((gate_turned, n + 1), (h_ok, n + 1))
                    else:
                        arrived((row_ok, n - GU + 1))
                    for k in range(2):
                        gp.indirect_dma_start(y_rows[:, t % GU, k, :], None, y_sorted[grp],
                                              bass.IndirectOffsetOnAxis(ap=place[:, grp, k, t:t + 1].bitcast(U32), axis=0)
                                              ).then_inc(gathered[t % GU], 16)

            scatter(0, 0)
            scatter(1, 1)
            with gp.Fori(0, ROUNDS - 1) as r:
                gather(r * 2 + 2, 0)
                scatter(r * 2 + 2, 0)
                gather(r * 2 + 3, 1)
                scatter(r * 2 + 3, 1)
            gather(PHASES, 0, False, True)
            gather(PHASES + 1, 1, False)

        @block.tensor
        def _(pe):
            for s, n in ((x_turned, 2), (hid_mult, 4), (g_turned, 2), (y_mult, 2), (gate_turned, GU), (gate_mult, GU)):
                pe.sem_inc(s, n)
            pe.wait_ge(loaded, 16 * 6)

            def turn_rows(ex, b, js):
                for j in js:
                    t = ex * GT + b * GU + j
                    pe.wait_ge(row_ok, t + 1)
                    pe.wait_ge(x_f_ok, t + GU if j == 0 else t + GU - 1)
                    for k in range(KC):
                        mm = pe.transpose(gate_slot(j)[:, k * CHUNK:(k + 1) * CHUNK], rows[:, j, 128 * k:128 * k + 128],
                                          ident[0:CHUNK, 0:CHUNK])
                    mm.then_inc(gate_turned, 1)

            def logits(ex, b, rnd):
                for j in range(GU):
                    pe.wait_ge(x_f_ok, ex * GT + b * GU + 2 * GU)
                    for k in range(KC):
                        mm = pe.matmul(ps[0:CHUNK, GL, ds((b * GU + j) * EXPERTS + LG_AT, EXPERTS)], x_f[:, j, k, :],
                                       w_g[:, k, ds(rnd, 1), :].rearrange("p o e -> p (o e)"), start=(k == 0), stop=(k == KC - 1))
                    mm.then_inc(gate_mult, 1)

            def count(ex):
                pe.wait_ge(hot_ok, ex + 1)
                chosen = rank[:, 1].rearrange("p t e -> p (t e)")
                pe.matmul(ps[0:CHUNK, GL, COUNT_AT:COUNT_AT + EXPERTS * GT], early[:], chosen, start=True, stop=True)
                pe.matmul(ps[0:CHUNK, GL, SUM_AT:SUM_AT + EXPERTS * GT], ones[:], chosen, start=True, stop=True).then_inc(counted, 1)

            def turn_x(s, q, loads):
                pe.wait_ge(x_loaded[s], loads * 16)
                pe.wait_ge(x_lo_ok, q + 2)
                for k in range(KC):
                    mm = pe.transpose(ps[:, XT, 256 * s + MROWS * k:256 * s + MROWS * k + MROWS], x[:, s, 128 * k:128 * k + 128], ident[:])
                mm.then_inc(x_turned, 1)

            def expert(n):
                return pe.value_load(tile_expert[0:1, ds(n, 1)], min_val=0, max_val=EXPERTS - 1)

            def hidden(s, hf, q, e):
                w = q * 2 + hf
                if hf == 0:
                    pe.wait_ge(x_lo_ok, q + 3)
                pe.wait_ge(gelu_ok, w + 1)
                at = HALF * hf
                pe.matmul(ps[:, HID + hf, :], ones_r[:], bias[:, ds(e, 1), at:at + HALF].rearrange("p o f -> p (o f)"),
                          start=True, stop=False)
                for a in range(KC):
                    for part, xs in ((0, x_hi), (0, x_lo), (1, x_hi)):
                        mm = pe.matmul(ps[:, HID + hf, :], xs[:, s, a, :],
                                       w1[part][:, ds(e, 1), a, at:at + HALF].rearrange("p o f -> p (o f)"),
                                       start=False, stop=(a == KC - 1 and part == 1))
                mm.then_inc(hid_mult, 1)

            def turn_g(hf, w):
                pe.wait_ge(gelu_ok, w + 3)
                pe.wait_ge(lo_ok, w + 1)
                for f in range(FT // 2):
                    mm = pe.transpose(ps[:, TURN + hf, 128 * f:128 * f + 128], g[:, hf, 128 * f:128 * f + 128], ident[:])
                mm.then_inc(g_turned, 1)

            def down(s, hf, q, e):
                pe.wait_ge(lo_ok, q * 2 + hf + 3)
                out = ps[:, Y, 256 * s:256 * s + D]
                if hf == 0:
                    pe.wait_ge(y_ok, q + 2)
                    pe.matmul(out, ones_r[:], bias[:, ds(e, 1), FF:BN].rearrange("p o d -> p (o d)"), start=True, stop=False)
                for f in range(FT // 2):
                    for part, gs in ((0, g_hi), (0, g_lo), (1, g_hi)):
                        mm = pe.matmul(out, gs[:, hf, 128 * f:128 * f + 128],
                                       w2[part][:, ds(e, 1), f + FT // 2 * hf, :].rearrange("p o d -> p (o d)"),
                                       start=False, stop=(hf == 1 and f == FT // 2 - 1 and part == 1))
                mm.then_inc(y_mult, 1)

            def body(ph, grp, i, part):
                kind, b, rnd = part or (None, None, None)
                ex = ph + 1
                gating = kind == "rows" and not (isinstance(ph, int) and ph == PHASES - 1)
                for s in range(2):
                    q = (ph * BODIES + i) * 2 + s
                    start = isinstance(q, int) and q == 0
                    end = isinstance(q, int) and q == PHASES * MT - 1
                    n = i * 2 + s + 1 + grp * MT
                    e_prev = e if s else None
                    e = expert(n)
                    hidden(s, 0, q, e)
                    if s == 0 and not start:
                        e_prev = expert(n - 1)
                    if gating and s == 1:
                        turn_rows(ex, b, (0, 1))
                    if not end:
                        turn_x(1 - s, q + 1, ph * BODIES + i + 1 + s)
                    if not start:
                        turn_g(1, q * 2 - 1)
                        down(1 - s, 0, q - 1, e_prev)
                    hidden(s, 1, q, e)
                    if gating and s == 1:
                        turn_rows(ex, b, (2,))
                    turn_g(0, q * 2)
                    if gating and s == 1:
                        logits(ex, b, rnd)
                    if kind == "choose" and s == 1:
                        count(ex)
                    if not start:
                        down(1 - s, 1, q - 1, e_prev)

            with pe.Fori(0, GB) as b:
                turn_rows(0, b, (0, 1, 2))
                logits(0, b, 0)
            count(0)
            pe.wait_ge(bias_ok, 16)
            pe.wait_ge(w_lo_ok, 4)
            pe.wait_ge(place_ok, 1)
            turn_x(0, 0, 1)
            all_phases(pe, body)
            turn_g(1, PHASES * MT * 2 - 1)
            e = expert(NG2 * MT)
            down(1, 0, PHASES * MT - 1, e)
            down(1, 1, PHASES * MT - 1, e)

        @block.scalar
        def _(act):
            for s, n in ((gelu_ok, 2), (x_f_ok, GU), (h_ok, GU)):
                act.sem_inc(s, n)
            act.wait_ge(var_ready, 1)
            nc.scalar.sqrt(small[:, 1, :], small[:, 0, :]).then_inc(root_done, 1)

            def keep_rows(ex, grp, b, js):
                for j in js:
                    t = ex * GT + b * GU + j
                    act.wait_ge(gate_turned, t + 1 + GU)
                    act.wait_ge(gate_mult, t + 1)
                    nc.scalar.copy(x_f[:, j].rearrange("p k t -> p (k t)"), gate_slot(j)).then_inc(x_f_ok, 1)
                    nc.scalar.copy(row_of(grp, b * GU + j), rows[:, j, :]).then_inc(h_ok, 1)

            def tanh(ex):
                act.wait_ge(arg_ok, ex + 1)
                nc.scalar.activation(cw[:], cw[:], ACT.Tanh).then_inc(tanh_ok, 1)

            def part_x(s, q):
                act.wait_ge(x_turned, q + 3)
                act.wait_ge(hid_mult, q * 2 + 2)
                nc.scalar.copy(x_hi[:, s].rearrange("p k t -> p (k t)"), ps[:, XT, 256 * s:256 * s + 256]).then_inc(x_hi_ok, 1)

            def gelu(hf, w):
                act.wait_ge(hid_mult, w + 1 + 4)
                act.wait_ge(g_turned, w + 1)
                nc.scalar.activation(g[:, hf, :], ps[:, HID + hf, :], ACT.Gelu_apprx_tanh).then_inc(gelu_ok, 1)

            def part_g(hf, w):
                act.wait_ge(g_turned, w + 3)
                act.wait_ge(y_mult, w + 1)
                nc.scalar.copy(g_hi[:, hf, :], ps[:, TURN + hf, :]).then_inc(hi_ok, 1)

            def body(ph, grp, i, part):
                kind, b, rnd = part or (None, None, None)
                gating = kind == "rows" and not (isinstance(ph, int) and ph == PHASES - 1)
                for s in range(2):
                    q = (ph * BODIES + i) * 2 + s
                    gelu(0, q * 2)
                    if not (isinstance(q, int) and q == PHASES * MT - 1):
                        part_x(1 - s, q + 1)
                    if gating and s == 1:
                        keep_rows(ph + 1, 1 - grp, b, (0, 1))
                    if not (isinstance(q, int) and q == 0):
                        part_g(1, q * 2 - 1)
                    gelu(1, q * 2 + 1)
                    if gating and s == 1:
                        keep_rows(ph + 1, 1 - grp, b, (2,))
                    part_g(0, q * 2)
                    if kind == "choose" and s == 1:
                        tanh(ph + 1)

            act.wait_ge(h_stored[0], 16)
            act.wait_ge(h_stored[1], 16)
            with act.Fori(0, GB) as b:
                keep_rows(0, 0, b, (0, 1, 2))
            tanh(0)
            for n in range(4):
                act.wait_ge(w_loaded[n], 16)
                nc.scalar.copy(w_hi[:, WQ * n:WQ * n + WQ], w_lo[:, WQ * n:WQ * n + WQ].bitcast(F32)).then_inc(w_hi_ok, 1)
            part_x(0, 0)
            all_phases(act, body)
            part_g(1, PHASES * MT * 2 - 1)

        @block.vector
        def _(v):
            for s, n in ((x_lo_ok, 2), (lo_ok, 2), (y_ok, 2)):
                v.sem_inc(s, n)
            v.memset(ones[:], 1.0).then_inc(ones_ok, 1)
            c = Chain(v, dve)
            row_stats(c, h, stats, mv)
            v.tensor_scalar(small[:, 0, :], mv[:, :, 1], LN_EPS, None, ALU.add).then_inc(var_ready, 1)
            v.wait_ge(ones_ok, 1)
            v.tensor_copy(ones_r[:], ones[0:2, 0:1].broadcast_to([2, MROWS])).then_inc(ones_ok, 1)
            v.wait_ge(root_done, 1)
            inverse_root(c, small[:, 0, :], small[:, 1, :], small[:, 2, :], small[:, 3, :])
            v.wait_ge(loaded, 16 * 6)

            def normal_rows(ex, grp, b):
                for j in range(GU):
                    t = b * GU + j
                    v.wait_ge(gate_turned, ex * GT + t + 1)
                    v.wait_ge(h_ok, ex * GT + t + 1)
                    v.tensor_scalar(rows[:, j, :], row_of(grp, t), mv[:, ds(grp * GT + t, 1), 0], small[:, 2, ds(grp * GT + t, 1)],
                                    ALU.subtract, ALU.mult).then_inc(row_ok, 1)

            def add_first(ex, grp, b):
                for j in range(GU):
                    v.wait_ge(gathered[j], ((ex - 2) * GB + b + 1) * 32)
                    v.scalar_tensor_tensor(y_rows[:, j, 0, :], y_rows[:, j, 0, :], weight[:, grp, 0, ds(b * GU + j, 1)],
                                           row_of(grp, b * GU + j), ALU.mult, ALU.add).then_inc(half_added, 1)

            def add_second(ex, grp, b, to_rows):
                for j in range(GU):
                    v.wait_ge(half_added, (ex - 2) * GT + b * GU + j + 1)
                    v.scalar_tensor_tensor(rows[:, j, :] if to_rows else row_of(grp, b * GU + j), y_rows[:, j, 1, :],
                                           weight[:, grp, 1, ds(b * GU + j, 1)], y_rows[:, j, 0, :],
                                           ALU.mult, ALU.add).then_inc(row_ok, 1)

            CHOOSE_STEPS, PLACE_STEPS = 12, 20
            STEPS = CHOOSE_STEPS + PLACE_STEPS
            by_e = [CHUNK, GT, EXPERTS]

            def choose(ex, rnd):
                c = Chain(v, gate_dve, ex * STEPS)
                by_pair = [CHUNK, GT, EXPERTS, EXPERTS]
                v.wait_ge(gate_mult, ex * GT + GT + GU)
                v.wait_ge(h_ok, ex * GT + GT + GU)
                c.step(v.tensor_tensor(lg[:], ps[0:CHUNK, GL, LG_AT:LG_AT + GT * EXPERTS].rearrange("p (t e) -> p t e", e=EXPERTS),
                                       b_g[:, ds(rnd, 1), :].broadcast_to(by_e), ALU.add))
                c.wait()
                other = lg[:].unsqueeze(2).broadcast_to(by_pair)
                own = lg[:].unsqueeze(3).broadcast_to(by_pair)
                c.step(v.tensor_tensor(cmp[:, 0], other, own, ALU.is_ge))
                c.step(v.tensor_tensor(cmp[:, 1], other, own, ALU.is_gt))
                c.wait()
                yield
                for a in range(2):
                    c.step(v.tensor_tensor(cmp[:, a], cmp[:, a], before[:, a:a + 1].broadcast_to(by_pair), ALU.mult))
                c.wait()
                c.step(v.tensor_tensor(cmp[:, 0], cmp[:, 0], cmp[:, 1], ALU.add))
                c.wait()
                c.step(v.tensor_reduce(rank[:, 0], cmp[:, 0], AX.X, ALU.add))
                c.wait()
                v.tensor_scalar(rank[:, 1], rank[:, 0], 2.0, None, ALU.is_lt).then_inc(hot_ok, 1)
                yield
                c.step(v.tensor_scalar(rank[:, 2], rank[:, 0], 0.0, None, ALU.is_equal))
                c.step(v.tensor_scalar(rank[:, 3], rank[:, 0], 1.0, None, ALU.is_equal))
                v.wait_ge(hot_ok, ex + 1)
                c.wait()
                c.step(v.tensor_tensor(rank[:, 0], rank[:, 1], lg[:], ALU.mult))
                c.wait()
                c.step(v.tensor_reduce(total[:], rank[:, 0], AX.X, ALU.add))
                c.wait()
                v.scalar_tensor_tensor(cw[:], total[:].unsqueeze(2).broadcast_to(by_e), -0.5, lg[:],
                                       ALU.mult, ALU.add).then_inc(arg_ok, 1)
                c.step(v.memset(ends[:, 3, :], 1.0))
                assert c.n == CHOOSE_STEPS, c.n
                yield

            def set_places(ex, grp):
                c = Chain(v, gate_dve, ex * STEPS + CHOOSE_STEPS)
                v.wait_ge(counted, ex + 1)
                so_far, whole, running = tables[:, 0, :], tables[:, 1, :], tables[:, 2, :]

                def e_first(ap):
                    return ap.rearrange("p (e t) -> p e t", e=EXPERTS)

                for dst, at in ((so_far, COUNT_AT), (whole, SUM_AT)):
                    c.step(v.tensor_copy(e_first(dst), ps[0:CHUNK, GL, at:at + GT * EXPERTS].rearrange("p (t e) -> p e t", e=EXPERTS)))
                c.wait()
                c.step(v.tensor_tensor_scan(running, keep[:], whole, 0.0, ALU.mult, ALU.add))
                c.step(v.tensor_tensor(so_far, so_far, whole, ALU.subtract))
                c.wait()
                count = e_first(running)[:, :, GT - 1]
                yield
                tiles, end, first = ends[:, 0, :], ends[:, 1, :], ends[:, 2, :]
                c.step(v.tensor_scalar(ends_i[:], count, MROWS - 1, None, ALU.add))
                c.step(v.tensor_tensor(so_far, so_far, running, ALU.add))
                c.wait()
                c.step(v.tensor_scalar(ends_i[:], ends_i[:], MROWS.bit_length() - 1, None, ALU.arith_shift_right))
                c.wait()
                c.step(v.tensor_copy(tiles, ends_i[:]))
                c.wait()
                c.step(v.tensor_tensor_scan(end, ends[:, 3, :], tiles, 0.0, ALU.mult, ALU.add))
                c.wait()
                c.step(v.tensor_tensor(first, end, tiles, ALU.subtract))
                c.step(v.tensor_tensor(tile_cmp, numbers[:].unsqueeze(2).broadcast_to([CHUNK, MT, EXPERTS]),
                                       end.unsqueeze(1).broadcast_to([CHUNK, MT, EXPERTS]), ALU.is_ge))
                c.wait()
                yield
                c.step(v.tensor_scalar(first, first, float(MROWS), None, ALU.mult))
                c.step(v.tensor_reduce(running[:, 0:MT], tile_cmp, AX.X, ALU.add))
                c.wait()
                c.step(v.tensor_tensor(e_first(so_far), e_first(so_far), first.unsqueeze(2).broadcast_to([CHUNK, EXPERTS, GT]), ALU.add))
                to = tile_expert[:, 1 + grp * MT:1 + grp * MT + MT]
                c.step(v.tensor_scalar(to, running[:, 0:MT], float(EXPERTS - 1), None, ALU.min))
                c.wait()
                for k in range(2):
                    c.step(v.tensor_tensor((rank[:, 0], lg[:])[k], so_far.rearrange("p (e t) -> p t e", e=EXPERTS), rank[:, 2 + k], ALU.mult))
                c.wait()
                for k in range(2):
                    c.step(v.tensor_reduce(place_f[:, k, :], (rank[:, 0], lg[:])[k], AX.X, ALU.add))
                c.step(v.tensor_copy(tile_expert[:, 0:1], tile_expert[:, NG2 * MT:NG2 * MT + 1]) if grp else
                       v.memset(ends[:, 3, :], 1.0))
                assert c.n == PLACE_STEPS, c.n
                c.wait()
                v.tensor_copy(place[:, grp], place_f[:]).then_inc(place_ok, 1)
                yield

            WEIGH_STEPS = 3

            def weigh(ex, grp):
                c = Chain(v, weigh_dve, ex * WEIGH_STEPS)
                v.wait_ge(tanh_ok, ex + 1)
                c.step(v.tensor_scalar(cw[:], cw[:], 1.0, 0.5, ALU.add, ALU.mult))
                v.wait_ge(place_ok, ex + 1)
                c.wait()
                for k in range(2):
                    c.step(v.tensor_tensor((rank[:, 0], lg[:])[k], rank[:, 2 + k], cw[:], ALU.mult))
                c.wait()
                for k in range(2):
                    v.tensor_reduce(weight[:, grp, k, :], (rank[:, 0], lg[:])[k], AX.X, ALU.add).then_inc(weight_ok, 1)
                assert c.n == WEIGH_STEPS

            def rest_x(s, q):
                v.wait_ge(x_hi_ok, q + 1)
                v.tensor_tensor(x_lo[:, s].rearrange("p k t -> p (k t)"), ps[:, XT, 256 * s:256 * s + 256],
                                x_hi[:, s].rearrange("p k t -> p (k t)").bitcast(F32), ALU.subtract).then_inc(x_lo_ok, 1)

            def rest_g(hf, w):
                v.wait_ge(hi_ok, w + 1)
                v.tensor_tensor(g_lo[:, hf, :], ps[:, TURN + hf, :], g_hi[:, hf, :].bitcast(F32), ALU.subtract).then_inc(lo_ok, 1)

            def keep_y(s, q, stores):
                v.wait_ge(y_mult, q * 2 + 4)
                wait_if(v, y_stored[s], stores * 16)
                v.tensor_copy(y[:, s, :], ps[:, Y, 256 * s:256 * s + D]).then_inc(y_ok, 1)

            def body(ph, grp, i, part):
                kind, b, rnd = part or (None, None, None)
                ex, other = ph + 1, 1 - grp
                to_rows = not (isinstance(ph, int) and ph == PHASES - 1)
                fresh = isinstance(ph, int) and ph == 0
                parts = iter(())
                if kind == "choose":
                    parts = choose(ex, rnd)
                if kind == "place":
                    parts = set_places(ex, other)
                for s in range(2):
                    q = (ph * BODIES + i) * 2 + s
                    start = isinstance(q, int) and q == 0
                    if not (isinstance(q, int) and q == PHASES * MT - 1):
                        rest_x(1 - s, q + 1)
                    if not start:
                        rest_g(1, q * 2 - 1)
                    if kind == "rows" and s == 0:
                        if fresh:
                            normal_rows(ex, other, b)
                        else:
                            add_first(ex, other, b)
                    next(parts, None)
                    rest_g(0, q * 2)
                    if kind == "rows" and s == 0 and not fresh:
                        add_second(ex, other, b, to_rows)
                    if s == 0:
                        next(parts, None)
                    if kind == "place" and s == 1:
                        weigh(ex, other)
                    if not start:
                        keep_y(1 - s, q - 1, ph * BODIES + i - 1 + s)

            with v.Fori(0, GB) as b:
                normal_rows(0, 0, b)
            v.wait_ge(bias_loaded, 16)
            v.tensor_copy(bias_hi[:], bias_raw[:]).then_inc(bias_split, 1)
            v.wait_ge(bias_split, 1)
            v.tensor_tensor(bias_lo[:], bias_raw[:], bias_hi[:].bitcast(F32), ALU.subtract).then_inc(bias_split, 1)
            for part in (choose(0, 0), set_places(0, 0)):
                for _ in part:
                    pass
            weigh(0, 0)
            for n in range(4):
                at = slice(WQ * n, WQ * n + WQ)
                v.wait_ge(w_hi_ok, n + 1)
                v.tensor_tensor(w_lo[:, at], w_lo[:, at].bitcast(F32), w_hi[:, at].bitcast(F32), ALU.subtract).then_inc(w_lo_ok, 1)
            rest_x(0, 0)
            all_phases(v, body)
            rest_g(1, PHASES * MT * 2 - 1)
            keep_y(1, PHASES * MT - 1, PHASES * BODIES - 1)
            part = h[:, 0:GT, :]
            v.wait_ge(row_ok, (PHASES + 1) * GT)
            v.wait_ge(kept_loaded[0], 16)
            v.tensor_tensor(part, part, kept(0), ALU.add)
            with v.Fori(0, GB) as b:
                add_first(PHASES + 1, 1, b)
                add_second(PHASES + 1, 1, b, False)
            part = h[:, GT:NT, :]
            v.wait_ge(row_ok, (PHASES + 2) * GT)
            v.wait_ge(kept_loaded[1], 16)
            v.tensor_tensor(part, part, kept(1), ALU.add)


def retention(nc, io, h, x_t, ident):
    with ExitStack() as ctx:
        def sb(name, shape, dt=F32):
            return ctx.enter_context(nc.sbuf_tensor("re_" + name, shape, dt))

        def sem(name):
            return ctx.enter_context(nc.semaphore("re_" + name))

        U = 2 * NCH
        GH = 4
        NG = HEADS // GH
        vg = sb("vg", [CHUNK, NT, 2 * D])
        out = sb("out", [CHUNK, NT, D])
        w = sb("w", [128, KC, 4 * D])
        w_o = sb("w_o", [128, KC, D])
        bias = sb("bias", [CHUNK, 4 * D])
        b_qk = sb("b_qk", [CHUNK, NCH, 2 * D])
        rows3 = sb("rows3", [CHUNK, 3, D])
        decay = sb("decay", [CHUNK, NCH, 2])
        causal = sb("causal", [CHUNK, CHUNK])
        head_mask = sb("head_mask", [128, 128])
        head_of = sb("head_of", [128, 8])
        x_s = sb("x_s", [128, 2, KC, CHUNK])
        qk = sb("qk", [CHUNK, NCH, 2 * D])
        qk_t = sb("qk_t", [128, 2, 2 * KC, CHUNK])
        q_h = sb("q_h", [128, 2, HEADS, CHUNK])
        sc = sb("sc", [CHUNK, HEADS, CHUNK])
        state = sb("state", [128, KC, 128])
        stats = sb("stats", [CHUNK, NT, 6])
        mv = sb("mv", [CHUNK, NT, 2])
        small = sb("small", [CHUNK, 4, NT])
        rows = sb("rows", [CHUNK, 2, D])
        ps = ctx.enter_context(nc.psum_tensor("re_ps", [128, 8, 512], F32))
        QK, VG, TURN, SC, OUT, ST = 0, 1, 2, 3, 5, 7
        loaded, dve, x_copied, projected = sem("loaded"), sem("dve"), sem("x_copied"), sem("projected")
        qkvg_ok, turned, qk_t_ok, q_h_ok = sem("qkvg_ok"), sem("turned"), sem("qk_t_ok"), sem("q_h_ok")
        sc_mult, sc_ok, st_ok, out_mult, out_ok = sem("sc_mult"), sem("sc_ok"), sem("st_ok"), sem("out_mult"), sem("out_ok")
        gate_ok, gates_ready, var_ready, root_done = sem("gate_ok"), sem("gates_ready"), sem("var_ready"), sem("root_done")
        pool_step, stats_ok, n_ok, r_ok, n_turned, n_t_ok, o_mult, h_ok = sem("pool_step"), sem("stats_ok"), sem("n_ok"), sem("r_ok"), sem("n_turned"), sem("n_t_ok"), sem("o_mult"), sem("h_ok")
        block = ctx.enter_context(nc.Block())

        @block.sync
        def _(sp):
            sp.dma_start(w[:], io["re_w"]).then_inc(loaded, 16)
            sp.dma_start(w_o[:], io["re_w_o"]).then_inc(loaded, 16)
            sp.dma_start(bias[:], io["re_bias"].broadcast_to([CHUNK, 4 * D])).then_inc(loaded, 16)
            sp.dma_start(rows3[:], io["re_rows3"].broadcast_to([CHUNK, 3, D])).then_inc(loaded, 16)
            sp.dma_start(decay[:], io["decay"]).then_inc(loaded, 16)
            sp.dma_start(causal[:], io["causal"]).then_inc(loaded, 16)
            sp.dma_start(head_mask[:], io["head_mask"]).then_inc(loaded, 16)
            sp.dma_start(head_of[:], io["head_of"]).then_inc(loaded, 16)

        LOADED = 16 * 8

        def one(ap, t):
            return ap[:, ds(t, 1), :].rearrange("p o d -> p (o d)")

        def states_before(t, u):
            done = u - u // NCH - 1
            return (t - u) // NCH * (NCH - 1) + done if isinstance(t, int) else (t - u) // U * (2 * NCH - 2) + done

        def is_at(t, n):
            return isinstance(t, int) and t == n

        def all_tiles(eng, body):
            for u in range(U):
                body(0, u)
            with eng.Fori(1, NT // U - 1) as i:
                for u in range(U):
                    body(i, u)
            for u in range(U):
                body(NT // U - 1, u)

        @block.gpsimd
        def _(g):
            g.wait_ge(loaded, LOADED)

            def take_x(t, u):
                g.wait_ge(projected, t + 1)
                g.tensor_copy(x_s[:, u % 2], x_t[:, :, ds(t * CHUNK, CHUNK)]).then_inc(x_copied, 1)

            def gates(t):
                g.wait_ge(gates_ready, t + 1)
                g.wait_ge(out_mult, t + 3)
                g.sem_inc(pool_step, 1)
                v_at, g_at, row = one(vg, t)[:, 0:D], one(vg, t)[:, D:2 * D], one(h, t)
                g.tensor_tensor(v_at, g_at, rows3[:, 2, :], ALU.mult).then_inc(gate_ok, 1)
                g.tensor_tensor(row, row, rows3[:, 0, :], ALU.add).then_inc(gate_ok, 1)
                g.wait_ge(gate_ok, t * 3 + 1)
                g.sem_inc(pool_step, 1)
                g.tensor_tensor(g_at, g_at, rows3[:, 1, :], ALU.mult).then_inc(gate_ok, 1)

            def body(i, u):
                t, p = i * U + u, u % 2
                if not is_at(t, NT - 1):
                    take_x(t + 1, u + 1)
                g.wait_ge(qk_t_ok, t + 2)
                g.wait_ge(sc_mult, t * NG + NG)
                for m in range(KC):
                    ins = g.tensor_tensor(q_h[:, p, 8 * m:8 * m + 8, :],
                                          qk_t[:, p, m:m + 1, :].broadcast_to([128, 8, CHUNK]),
                                          head_of[:].unsqueeze(2).broadcast_to([128, 8, CHUNK]), ALU.mult)
                ins.then_inc(q_h_ok, 1)
                if not is_at(t, 0) and not is_at(t, 1):
                    gates(t - 2)

            take_x(0, 0)
            all_tiles(g, body)
            gates(NT - 2)
            gates(NT - 1)

        @block.tensor
        def _(pe):
            for s, n in ((projected, 2), (sc_mult, 2 * NG), (out_mult, 2), (n_turned, 2), (o_mult, 2)):
                pe.sem_inc(s, n)
            pe.wait_ge(loaded, LOADED)

            def project(t, u):
                pe.wait_ge(x_copied, t + 1)
                pe.wait_ge(qkvg_ok, t + 1)
                for bank in (QK, VG):
                    for k in range(KC):
                        mm = pe.matmul(ps[0:CHUNK, bank, :], x_s[:, u % 2, k, :], w[:, k, 512 * bank:512 * bank + 512],
                                       start=(k == 0), stop=(k == KC - 1))
                mm.then_inc(projected, 1)

            def turn(t, u):
                pe.wait_ge(qkvg_ok, t + 2)
                pe.wait_ge(qk_t_ok, t + 1)
                for k in range(2 * KC):
                    mm = pe.transpose(ps[:, TURN, k * CHUNK:(k + 1) * CHUNK], qk[:, u % NCH, 128 * k:128 * k + 128],
                                      ident[0:CHUNK, 0:CHUNK])
                mm.then_inc(turned, 1)

            def scores(t, u):
                pe.wait_ge(q_h_ok, t + 1)
                for n in range(NG):
                    pe.wait_ge(sc_ok, t * NG + n + 1)
                    pe.matmul(ps[0:CHUNK, SC + n % 2, 0:GH * CHUNK], qk_t[:, u % 2, KC + n // 2, :],
                              q_h[:, u % 2, GH * n:GH * n + GH, :], start=True, stop=True).then_inc(sc_mult, 1)

            def outputs(t, u):
                j = u % NCH
                pe.wait_ge(sc_ok, t * NG + NG + 2)
                pe.wait_ge(out_ok, t + 1)
                if j > 0:
                    pe.wait_ge(st_ok, states_before(t, u) + 1)
                    for m in range(KC):
                        pe.matmul(ps[0:CHUNK, OUT + u % 2, 128 * m:128 * m + 128], qk_t[:, u % 2, m, :], state[:, m, :],
                                  start=(m == 0), stop=False, skip_group_check=True)
                for e in range(HEADS):
                    mm = pe.matmul(ps[0:CHUNK, OUT + u % 2, DH * e:DH * e + DH], sc[:, e, :],
                                   vg[:, ds(t, 1), DH * e:DH * e + DH].rearrange("p o d -> p (o d)"),
                                   start=(j == 0 and e == 0), stop=True, skip_group_check=True)
                if j < NCH - 1:
                    for m in range(KC):
                        mm = pe.matmul(ps[:, ST, 128 * m:128 * m + 128], qk[:, u % NCH, D + 128 * m:D + 128 * m + 128],
                                       vg[:, ds(t, 1), 128 * m:128 * m + 128].rearrange("p o d -> p (o d)"),
                                       start=(j == 0 and m == 0), stop=True, skip_group_check=True)
                mm.then_inc(out_mult, 1)

            def body(i, u):
                t = i * U + u
                turn(t, u)
                if not is_at(t, 0):
                    scores(t - 1, u - 1)
                if not is_at(t, NT - 1):
                    project(t + 1, u + 1)
                if not is_at(t, 0):
                    outputs(t - 1, (u - 1) % U)

            project(0, 0)
            all_tiles(pe, body)
            scores(NT - 1, U - 1)
            outputs(NT - 1, U - 1)
            pe.wait_ge(out_ok, NT + 2)
            def turn_pair(i):
                for p in range(2):
                    t = i * 2 + p
                    pe.wait_ge(n_ok, t + 1)
                    pe.wait_ge(n_t_ok, t + 1)
                    for k in range(KC):
                        mm = pe.transpose(ps[:, p, k * CHUNK:(k + 1) * CHUNK], rows[:, p, 128 * k:128 * k + 128],
                                          ident[0:CHUNK, 0:CHUNK])
                    mm.then_inc(n_turned, 1)

            def project_pair(i):
                for p in range(2):
                    t = i * 2 + p
                    pe.wait_ge(n_t_ok, t + 3)
                    pe.wait_ge(h_ok, t + 1)
                    for k in range(KC):
                        mm = pe.matmul(ps[0:CHUNK, 2 + p, 0:D], x_s[:, p, k, :], w_o[:, k, :],
                                       start=(k == 0), stop=(k == KC - 1))
                    mm.then_inc(o_mult, 1)

            turn_pair(0)
            with pe.Fori(0, NT // 2 - 1) as i:
                project_pair(i)
                turn_pair(i + 1)
            project_pair(NT // 2 - 1)

        @block.scalar
        def _(act):
            for s, n in ((qk_t_ok, 1), (out_ok, 2), (n_t_ok, 2)):
                act.sem_inc(s, n)
            def out_rows(t, u):
                act.wait_ge(out_mult, t + 3)
                nc.scalar.copy(one(out, t), ps[0:CHUNK, OUT + u % 2, 0:D]).then_inc(out_ok, 1)
                gate = one(vg, t)[:, D:2 * D]
                nc.scalar.activation(gate, gate, ACT.Sigmoid).then_inc(gates_ready, 1)

            def body(i, u):
                t = i * U + u
                act.wait_ge(turned, t + 1)
                act.wait_ge(out_mult, t + 1)
                nc.scalar.copy(qk_t[:, u % 2].rearrange("p k t -> p (k t)"), ps[:, TURN, 0:2 * KC * CHUNK]).then_inc(qk_t_ok, 1)
                if not is_at(t, 0):
                    out_rows(t - 1, u - 1)

            all_tiles(act, body)
            out_rows(NT - 1, NT - 1)
            act.wait_ge(var_ready, 1)
            nc.scalar.sqrt(small[:, 1, :], small[:, 0, :]).then_inc(root_done, 1)
            with act.Fori(0, NT // 2) as i:
                for p in range(2):
                    t = i * 2 + p
                    act.wait_ge(n_turned, t + 3)
                    act.wait_ge(o_mult, t + 1)
                    nc.scalar.copy(x_s[:, p].rearrange("p k t -> p (k t)"), ps[:, p, 0:KC * CHUNK]).then_inc(n_t_ok, 1)

        @block.vector
        def _(v):
            for s, n in ((qkvg_ok, 1), (sc_ok, 2), (h_ok, 2)):
                v.sem_inc(s, n)
            c = Chain(v, dve)
            v.wait_ge(loaded, LOADED)
            for j in range(NCH):
                for a in range(2):
                    c.step(v.tensor_scalar(b_qk[:, j, a * D:a * D + D], bias[:, a * D:a * D + D], decay[:, j, a:a + 1],
                                           None, ALU.mult))
            c.wait()
            def take_projected(t, u):
                j = u % NCH
                v.wait_ge(projected, t + 3)
                for a in range(2):
                    v.scalar_tensor_tensor(qk[:, j, a * D:a * D + D], ps[0:CHUNK, QK, a * D:a * D + D],
                                           decay[:, j, a:a + 1], b_qk[:, j, a * D:a * D + D], ALU.mult, ALU.add)
                v.tensor_tensor(one(vg, t), ps[0:CHUNK, VG, :], bias[:, 2 * D:4 * D], ALU.add).then_inc(qkvg_ok, 1)

            def mask_scores(t, u):
                v.wait_ge(out_mult, t + 2)
                if u % NCH > 0:
                    v.tensor_tensor(state[:], ps[:, ST, 0:D].rearrange("p (m e) -> p m e", m=KC),
                                    head_mask[:].unsqueeze(1).broadcast_to([128, KC, 128]), ALU.mult).then_inc(st_ok, 1)
                for n in range(NG):
                    v.wait_ge(sc_mult, t * NG + n + 1 + 2 * NG)
                    v.tensor_tensor(sc[:, GH * n:GH * n + GH, :],
                                    ps[0:CHUNK, SC + n % 2, 0:GH * CHUNK].rearrange("p (g i) -> p g i", g=GH),
                                    causal[:].unsqueeze(1).broadcast_to([CHUNK, GH, CHUNK]), ALU.mult).then_inc(sc_ok, 1)

            def out_stats(t):
                v.wait_ge(out_ok, t + 3)
                v.bn_stats(one(stats, t), one(out, t)).then_inc(stats_ok, 1)

            def body(i, u):
                t = i * U + u
                if not is_at(t, 0):
                    mask_scores(t - 1, (u - 1) % U)
                if not is_at(t, NT - 1):
                    take_projected(t + 1, u + 1)
                if not is_at(t, 0) and not is_at(t, 1):
                    out_stats(t - 2)

            take_projected(0, 0)
            all_tiles(v, body)
            mask_scores(NT - 1, U - 1)
            out_stats(NT - 2)
            out_stats(NT - 1)
            v.wait_ge(stats_ok, NT)
            moments(c, stats, mv)
            v.tensor_scalar(small[:, 0, :], mv[:, :, 1], LN_EPS, None, ALU.add).then_inc(var_ready, 1)
            v.wait_ge(root_done, 1)
            inverse_root(c, small[:, 0, :], small[:, 1, :], small[:, 2, :], small[:, 3, :])
            v.wait_ge(gate_ok, 3 * NT)
            def rows_pair(i):
                for p in range(2):
                    t = i * 2 + p
                    v.wait_ge(n_turned, t + 1)
                    v.tensor_scalar(rows[:, p, :], one(out, t), mv[:, ds(t, 1), 0], small[:, 2, ds(t, 1)],
                                    ALU.subtract, ALU.mult).then_inc(r_ok, 1)
                for p in range(2):
                    v.wait_ge(r_ok, i * 4 + p + 1)
                    v.tensor_tensor(rows[:, p, :], rows[:, p, :], one(vg, i * 2 + p)[:, D:2 * D], ALU.mult).then_inc(r_ok, 1)
                for p in range(2):
                    v.wait_ge(r_ok, i * 4 + p + 3)
                    v.tensor_tensor(rows[:, p, :], rows[:, p, :], one(vg, i * 2 + p)[:, 0:D], ALU.add).then_inc(n_ok, 1)

            def add_pair(i):
                for p in range(2):
                    t = i * 2 + p
                    v.wait_ge(o_mult, t + 3)
                    row = h[:, ds(t, 1), :].rearrange("p o d -> p (o d)")
                    v.tensor_tensor(row, row, ps[0:CHUNK, 2 + p, 0:D], ALU.add).then_inc(h_ok, 1)

            rows_pair(0)
            with v.Fori(0, NT // 2 - 1) as i:
                rows_pair(i + 1)
                add_pair(i)
            add_pair(NT // 2 - 1)


NEXP, EF, SF = 16, 256, 1024
ST = SF // 128
ROWS = 128
G_TILES = (T + NEXP * (ROWS - 1)) // ROWS
SHW = ST * (2 * KC * 128 + D)


def route_and_share(nc, io, h, x_sorted, place, tile_expert, w_gu, ident):
    with ExitStack() as ctx:
        def sb(name, shape, dt=F32):
            return ctx.enter_context(nc.sbuf_tensor("sh_" + name, shape, dt))

        def sem(name):
            return ctx.enter_context(nc.semaphore("sh_" + name))

        w_hi, w_lo = sb("w_hi", [128, SHW], F32R), sb("w_lo", [128, SHW], F32R)
        stats = sb("stats", [CHUNK, NT, 6])
        mv = sb("mv", [CHUNK, NT, 2])
        small = sb("small", [CHUNK, 6, NT])
        x_rows = sb("x_rows", [CHUNK, NT, D])
        x_f = sb("x_f", [128, KC, TW])
        x_hi, x_lo = sb("x_hi", [128, 2, KC, TW], F32R), sb("x_lo", [128, 2, KC, TW], F32R)
        router = sb("router", [128, KC, NEXP])
        lg = sb("lg", [CHUNK, NT, NEXP])
        hot = sb("hot", [CHUNK, NT, NEXP])
        early = sb("early", [CHUNK, CHUNK])
        ones = sb("ones", [CHUNK, CHUNK])
        numbers = sb("numbers", [CHUNK, NEXP + G_TILES])
        keep = sb("keep", [CHUNK, NEXP * NT])
        ends = sb("ends", [CHUNK, 4, NEXP])
        ends_i = sb("ends_i", [CHUNK, NEXP], I32)
        big = sb("big", [128, 6 * TW])
        g = big[:, 0:2 * TW].rearrange("p (s t) -> p s t", s=2)
        pr = big[:, 2 * TW:4 * TW].rearrange("p (s t) -> p s t", s=2)
        g_hi, g_lo = sb("g_hi", [128, 2, TW], F32R), sb("g_lo", [128, 2, TW], F32R)
        rows = sb("rows", [CHUNK, 2, D])
        y_f = big[:, 4 * TW:6 * TW].rearrange("p (m t) -> p m t", m=KC)
        stage = big[:, 0:2 * 1024].rearrange("p (s n) -> p s n", s=2)
        ps = ctx.enter_context(nc.psum_tensor("sh_ps", [128, 8, 512], F32))
        GATE, UP, Y, XT = 0, 2, 4, 6
        loaded, gu_loaded, lo_ok_w, hi_ok_w = (sem("loaded"), sem("gu_loaded"),
                                                                sem("lo_ok_w"), sem("hi_ok_w"))
        staged = [sem("staged0"), sem("staged1")]
        dve, var_ready, root_done, rows_ok, r_turned, r_t_ok = (sem("dve"), sem("var_ready"), sem("root_done"), sem("rows_ok"),
                                                                sem("r_turned"), sem("r_t_ok"))
        lg_mult, lg_ok, hot_ok, counted, score_arg, score_ok = (sem("lg_mult"), sem("lg_ok"), sem("hot_ok"), sem("counted"),
                                                                sem("score_arg"), sem("score_ok"))
        scale_ok, x_rows_ok, scattered = sem("scale_ok"), sem("x_rows_ok"), sem("scattered")
        rows2_ok, turned, x_f_ok, x_hi_ok, x_lo_ok = sem("rows2_ok"), sem("turned"), sem("x_f_ok"), sem("x_hi_ok"), sem("x_lo_ok")
        hid_mult, silu_ok, prod_ok, hi_ok, lo_ok = sem("hid_mult"), sem("silu_ok"), sem("prod_ok"), sem("hi_ok"), sem("lo_ok")
        y_mult, y_f_ok, back_turned, h_ok = sem("y_mult"), sem("y_f_ok"), sem("back_turned"), sem("h_ok")
        block = ctx.enter_context(nc.Block())
        NPIECE = SHW // 1024
        Y_FREE = ST + 1
        w1 = [w[:, 0:ST * 2 * KC * 128].rearrange("p (f u k c) -> p f u k c", f=ST, u=2, k=KC) for w in (w_hi, w_lo)]
        w2 = [w[:, ST * 2 * KC * 128:].rearrange("p (f d) -> p f d", f=ST) for w in (w_hi, w_lo)]

        @block.sync
        def _(sp):
            for dst, name in ((router, "router"), (early, "early"), (keep, "keep"), (numbers, "numbers")):
                src = io[name]
                sp.dma_start(dst[:], src if src.shape[0] > 1 else src.broadcast_to([CHUNK, src.shape[1]])).then_inc(loaded, 16)
            with sp.Fori(0, NPIECE // 2) as i:
                for p in range(2):
                    sp.wait_ge(lo_ok_w, i * 2 + p + 1)
                    sp.dma_start(stage[:, p, :], io["sh_w"][:, ds((i * 2 + p) * 1024, 1024)]).then_inc(staged[p], 16)
            sp.dma_start(w_gu[:], io["ex_gu"]).then_inc(gu_loaded, 16)
            sp.wait_ge(gu_loaded, 16)

        @block.gpsimd
        def _(gp):
            gp.wait_ge(scale_ok, 2)
            for t in range(NT):
                gp.wait_ge(x_rows_ok, t + 1)
                gp.indirect_dma_start(x_sorted, bass.IndirectOffsetOnAxis(ap=place[:, t:t + 1].bitcast(U32), axis=0),
                                      x_rows[:, t, :], None).then_inc(scattered, 16)
            gp.wait_ge(scattered, 16 * NT)

        @block.tensor
        def _(pe):
            for s, n in ((r_turned, 2), (lg_mult, 2), (turned, 2), (y_mult, Y_FREE), (back_turned, 1)):
                pe.sem_inc(s, n)
            pe.wait_ge(loaded, 16 * 4)
            with pe.Fori(0, NT // 2) as i:
                for p in range(2):
                    t = i * 2 + p
                    pe.wait_ge(rows_ok, t + 1)
                    pe.wait_ge(r_t_ok, t + 1)
                    for k in range(KC):
                        mm = pe.transpose(ps[:, p, k * CHUNK:(k + 1) * CHUNK], rows[:, p, 128 * k:128 * k + 128],
                                          ident[0:CHUNK, 0:CHUNK])
                    mm.then_inc(r_turned, 1)
                for p in range(2):
                    t = i * 2 + p
                    pe.wait_ge(r_t_ok, t + 3)
                    pe.wait_ge(lg_ok, t + 1)
                    for k in range(KC):
                        mm = pe.matmul(ps[0:CHUNK, 2 + p, 0:NEXP], x_f[:, p, k * CHUNK:(k + 1) * CHUNK], router[:, k, :],
                                       start=(k == 0), stop=(k == KC - 1))
                    mm.then_inc(lg_mult, 1)
            pe.wait_ge(hot_ok, 1)
            all_hot = hot[:].rearrange("p t e -> p (t e)")
            pe.matmul(ps[0:CHUNK, 4, 0:NT * NEXP], early[:], all_hot, start=True, stop=True)
            pe.matmul(ps[0:CHUNK, 5, 0:NT * NEXP], ones[:], all_hot, start=True, stop=True).then_inc(counted, 1)
            pe.wait_ge(scale_ok, 2)

            def back(j, p):
                pe.wait_ge(y_f_ok, j + 2)
                pe.wait_ge(h_ok, j + 1)
                pe.wait_ge(x_f_ok, (j - p) * TC + 2 * TC + 2)
                for c in range(TC):
                    for m in range(KC):
                        at = 256 * (c % 2) + 128 * m
                        mm = pe.transpose(ps[0:CHUNK, XT + c // 2, at:at + 128], y_f[:, m, c * CHUNK:(c + 1) * CHUNK], ident[:])
                mm.then_inc(back_turned, 1)

            with pe.Fori(0, NP) as i:
                for p in range(2):
                    j = i * 2 + p
                    for c in range(TC):
                        pe.wait_ge(rows2_ok, j * TC + c + 1)
                        pe.wait_ge(x_f_ok, j * TC + c + 1)
                        pe.wait_ge(h_ok, i * 2 + 1)
                        for k in range(KC):
                            mm = pe.transpose(ps[:, XT + c % 2, k * CHUNK:(k + 1) * CHUNK], rows[:, c % 2, 128 * k:128 * k + 128],
                                              ident[0:CHUNK, 0:CHUNK])
                        mm.then_inc(turned, 1)
                for p in range(2):
                    j = i * 2 + p
                    pe.wait_ge(x_lo_ok, j + 2)
                    for k in range(ST + 2):
                        if k < ST:
                            q = j * ST + k
                            pe.wait_ge(prod_ok, q + 1)
                            for u, bank in ((0, GATE), (1, UP)):
                                for a in range(KC):
                                    for part, xs in ((0, x_hi), (0, x_lo), (1, x_hi)):
                                        mm = pe.matmul(ps[:, bank + k % 2, 0:TW], w1[part][:, k, u, a, :], xs[:, p, a, :],
                                                       start=(a == 0 and part == 0 and xs is x_hi), stop=(a == KC - 1 and part == 1))
                            mm.then_inc(hid_mult, 1)
                        if k == 2:
                            pe.wait_ge(y_f_ok, j + 1)
                        if k >= 2:
                            f = k - 2
                            pe.wait_ge(lo_ok, j * ST + f + 3)
                            for m in range(KC):
                                for part, gs in ((0, g_hi), (0, g_lo), (1, g_hi)):
                                    mm = pe.matmul(ps[:, Y + m, 0:TW], w2[part][:, f, 128 * m:128 * m + 128], gs[:, f % 2, :],
                                                   start=(f == 0 and part == 0 and gs is g_hi), stop=(f == ST - 1 and part == 1))
                            mm.then_inc(y_mult, 1)
                        if k == 1 and p == 1:
                            back(j - 1, 0)
                back(i * 2 + 1, 1)

        @block.scalar
        def _(act):
            for s, n in ((r_t_ok, 2), (x_f_ok, 2), (y_f_ok, 1)):
                act.sem_inc(s, n)
            with act.Fori(0, NPIECE // 2) as i:
                for p in range(2):
                    act.wait_ge(staged[p], i * 16 + 16)
                    nc.scalar.copy(w_hi[:, ds((i * 2 + p) * 1024, 1024)], stage[:, p, :]).then_inc(hi_ok_w, 1)
            act.wait_ge(var_ready, 1)
            nc.scalar.sqrt(small[:, 1, :], small[:, 0, :]).then_inc(root_done, 1)
            with act.Fori(0, NT // 2) as i:
                for p in range(2):
                    t = i * 2 + p
                    act.wait_ge(r_turned, t + 3)
                    act.wait_ge(lg_mult, t + 1)
                    nc.scalar.copy(x_f[:, p, 0:KC * CHUNK], ps[:, p, 0:KC * CHUNK]).then_inc(r_t_ok, 1)
            act.wait_ge(score_arg, 1)
            nc.scalar.activation(small[:, 4, :], small[:, 3, :], ACT.Sigmoid).then_inc(score_ok, 1)
            act.wait_ge(scale_ok, 2)
            with act.Fori(0, NT) as t:
                nc.scalar.activation(x_rows[:, ds(t, 1), :].rearrange("p o d -> p (o d)"),
                                     h[:, ds(t, 1), :].rearrange("p o d -> p (o d)"), ACT.Identity,
                                     bias=small[:, 5, ds(t, 1)], scale=small[:, 4, ds(t, 1)]).then_inc(x_rows_ok, 1)

            def silu(j, k):
                q = j * ST + k
                act.wait_ge(hid_mult, q + 1)
                nc.scalar.activation(g[:, k % 2, :], ps[:, GATE + k % 2, 0:TW], ACT.Silu).then_inc(silu_ok, 1)
                act.wait_ge(prod_ok, q + 3)
                act.wait_ge(y_mult, q + ST)
                nc.scalar.copy(g_hi[:, k % 2, :], pr[:, k % 2, :]).then_inc(hi_ok, 1)

            with act.Fori(0, NP) as i:
                for p in range(2):
                    j = i * 2 + p
                    act.wait_ge(x_lo_ok, j + 1)
                    for c in range(TC):
                        act.wait_ge(turned, j * TC + c + 3)
                        nc.scalar.copy(x_f[:, :, c * CHUNK:(c + 1) * CHUNK],
                                       ps[:, XT + c % 2, 0:KC * CHUNK].rearrange("p (k t) -> p k t", k=KC)).then_inc(x_f_ok, 1)
                    act.wait_ge(x_f_ok, j * TC + TC + 2)
                    act.wait_ge(y_mult, j * ST + 1)
                    nc.scalar.copy(x_hi[:, p], x_f[:]).then_inc(x_hi_ok, 1)
                for p in range(2):
                    j = i * 2 + p
                    for k in range(ST):
                        silu(j, k)
                    act.wait_ge(y_mult, j * ST + ST + Y_FREE)
                    act.wait_ge(back_turned, j + 1)
                    nc.scalar.copy(y_f[:], ps[:, Y:Y + KC, 0:TW]).then_inc(y_f_ok, 1)

        @block.vector
        def _(v):
            for s, n in ((lo_ok_w, 2), (lg_ok, 2), (x_lo_ok, 1), (prod_ok, 2), (lo_ok, 2), (h_ok, 1)):
                v.sem_inc(s, n)
            c = Chain(v, dve)
            with v.Fori(0, NPIECE // 2) as i:
                for p in range(2):
                    v.wait_ge(hi_ok_w, i * 2 + p + 1)
                    at = ds((i * 2 + p) * 1024, 1024)
                    v.tensor_tensor(w_lo[:, at], stage[:, p, :], w_hi[:, at].bitcast(F32), ALU.subtract).then_inc(lo_ok_w, 1)
            c.step(v.memset(ones[:], 1.0))
            row_stats(c, h, stats, mv)
            v.tensor_scalar(small[:, 0, :], mv[:, :, 1], LN_EPS, None, ALU.add).then_inc(var_ready, 1)
            v.wait_ge(root_done, 1)
            inverse_root(c, small[:, 0, :], small[:, 1, :], small[:, 2, :], small[:, 3, :])

            def row_tile(t, slot):
                return v.tensor_scalar(rows[:, slot, :], h[:, ds(t, 1), :].rearrange("p o d -> p (o d)"),
                                       mv[:, ds(t, 1), 0], small[:, 2, ds(t, 1)], ALU.subtract, ALU.mult)

            with v.Fori(0, NT // 2) as i:
                for p in range(2):
                    v.wait_ge(r_turned, i * 2 + p + 1)
                    row_tile(i * 2 + p, p).then_inc(rows_ok, 1)
                for p in range(2):
                    v.wait_ge(lg_mult, i * 2 + p + 3)
                    v.tensor_copy(lg[:, ds(i * 2 + p, 1), :].rearrange("p o e -> p (o e)"),
                                  ps[0:CHUNK, 2 + p, 0:NEXP]).then_inc(lg_ok, 1)
            v.wait_ge(lg_ok, NT + 2)
            v.wait_ge(loaded, 16 * 4)
            by_e = [CHUNK, NT, NEXP]
            tables = big[0:CHUNK, 0:4 * NT * NEXP].rearrange("p (a n) -> p a n", a=4)
            v.tensor_reduce(small[:, 3, :], lg[:], AX.X, ALU.max).then_inc(score_arg, 1)
            v.wait_ge(score_arg, 1)
            number = numbers[:, 0:NEXP].unsqueeze(1).broadcast_to(by_e)
            c.step(v.tensor_tensor(hot[:], lg[:], small[:, 3, :].unsqueeze(2).broadcast_to(by_e), ALU.is_ge))
            c.wait()
            c.step(v.tensor_tensor(lg[:], hot[:], number, ALU.mult))
            c.wait()
            c.step(v.tensor_reduce(small[:, 5, :], lg[:], AX.X, ALU.min))
            c.wait()
            v.tensor_tensor(hot[:], number, small[:, 5, :].unsqueeze(2).broadcast_to(by_e), ALU.is_equal).then_inc(hot_ok, 1)
            v.wait_ge(counted, 1)
            before, total, running = tables[:, 0, :], tables[:, 1, :], tables[:, 2, :]

            def expert_first(ap):
                return ap.rearrange("p (t e) -> p e t", e=NEXP)

            c.step(v.tensor_copy(before.rearrange("p (e t) -> p e t", e=NEXP), expert_first(ps[0:CHUNK, 4, 0:NT * NEXP])))
            c.step(v.tensor_copy(total.rearrange("p (e t) -> p e t", e=NEXP), expert_first(ps[0:CHUNK, 5, 0:NT * NEXP])))
            c.wait()
            c.step(v.tensor_tensor_scan(running, keep[:], total, 0.0, ALU.mult, ALU.add))
            c.wait()
            count = running.rearrange("p (e t) -> p e t", e=NEXP)[:, :, NT - 1]
            tiles, end = ends[:, 0, :], ends[:, 1, :]
            c.step(v.tensor_scalar(ends_i[:], count, ROWS - 1, None, ALU.add))
            c.step(v.memset(ends[:, 3, :], 1.0))
            c.wait()
            c.step(v.tensor_scalar(ends_i[:], ends_i[:], 7, None, ALU.arith_shift_right))
            c.wait()
            c.step(v.tensor_copy(tiles, ends_i[:]))
            c.wait()
            c.step(v.tensor_tensor_scan(end, ends[:, 3, :], tiles, 0.0, ALU.mult, ALU.add))
            c.step(v.tensor_tensor(before, before, running, ALU.add))
            c.wait()
            c.step(v.tensor_tensor(ends[:, 2, :], end, tiles, ALU.subtract))
            c.step(v.tensor_tensor(before, before, total, ALU.subtract))
            c.wait()
            c.step(v.tensor_scalar(ends[:, 2, :], ends[:, 2, :], float(ROWS), None, ALU.mult))
            c.wait()
            c.step(v.tensor_tensor(before.rearrange("p (e t) -> p e t", e=NEXP), before.rearrange("p (e t) -> p e t", e=NEXP),
                                   ends[:, 2, :].unsqueeze(2).broadcast_to([CHUNK, NEXP, NT]), ALU.add))
            c.wait()
            c.step(v.tensor_tensor(lg[:], before.rearrange("p (e t) -> p t e", e=NEXP), hot[:], ALU.mult))
            c.wait()
            v.wait_ge(score_ok, 1)
            c.step(v.tensor_reduce(small[:, 3, :], lg[:], AX.X, ALU.add))
            c.wait()
            v.tensor_copy(place[:], small[:, 3, :]).then_inc(scale_ok, 1)
            cmp = big[0:CHUNK, 4 * NT * NEXP:4 * NT * NEXP + G_TILES * NEXP].rearrange("p (g e) -> p g e", e=NEXP)
            c.step(v.tensor_tensor(cmp, numbers[:, NEXP:].unsqueeze(2).broadcast_to([CHUNK, G_TILES, NEXP]),
                                   end.unsqueeze(1).broadcast_to([CHUNK, G_TILES, NEXP]), ALU.is_ge))
            c.wait()
            c.step(v.tensor_reduce(tables[:, 3, 0:G_TILES], cmp, AX.X, ALU.add))
            c.wait()
            c.step(v.tensor_scalar(tile_expert[:], tables[:, 3, 0:G_TILES], float(NEXP - 1), None, ALU.min))
            c.step(v.tensor_tensor(small[:, 4, :], small[:, 4, :], small[:, 2, :], ALU.mult))
            c.wait()
            v.scalar_tensor_tensor(small[:, 5, :], mv[:, :, 0], -1.0, small[:, 4, :], ALU.mult, ALU.mult).then_inc(scale_ok, 1)
            v.wait_ge(x_rows_ok, NT)
            with v.Fori(0, NP) as i:
                for p in range(2):
                    j = i * 2 + p
                    for cc in range(TC):
                        v.wait_ge(turned, j * TC + cc + 1)
                        row_tile(j * TC + cc, cc % 2).then_inc(rows2_ok, 1)
                    v.wait_ge(x_hi_ok, j + 1)
                    v.tensor_tensor(x_lo[:, p], x_f[:], x_hi[:, p].bitcast(F32), ALU.subtract).then_inc(x_lo_ok, 1)

                def add_back(j):
                    v.wait_ge(back_turned, j + 2)
                    out = h[:, ds(j * TC, TC), :].rearrange("p (a b) d -> p a (b d)", a=2)
                    v.tensor_tensor(out, out, ps[0:CHUNK, XT:XT + 2, :], ALU.add).then_inc(h_ok, 1)

                for p in range(2):
                    j = i * 2 + p
                    for k in range(ST + 1):
                        if k < ST:
                            q = j * ST + k
                            v.wait_ge(silu_ok, q + 1)
                            v.wait_ge(lo_ok, q + 1)
                            v.tensor_tensor(pr[:, k % 2, :], g[:, k % 2, :], ps[:, UP + k % 2, 0:TW], ALU.mult).then_inc(prod_ok, 1)
                        if k >= 1:
                            q = j * ST + k - 1
                            v.wait_ge(hi_ok, q + 1)
                            v.wait_ge(y_mult, q + ST)
                            v.tensor_tensor(g_lo[:, (k - 1) % 2, :], pr[:, (k - 1) % 2, :], g_hi[:, (k - 1) % 2, :].bitcast(F32),
                                            ALU.subtract).then_inc(lo_ok, 1)
                        if k == 4 and p == 1:
                            add_back(j - 1)
                add_back(i * 2 + 1)


def routed_experts(nc, io, h, out, x_sorted, y_sorted, place, tile_expert, w_gu, ident):
    with ExitStack() as ctx:
        def sb(name, shape, dt=F32):
            return ctx.enter_context(nc.sbuf_tensor("ex_" + name, shape, dt))

        def sem(name):
            return ctx.enter_context(nc.semaphore("ex_" + name))

        U = 4
        NGATHER = 4
        TG = NT // NGATHER
        w_d = sb("w_d", [128, NEXP, EF // 128, D])
        x = sb("x", [ROWS, U, D])
        x_t = sb("x_t", [128, 2, KC, ROWS])
        g = sb("g", [ROWS, 2, EF])
        pr = sb("pr", [ROWS, 2, EF])
        pr_t = sb("pr_t", [128, 2, EF // 128, ROWS])
        y = sb("y", [ROWS, G_TILES, D])
        y_rows = sb("y_rows", [CHUNK, NT, D])
        ps = ctx.enter_context(nc.psum_tensor("ex_ps", [128, 8, 512], F32))
        XT, GU, PT, Y = 0, 2, 4, 6
        w_loaded, x_turned, x_t_ok, gu_mult, silu_ok = sem("w_loaded"), sem("x_turned"), sem("x_t_ok"), sem("gu_mult"), sem("silu_ok")
        x_loaded = [sem(f"x_loaded{u}") for u in range(U)]
        prod_ok, p_turned, p_t_ok, y_mult, y_ok, y_stored = (sem("prod_ok"), sem("p_turned"), sem("p_t_ok"), sem("y_mult"),
                                                             sem("y_ok"), sem("y_stored"))
        gathered = [sem(f"gathered{n}") for n in range(NGATHER)]
        h_ok, out_stored = sem("h_ok"), sem("out_stored")
        block = ctx.enter_context(nc.Block())

        @block.sync
        def _(sp):
            with sp.Fori(0, G_TILES // U) as i:
                for u in range(U):
                    q = i * U + u
                    sp.wait_ge(x_turned, q + 1)
                    sp.dma_start(x[:, u, :], x_sorted[ds(q * ROWS, ROWS), :]).then_inc(x_loaded[u], 16)
            for n in range(NGATHER):
                sp.wait_ge(h_ok, n + 1)
                sp.dma_start(out.rearrange("c (j p) d -> p (c j) d", p=CHUNK)[:, TG * n:TG * n + TG, :],
                             h[:, TG * n:TG * n + TG, :]).then_inc(out_stored, 16)
            sp.wait_ge(out_stored, 16 * NGATHER)

        @block.gpsimd
        def _(gp):
            gp.dma_start(w_d[:], io["ex_d"]).then_inc(w_loaded, 16)
            with gp.Fori(0, G_TILES // U) as i:
                for u in range(U):
                    q = i * U + u
                    gp.wait_ge(y_ok, q + 3)
                    gp.dma_start(y_sorted[ds(q * ROWS, ROWS), :], y[:, ds(q, 1), :].rearrange("p o d -> p (o d)")).then_inc(y_stored, 16)
            gp.wait_ge(y_stored, 16 * G_TILES)
            for t in range(NT):
                gp.indirect_dma_start(y_rows[:, t, :], None, y_sorted,
                                      bass.IndirectOffsetOnAxis(ap=place[:, t:t + 1].bitcast(U32), axis=0)).then_inc(gathered[t // TG], 16)

        @block.tensor
        def _(pe):
            for s, n in ((x_turned, U), (gu_mult, 2), (p_turned, 2), (y_mult, 2)):
                pe.sem_inc(s, n)
            with pe.Fori(0, G_TILES // U) as i:
                for s in range(U + 1):
                    if s < U:
                        q, b = i * U + s, s % 2
                        pe.wait_ge(x_loaded[s], i * 16 + 16)
                        pe.wait_ge(x_t_ok, q + 1)
                        for k in range(KC):
                            mm = pe.transpose(ps[:, XT + b, ROWS * k:ROWS * k + ROWS], x[:, s, 128 * k:128 * k + 128], ident[:])
                        mm.then_inc(x_turned, 1)
                    if s >= 1:
                        q, b = i * U + s - 1, (s - 1) % 2
                        pe.wait_ge(prod_ok, q + 3)
                        pe.wait_ge(p_t_ok, q + 1)
                        for k in range(EF // 128):
                            mm = pe.transpose(ps[:, PT + b, ROWS * k:ROWS * k + ROWS], pr[:, b, 128 * k:128 * k + 128], ident[:])
                        mm.then_inc(p_turned, 1)
                    if s < U:
                        q, b = i * U + s, s % 2
                        e = pe.value_load(tile_expert[0:1, ds(q, 1)], min_val=0, max_val=NEXP - 1)
                        pe.wait_ge(x_t_ok, q + 3)
                        pe.wait_ge(prod_ok, q + 1)
                        for k in range(KC):
                            mm = pe.matmul(ps[0:ROWS, GU + b, :], x_t[:, b, k, :],
                                           w_gu[:, ds(e, 1), k, :].rearrange("p o f -> p (o f)"), start=(k == 0), stop=(k == KC - 1))
                        mm.then_inc(gu_mult, 1)
                    if s >= 1:
                        q, b = i * U + s - 1, (s - 1) % 2
                        if s == 1:
                            pe.wait_ge(w_loaded, 16)
                        e = pe.value_load(tile_expert[0:1, ds(q, 1)], min_val=0, max_val=NEXP - 1)
                        pe.wait_ge(p_t_ok, q + 3)
                        pe.wait_ge(y_ok, q + 1)
                        for k in range(EF // 128):
                            mm = pe.matmul(ps[0:ROWS, Y + b, 0:D], pr_t[:, b, k, :],
                                           w_d[:, ds(e, 1), k, :].rearrange("p o d -> p (o d)"), start=(k == 0), stop=(k == EF // 128 - 1))
                        mm.then_inc(y_mult, 1)

        @block.scalar
        def _(act):
            for s, n in ((x_t_ok, 2), (p_t_ok, 2)):
                act.sem_inc(s, n)
            with act.Fori(0, G_TILES // U) as i:
                for s in range(U + 1):
                    if s < U:
                        q, b = i * U + s, s % 2
                        act.wait_ge(x_turned, q + 1 + U)
                        act.wait_ge(gu_mult, q + 1)
                        nc.scalar.copy(x_t[:, b].rearrange("p k t -> p (k t)"), ps[:, XT + b, 0:KC * ROWS]).then_inc(x_t_ok, 1)
                    if s >= 1:
                        q, b = i * U + s - 1, (s - 1) % 2
                        act.wait_ge(p_turned, q + 3)
                        act.wait_ge(y_mult, q + 1)
                        nc.scalar.copy(pr_t[:, b].rearrange("p k t -> p (k t)"), ps[:, PT + b, 0:EF]).then_inc(p_t_ok, 1)
                    if s < U:
                        q, b = i * U + s, s % 2
                        act.wait_ge(gu_mult, q + 3)
                        act.wait_ge(prod_ok, q + 1)
                        nc.scalar.activation(g[:, b, :], ps[0:ROWS, GU + b, 0:EF], ACT.Silu).then_inc(silu_ok, 1)

        @block.vector
        def _(v):
            for s, n in ((prod_ok, 2), (y_ok, 2)):
                v.sem_inc(s, n)
            with v.Fori(0, G_TILES // U) as i:
                for s in range(U + 1):
                    if s < U:
                        q, b = i * U + s, s % 2
                        v.wait_ge(silu_ok, q + 1)
                        v.wait_ge(p_turned, q + 1)
                        v.tensor_tensor(pr[:, b, :], g[:, b, :], ps[0:ROWS, GU + b, EF:2 * EF], ALU.mult).then_inc(prod_ok, 1)
                    if s >= 1:
                        q, b = i * U + s - 1, (s - 1) % 2
                        v.wait_ge(y_mult, q + 3)
                        v.tensor_copy(y[:, ds(q, 1), :].rearrange("p o d -> p (o d)"), ps[0:ROWS, Y + b, 0:D]).then_inc(y_ok, 1)
            for n in range(NGATHER):
                v.wait_ge(gathered[n], 16 * TG)
                part = h[:, TG * n:TG * n + TG, :]
                v.tensor_tensor(part, part, y_rows[:, TG * n:TG * n + TG, :], ALU.add).then_inc(h_ok, 1)


def build(nc, io, out):
    with ExitStack() as ctx:
        h = ctx.enter_context(nc.sbuf_tensor("h", [CHUNK, NT, D], F32))
        ident = ctx.enter_context(nc.sbuf_tensor("ident", [128, 128], F32))
        ident_ready = ctx.enter_context(nc.semaphore("ident_ready"))
        mx_sorted, my_sorted = ([nc.dram_tensor(f"m{n}_sorted{grp}", (SORTED, D), F32, kind="Internal").ap()
                                 for grp in range(NG2)] for n in "xy")
        x_sorted = nc.dram_tensor("x_sorted", (G_TILES * ROWS, D), F32, kind="Internal").ap()
        y_sorted = nc.dram_tensor("y_sorted", (G_TILES * ROWS, D), F32, kind="Internal").ap()
        embed_tokens(nc, io, h, ident, ident_ready)
        embed_text(nc, io, h, ident, ident_ready)
        with nc.sbuf_tensor("x0_t", [128, KC, T], F32) as x_t:
            normalise(nc, "n0", h, x_t, ident, ident_ready)
            linear_attention(nc, io, h, x_t, mx_sorted + [x_sorted], ident, ident_ready)
        h_dram = nc.dram_tensor("h_rows", (CHUNK, NT, D), F32, kind="Internal").ap()
        bias_dram = nc.dram_tensor("bias_parts", (2, EXPERTS * (FF + D)), F32, kind="Internal").ap()
        recursive_mixture(nc, io, h, mx_sorted, my_sorted, h_dram, bias_dram, ident)
        with nc.sbuf_tensor("x2_t", [128, KC, T], F32) as x_t:
            normalise(nc, "n2", h, x_t, ident, ident_ready)
            retention(nc, io, h, x_t, ident)
        place = ctx.enter_context(nc.sbuf_tensor("place", [CHUNK, NT], I32))
        tile_expert = ctx.enter_context(nc.sbuf_tensor("tile_expert", [CHUNK, G_TILES], I32))
        w_gu = ctx.enter_context(nc.sbuf_tensor("ex_w_gu", [128, NEXP, KC, 2 * EF], F32))
        route_and_share(nc, io, h, x_sorted, place, tile_expert, w_gu, ident)
        routed_experts(nc, io, h, out, x_sorted, y_sorted, place, tile_expert, w_gu, ident)


def host_arrays(inputs):
    import numpy as np
    f = lambda n: np.asarray(inputs[n])

    def pairs(w):
        return w.reshape(w.shape[0] // 128, 128, -1).transpose(1, 0, 2)

    io = {
        "x": f("x").transpose(3, 2, 0, 1), "log_dt": f("L0_tok_log_dt"), "inv_A_real": f("L0_tok_inv_A_real").T,
        "A_imag": f("L0_tok_A_imag").T, "B_ri": f("L0_tok_B_ri").transpose(2, 1, 0),
        "sign": np.repeat(np.array([[1.0], [-1.0]], np.float32), MODES, axis=0),
        "x_txt": f("x_txt").T, "W_txt": np.concatenate([f("L0_txt_W0"), f("L0_txt_W1"), f("L0_txt_W2")]).reshape(3, 128, D).transpose(1, 0, 2),
        "E0": f("L0_txt_E0"), "E1": f("L0_txt_E1"), "E2": f("L0_txt_E2"),
        "la_w_qv": pairs(np.concatenate([f("L0_attn_Wq").T, f("L0_attn_Wv").T], axis=1)),
        "la_w_k": pairs(f("L0_attn_Wk").T), "la_w_o": pairs(f("L0_attn_Wo").T),
        "la_b_qv": np.concatenate([f("L0_attn_bq"), f("L0_attn_bv")])[None], "la_b_o": f("L0_attn_bo")[None],
        "la_cols": np.stack([f("L0_attn_bk"), f("L0_attn_ln_g"), f("L0_attn_ln_b")]).reshape(3, KC, 128).transpose(2, 0, 1),
        "head_mask": np.kron(np.eye(8, dtype=np.float32), np.ones((16, 16), np.float32)),
        "mo_w": np.concatenate([
            f("L0_ffn_W1").reshape(EXPERTS, KC, 128, FF).transpose(2, 0, 1, 3).reshape(128, -1),
            f("L0_ffn_W2").reshape(EXPERTS, FT, 128, D).transpose(2, 0, 1, 3).reshape(128, -1)], axis=1),
        "mo_w_g": f("L0_ffn_Wg").reshape(ROUNDS, KC, 128, EXPERTS).transpose(2, 1, 0, 3), "mo_b_g": f("L0_ffn_bg")[None],
        "mo_b": np.concatenate([f("L0_ffn_b1"), f("L0_ffn_b2")], axis=1).reshape(128, -1),
        "mo_numbers": np.arange(MT, dtype=np.float32)[None],
        "mo_keep": (np.arange(EXPERTS * GT) % GT != 0).astype(np.float32)[None],
        "before": np.stack([np.tri(EXPERTS, k=-1), np.tri(EXPERTS, k=-1).T]).astype(np.float32)[None],
        "re_w": pairs(np.concatenate([f("L1_attn_W" + n) for n in "qkvg"], axis=1)), "re_w_o": pairs(f("L1_attn_Wo")),
        "re_bias": np.concatenate([f("L1_attn_b" + n) for n in "qkvg"])[None],
        "re_rows3": np.stack([f("L1_attn_bo"), f("L1_attn_gamma"), f("L1_attn_beta")])[None],
        "decay": np.stack([0.25 * 0.99 ** np.arange(S), 0.99 ** -np.arange(S).astype(np.float64)], axis=1)
        .astype(np.float32).reshape(NCH, CHUNK, 2).transpose(1, 0, 2),
        "causal": np.tri(CHUNK, dtype=np.float32).T, "head_of": np.kron(np.eye(8, dtype=np.float32), np.ones((16, 1), np.float32)),
        "router": pairs(f("L1_ffn_router_w").T), "early": np.tri(CHUNK, k=-1, dtype=np.float32).T,
        "keep": (np.arange(NEXP * NT) % NT != 0).astype(np.float32)[None],
        "numbers": np.concatenate([np.arange(NEXP) - NEXP, np.arange(G_TILES)]).astype(np.float32)[None],
        "sh_w": np.concatenate([
            np.stack([f("L1_ffn_shared_gate_w"), f("L1_ffn_shared_up_w")]).reshape(2, ST, 128, KC, 128)
            .transpose(4, 1, 0, 3, 2).reshape(128, -1),
            f("L1_ffn_shared_down_w").T.reshape(ST, 128, D).transpose(1, 0, 2).reshape(128, -1)], axis=1),
        "ex_gu": f("L1_ffn_gate_up_proj").reshape(NEXP, KC, 128, 2 * EF).transpose(2, 0, 1, 3),
        "ex_d": f("L1_ffn_down_proj").reshape(NEXP, EF // 128, 128, D).transpose(2, 0, 1, 3),
        "ident": np.eye(128, dtype=np.float32),
    }
    return {k: np.ascontiguousarray(v) for k, v in io.items()}


def kernel(**inputs):
    import concourse.bacc as _bacc
    from concourse.bass_utils import run_bass_kernel_spmd as _run

    nc = _bacc.Bacc("TRN2", target_bir_lowering=False, num_devices=1)
    arrays, io = {}, {}
    for name, a in host_arrays(inputs).items():
        arrays[f"in_{name}_dram"] = a
        io[name] = nc.dram_tensor(f"in_{name}_dram", a.shape, mybir.dt.from_np(a.dtype), kind="ExternalInput").ap()
    out = nc.dram_tensor("out_0_dram", (B, S, D), F32, kind="ExternalOutput").ap()
    build(nc, io, out)
    r = _run(nc, [arrays], core_ids=[0])
    return r.results[0]["out_0_dram"]
```

```python
from contextlib import ExitStack, contextmanager

import concourse.bass as bass
from concourse import mybir

F32 = mybir.dt.float32
F32R = mybir.dt.float32r
I32 = mybir.dt.int32
U32 = mybir.dt.uint32
ALU = mybir.AluOpType
ACT = mybir.ActivationFunctionType
AX = mybir.AxisListType
ds = bass.ds

B, SSM_ROWS, TXT_ROWS, D = 8, 256, 77, 256
S = SSM_ROWS + TXT_ROWS
CHUNK = S // 3
NCH = S // CHUNK
NT = B * NCH
T = B * S
KC = D // 128
MODES = 64
NA, NB = 8, 32
CA = B * NA
HG = 16
CUT = (0, 5000, 10000, 50257)
TXT_AT = SSM_ROWS - (NCH - 1) * CHUNK
HEADS, DH = 16, 16
LN_EPS = 1e-05


class Chain:

    def __init__(self, eng, sem, start=0):
        self.eng, self.sem, self.start, self.n = eng, sem, start, 0

    def step(self, ins):
        ins.then_inc(self.sem, 1)
        self.n += 1

    def wait(self):
        self.eng.wait_ge(self.sem, self.start + self.n)


def exact_exp(c, out, x, power, rest):
    v = c.eng
    c.step(v.tensor_scalar(x, x, -87.0, 88.0, ALU.max, ALU.min))
    c.wait()
    c.step(v.tensor_scalar(power, x, 1.4426950408889634, 12582912.0, ALU.mult, ALU.add))
    c.wait()
    c.step(v.tensor_scalar(rest, power, 12582912.0, None, ALU.subtract))
    c.wait()
    c.step(v.scalar_tensor_tensor(x, rest, -0.693359375, x, ALU.mult, ALU.add))
    c.wait()
    c.step(v.scalar_tensor_tensor(x, rest, 2.12194440054690583e-4, x, ALU.mult, ALU.add))
    bits = power.bitcast(I32)
    c.step(v.tensor_scalar(bits, bits, 23, None, ALU.logical_shift_left))
    c.wait()
    c.step(v.tensor_scalar(bits, bits, 127 << 23, None, ALU.add))
    c.step(v.tensor_scalar(out, x, 1 / 5040, None, ALU.mult))
    for k in (720, 120, 24, 6, 2, 1):
        c.wait()
        c.step(v.scalar_tensor_tensor(out, out, 1 / k, x, ALU.add, ALU.mult))
    c.wait()
    c.step(v.scalar_tensor_tensor(out, out, 1.0, power, ALU.add, ALU.mult))
    c.wait()


@contextmanager
def cleared_semaphores(nc, prefix):
    sems = []

    def sem(name):
        sems.append(nc.alloc_semaphore(name=prefix + name))
        return sems[-1]

    yield sem
    nc.clear_and_free_semaphores(sems)
    nc.all_engine_barrier()


def embed(nc, io, h, ident, ident_ready):
    with ExitStack() as ctx:
        def sb(name, shape, dt=F32):
            return ctx.enter_context(nc.sbuf_tensor(name, shape, dt))

        def sem(name):
            return ctx.enter_context(nc.semaphore(name))

        pool_ram = sb("pool_ram", [128, 2 * B * D + NB // 2 * D])
        ssm_x = pool_ram[:, 0:2 * B * D].rearrange("p (s c h) -> p s c h", s=2, c=B)
        z_swap = pool_ram[:, 2 * B * D:].rearrange("p (b h) -> p b h", h=D)
        prod = pool_ram[0:CA].rearrange("p (h b) -> p h b", b=NB)
        left_h = sb("left_h", [128, 2, HG, CA])
        z_low = sb("z_low", [128, NB, D])
        left = sb("left", [128, B, NA, D])
        ct_im = sb("ct_im", [128, B, D])
        w_hi = sb("w_hi", [128, 2, NA, D])
        par = sb("par", [128, 5, D])
        tmp = sb("tmp", [128, 6, D])
        sq = sb("sq", [128, 5, 2, D])
        sign = sb("sign", [128, 1])
        loaded, params = sem("ssm_loaded"), sem("ssm_params")
        dve, pool = sem("ssm_dve"), sem("ssm_pool")
        left_done = sem("ssm_left")
        staged, multiplied, stored = sem("ssm_staged"), sem("ssm_multiplied"), sem("ssm_stored")
        turned, kept_even, kept_odd = sem("ssm_turned"), sem("ssm_kept_even"), sem("ssm_kept_odd")
        product = ctx.enter_context(nc.psum_tensor("ssm_product", [128, 2, HG, NB], F32))
        rows_ps = ctx.enter_context(nc.psum_tensor("ssm_rows", [128, 2, 8, CA], F32))
        NBAND = len(CUT) - 1
        col = (0, 256, 320, 384)
        KT = col[-1] // 128
        SLOTS = 4
        tokens = sb("txt_tokens", [TXT_ROWS, B], I32)
        row = sb("txt_row", [TXT_ROWS, NBAND, B], I32)
        inside = sb("txt_inside", [TXT_ROWS, NBAND, B])
        below = sb("txt_below", [TXT_ROWS, NBAND, B])
        txt_room = left_h[:].rearrange("p s h c -> p (s h c)")
        txt_w = txt_room[:, 0:KT * D].rearrange("p (k d) -> p k d", k=KT)
        emb_t = txt_room[:, KT * D:KT * D + 2 * KT * TXT_ROWS].rearrange("p (s n) -> p s n", s=2)
        ct_room = ct_im[0:TXT_ROWS].rearrange("p c h -> p (c h)")
        emb = ct_room[:, 0:SLOTS * col[-1]].rearrange("p (s n) -> p s n", s=SLOTS)
        res = ct_room[:, SLOTS * col[-1]:SLOTS * col[-1] + 2 * D].rearrange("p (s d) -> p s d", s=2)
        turn_ps = ctx.enter_context(nc.psum_tensor("txt_turn", [128, 2, 512], F32))
        out_ps = ctx.enter_context(nc.psum_tensor("txt_out", [128, 2, 512], F32))
        t_loaded, w_loaded, rows_known = sem("txt_loaded"), sem("txt_wloaded"), sem("txt_rows_known")
        gathered = [sem(f"txt_gathered{n}") for n in range(SLOTS)]
        masked_ok, t_turned, copied, t_mult, res_ok = (sem("txt_masked_ok"), sem("txt_turned"), sem("txt_copied"), sem("txt_mult"),
                                                       sem("txt_res_ok"))
        placed = [sem("txt_placed0"), sem("txt_placed1")]
        block = ctx.enter_context(nc.Block())

        scratch = left[:].rearrange("p c a h -> p (c a) h")

        turns = [(j, g) for g in range(NB // 8) for j in range(NCH)]

        def rows_of(j):
            return min(CHUNK, D - j * CHUNK)

        def row_in(n, j):
            return rows_ps[0:rows_of(j), n % 2].rearrange("p b (c a) -> p c a b", a=NA)

        def row_out(j, g):
            out = h[0:rows_of(j)].rearrange("p (c j) (a b) -> p j c a b", j=NCH, b=NB)
            return out[:, j, :, :, 8 * g:8 * g + 8]

        @block.sync
        def _(sp):
            sp.dma_start(tokens[:], io["x_txt"]).then_inc(t_loaded, 16)
            for half in range(2):
                rows = slice(64 * half, 64 * half + 64)
                sp.dma_start(par[rows, 0, :], io["log_dt"].rearrange("(o h) -> o h", o=1).broadcast_to([64, D])).then_inc(params, 16)
                sp.dma_start(par[rows, 1, :], io["inv_A_real"]).then_inc(params, 16)
                sp.dma_start(par[rows, 2, :], io["A_imag"]).then_inc(params, 16)
                sp.dma_start(par[rows, 3, :], io["B_ri"][0]).then_inc(params, 16)
                sp.dma_start(par[rows, 4, :], io["B_ri"][1]).then_inc(params, 16)
            sp.dma_start(sign[:], io["sign"]).then_inc(params, 16)
            sp.dma_start(ssm_x[:, 0], io["x"].rearrange("r n c h -> (r n) c h")).then_inc(loaded, 16)
            sp.dma_start(ssm_x[0:64, 1], io["x"][1]).then_inc(loaded, 16)
            sp.dma_start(ssm_x[64:128, 1], io["x"][0]).then_inc(loaded, 16)
            sp.dma_start(ident[:], io["ident"]).then_inc(ident_ready, 16)
            sp.dma_start(txt_w, io["W_txt"]).then_inc(w_loaded, 16)
            last = h[:].rearrange("p (c j) d -> p c j d", j=NCH)[TXT_AT:CHUNK, :, NCH - 1, :]
            for b in range(B):
                sp.wait_ge(res_ok, b + 1)
                sp.dma_start(last[:, b, :], res[:, b % 2, :]).then_inc(placed[b % 2], 16)

        @block.scalar
        def _(act):
            for b in range(B):
                act.wait_ge(t_turned, b + 1)
                nc.scalar.copy(emb_t[:, b % 2, :], turn_ps[:, b % 2, 0:KT * TXT_ROWS]).then_inc(copied, 1)
                act.wait_ge(t_mult, b + 1)
                if b >= 2:
                    act.wait_ge(placed[b % 2], b // 2 * 16)
                nc.scalar.copy(res[:, b % 2, :], out_ps[0:TXT_ROWS, b % 2, 0:D]).then_inc(res_ok, 1)
            act.wait_ge(left_done, NA)
            with act.Fori(0, D // HG // 2) as i:
                for p in range(2):
                    act.wait_ge(multiplied, i * 2 + p + 1)
                    nc.scalar.copy(left_h[:, p].rearrange("p h c -> p c h"),
                                   scratch[:, :, ds(i * 2 * HG + p * HG, HG)]).then_inc(staged, 1)
            for n, (j, g) in enumerate(turns):
                if n % 2:
                    act.wait_ge(turned, n + 1)
                    nc.scalar.copy(row_out(j, g), row_in(n, j)).then_inc(kept_odd, 1)

        @block.vector
        def _(v):
            c = Chain(v, dve)
            v.sem_inc(stored, 2)

            def tt(out, a, b, op):
                c.step(v.tensor_tensor(out, a, b, op))

            v.wait_ge(t_loaded, 16)
            for k in range(NBAND):
                c.step(v.tensor_scalar(row[:, k, :], tokens[:], -CUT[k], 0, ALU.add, ALU.max))
                c.step(v.tensor_scalar(inside[:, k, :], tokens[:], CUT[k], None, ALU.is_ge))
                c.step(v.tensor_scalar(below[:, k, :], tokens[:], CUT[k + 1], None, ALU.is_lt))
            c.wait()
            for k in range(NBAND):
                c.step(v.tensor_scalar(row[:, k, :], row[:, k, :], CUT[k + 1] - CUT[k] - 1, None, ALU.min))
            c.wait()
            v.tensor_tensor(inside[:], inside[:], below[:], ALU.mult).then_inc(rows_known, 1)

            dt, ea, t2, t3, ur, ui = (tmp[:, k, :] for k in range(6))
            v.wait_ge(params, 16 * 11)
            exact_exp(c, tmp[:, 0:2, :], par[:, 0:2, :], tmp[:, 2:4, :], tmp[:, 4:6, :])
            c.step(v.scalar_tensor_tensor(ur, ea, -0.5, dt, ALU.mult, ALU.mult))
            c.step(v.scalar_tensor_tensor(ui, par[:, 2, :], 0.5, dt, ALU.mult, ALU.mult))
            c.wait()
            c.step(v.tensor_scalar(t2, ur, -1.0, 1.0, ALU.mult, ALU.add))
            tt(t3, ui, ui, ALU.mult)
            tt(ea, ur, ur, ALU.mult)
            c.wait()
            tt(t2, t2, t2, ALU.mult)
            tt(ea, ea, t3, ALU.add)
            c.wait()
            tt(t2, t2, t3, ALU.add)
            c.step(v.tensor_scalar(ea, ea, -1.0, 1.0, ALU.mult, ALU.add))
            c.wait()
            c.step(v.reciprocal(t2, t2))
            c.wait()
            tt(sq[:, 0, 0, :], ea, t2, ALU.mult)
            c.step(v.scalar_tensor_tensor(sq[:, 0, 1, :], ui, 2.0, t2, ALU.mult, ALU.mult))
            power = [(sq[:, k, 0, :], sq[:, k, 1, :]) for k in range(5)]
            power += [(w_hi[:, 0, a, :], w_hi[:, 1, a, :]) for a in (1, 2, 4)]
            for k in range(7):
                (re, im), (re2, im2) = power[k], power[k + 1]
                c.wait()
                tt(t2, re, re, ALU.mult)
                tt(t3, im, im, ALU.mult)
                c.step(v.scalar_tensor_tensor(im2, re, 2.0, im, ALU.mult, ALU.mult))
                c.wait()
                tt(re2, t2, t3, ALU.subtract)
            c.step(v.memset(w_hi[:, 0, 0, :], 1.0))
            c.step(v.memset(w_hi[:, 1, 0, :], 0.0))
            c.wait()
            for n, lo, by, to in ((1, 1, 2, 3), (3, 1, 4, 5)):
                ar, ai = w_hi[:, 0, lo:lo + n, :], w_hi[:, 1, lo:lo + n, :]
                br = w_hi[:, 0, by:by + 1, :].broadcast_to([128, n, D])
                bi = w_hi[:, 1, by:by + 1, :].broadcast_to([128, n, D])
                m = [scratch[:, 3 * k:3 * k + n, :] for k in range(4)]
                tt(m[0], ar, br, ALU.mult)
                tt(m[1], ai, bi, ALU.mult)
                tt(m[2], ar, bi, ALU.mult)
                tt(m[3], ai, br, ALU.mult)
                c.wait()
                tt(w_hi[:, 0, to:to + n, :], m[0], m[1], ALU.subtract)
                tt(w_hi[:, 1, to:to + n, :], m[2], m[3], ALU.add)
                c.wait()
            c.step(v.memset(z_low[0:64, 0, :], 1.0))
            c.step(v.memset(z_low[64:128, 0, :], 0.0))
            c.step(v.memset(z_swap[0:64, 0, :], 0.0))
            c.step(v.memset(z_swap[64:128, 0, :], 1.0))
            for k in range(5):
                n = 1 << k
                wr = sq[:, k, 0:1, :].broadcast_to([128, n, D])
                wi = sq[:, k, 1:2, :].broadcast_to([128, n, D])
                z0, s0 = z_low[:, 0:n, :], z_swap[:, 0:n, :]
                z1 = z_low[:, n:2 * n, :]
                ta, tb = scratch[:, 0:n, :], scratch[:, 16:16 + n, :]
                c.wait()
                tt(ta, s0, wi, ALU.mult)
                tt(z1, z0, wr, ALU.mult)
                if k < 4:
                    s1 = z_swap[:, n:2 * n, :]
                    tt(tb, z0, wi, ALU.mult)
                    tt(s1, s0, wr, ALU.mult)
                c.wait()
                tt(z1, z1, ta, ALU.add)
                if k < 4:
                    tt(s1, s1, tb, ALU.subtract)
            c.step(v.tensor_scalar(tmp[:, 0, :], par[:, 3, :], sign[:, 0:1], 2.0, ALU.mult, ALU.mult))
            c.step(v.tensor_scalar(tmp[:, 1, :], par[:, 4, :], 2.0, None, ALU.mult))
            c.step(v.tensor_scalar(tmp[:, 2, :], par[:, 3, :], -2.0, None, ALU.mult))
            c.step(v.tensor_scalar(tmp[:, 3, :], par[:, 4, :], sign[:, 0:1], -2.0, ALU.mult, ALU.mult))
            c.wait()
            v.wait_ge(loaded, 48)
            coef = [tmp[:, k:k + 1, :].broadcast_to([128, B, D]) for k in range(4)]
            x1, x2 = ssm_x[:, 0], ssm_x[:, 1]
            spare = left[:, :, 1, :]
            tt(left[:, :, 0, :], x1, coef[0], ALU.mult)
            tt(spare, x2, coef[1], ALU.mult)
            for p in range(2):
                v.wait_ge(placed[p], B // 2 * 16)
            tt(ct_im[:], x2, coef[2], ALU.mult)
            c.wait()
            tt(left[:, :, 0, :], left[:, :, 0, :], spare, ALU.subtract)
            tt(left[:, :, 2, :], x1, coef[3], ALU.mult)
            c.wait()
            tt(ct_im[:], ct_im[:], left[:, :, 2, :], ALU.add)
            c.wait()
            for a in range(1, NA):
                wr = w_hi[:, 0, a:a + 1, :].broadcast_to([128, B, D])
                if a == 1:
                    v.sem_inc(left_done, 1)
                tt(left[:, :, a, :], left[:, :, 0, :], wr, ALU.mult)
                c.wait()
                v.wait_ge(pool, a)
                v.tensor_tensor(left[:, :, a, :], left[:, :, a, :], ssm_x[:, a % 2], ALU.add).then_inc(left_done, 1)
            v.wait_ge(left_done, NA)
            with v.Fori(0, D // HG // 2) as i:
                for p in range(2):
                    v.wait_ge(multiplied, i * 2 + p + 3)
                    v.tensor_copy(prod[:, ds(i * 2 * HG + p * HG, HG), :], product[0:CA, p]).then_inc(stored, 1)
            for n, (j, g) in enumerate(turns):
                if n % 2 == 0:
                    v.wait_ge(turned, n + 1)
                    v.tensor_copy(row_out(j, g), row_in(n, j)).then_inc(kept_even, 1)

        @block.tensor
        def _(pe):
            pe.sem_inc(multiplied, 2)
            pe.wait_ge(ident_ready, 16)
            pe.wait_ge(w_loaded, 16)

            def turn_text(b):
                pe.wait_ge(masked_ok, b + 1)
                if b >= 2:
                    pe.wait_ge(copied, b - 1)
                for k in range(KT):
                    mm = pe.transpose(turn_ps[:, b % 2, k * TXT_ROWS:(k + 1) * TXT_ROWS],
                                      emb[:, b % SLOTS, 128 * k:128 * k + 128], ident[0:TXT_ROWS, 0:TXT_ROWS])
                mm.then_inc(t_turned, 1)

            for b in range(B):
                turn_text(b)
                pe.wait_ge(copied, b + 1)
                if b >= 2:
                    pe.wait_ge(res_ok, b - 1)
                for k in range(KT):
                    mm = pe.matmul(out_ps[0:TXT_ROWS, b % 2, 0:D], emb_t[:, b % 2, k * TXT_ROWS:(k + 1) * TXT_ROWS], txt_w[:, k, :],
                                   start=(k == 0), stop=(k == KT - 1))
                mm.then_inc(t_mult, 1)
            with pe.Fori(0, D // HG // 2) as i:
                for p in range(2):
                    pe.wait_ge(staged, i * 2 + p + 1)
                    pe.wait_ge(stored, i * 2 + p + 1)
                    for k in range(HG):
                        mm = pe.matmul(product[0:CA, p, k, :], left_h[:, p, k, :],
                                       z_low[:, :, ds(i * 2 * HG + p * HG + k, 1)].rearrange("p b o -> p (b o)"),
                                       start=True, stop=True)
                    mm.then_inc(multiplied, 1)
            pe.wait_ge(stored, D // HG + 2)
            for n, (j, g) in enumerate(turns):
                if n >= 2:
                    pe.wait_ge(kept_odd if n % 2 else kept_even, n // 2)
                w = rows_of(j)
                for k in range(8):
                    mm = pe.transpose(rows_ps[0:w, n % 2, k, :], prod[:, j * CHUNK:j * CHUNK + w, 8 * g + k],
                                      ident[0:CA, 0:CA])
                mm.then_inc(turned, 1)

        @block.gpsimd
        def _(g):
            def gather(b):
                for k in range(NBAND):
                    g.indirect_dma_start(
                        emb[:, b % SLOTS, col[k]:col[k + 1]], None, io[f"E{k}"],
                        bass.IndirectOffsetOnAxis(ap=row[:, k, b:b + 1].bitcast(U32), axis=0)).then_inc(gathered[b % SLOTS], 16)

            g.wait_ge(rows_known, 1)
            for b in range(SLOTS):
                gather(b)
            for b in range(B):
                g.wait_ge(gathered[b % SLOTS], (b // SLOTS + 1) * NBAND * 16)
                for k in range(NBAND):
                    band = emb[:, b % SLOTS, col[k]:col[k + 1]]
                    ins = g.tensor_tensor(band, band, inside[:, k, b:b + 1].broadcast_to([TXT_ROWS, col[k + 1] - col[k]]), ALU.mult)
                ins.then_inc(masked_ok, 1)
                if b + SLOTS < B:
                    g.wait_ge(t_turned, b + 1)
                    gather(b + SLOTS)
            for a in range(1, NA):
                g.wait_ge(left_done, 1 if a < 3 else a - 1)
                wi = w_hi[:, 1, a:a + 1, :].broadcast_to([128, B, D])
                g.tensor_tensor(ssm_x[:, a % 2], ct_im[:], wi, ALU.mult).then_inc(pool, 1)


def row_stats(c, src, stats, mv, n=NT):
    v = c.eng
    with v.Fori(0, n) as t:
        v.bn_stats(stats[:, ds(t, 1), :].rearrange("p o s -> p (o s)"),
                   src[:, ds(t, 1), :].rearrange("p o d -> p (o d)")).then_inc(c.sem, 1)
    c.n += n
    c.wait()
    moments(c, stats, mv)


def moments(c, stats, mv):
    v = c.eng
    mean, var = mv[:, :, 0], mv[:, :, 1]
    c.step(v.tensor_tensor(mean, stats[:, :, 1], stats[:, :, 4], ALU.add))
    c.step(v.tensor_tensor(var, stats[:, :, 1], stats[:, :, 4], ALU.subtract))
    c.step(v.tensor_tensor(stats[:, :, 0], stats[:, :, 2], stats[:, :, 5], ALU.add))
    c.wait()
    c.step(v.tensor_scalar(mean, mean, 0.5, None, ALU.mult))
    c.step(v.tensor_tensor(stats[:, :, 3], var, var, ALU.mult))
    c.step(v.tensor_scalar(stats[:, :, 0], stats[:, :, 0], 1 / D, None, ALU.mult))
    c.wait()
    c.step(v.scalar_tensor_tensor(var, stats[:, :, 3], 0.25, stats[:, :, 0], ALU.mult, ALU.add))
    c.wait()


def inverse_root(c, var_eps, root, inv, spare):
    v = c.eng
    c.step(v.reciprocal(inv, root))
    c.wait()
    c.step(v.tensor_tensor(spare, inv, inv, ALU.mult))
    c.wait()
    c.step(v.tensor_tensor(spare, spare, var_eps, ALU.mult))
    c.wait()
    c.step(v.tensor_scalar(spare, spare, -0.5, 1.5, ALU.mult, ALU.add))
    c.wait()
    c.step(v.tensor_tensor(inv, inv, spare, ALU.mult))
    c.wait()


def normalise(nc, name, src, dst_t, ident, ident_ready, known_stats=None):
    with ExitStack() as ctx:
        def sb(what, shape, dt=F32):
            return ctx.enter_context(nc.sbuf_tensor(f"{name}_{what}", shape, dt))

        def sem(what):
            return ctx.enter_context(nc.semaphore(f"{name}_{what}"))

        U = 4
        stats = sb("stats", [CHUNK, NT, 6])
        mv = sb("mv", [CHUNK, NT, 2])
        small = sb("small", [CHUNK, 4, NT])
        rows = sb("rows", [CHUNK, U, D])
        ps = ctx.enter_context(nc.psum_tensor(f"{name}_ps", [128, U, 512], F32))
        dve, var_ready, root_done = sem("dve"), sem("var_ready"), sem("root_done")
        rows_ok, turned, copied = sem("rows_ok"), sem("turned"), sem("copied")
        block = ctx.enter_context(nc.Block())

        @block.vector
        def _(v):
            c = Chain(v, dve)
            if known_stats is None:
                row_stats(c, src, stats, mv)
            else:
                moments(c, known_stats, mv)
            v.tensor_scalar(small[:, 0, :], mv[:, :, 1], LN_EPS, None, ALU.add).then_inc(var_ready, 1)
            v.wait_ge(root_done, 1)
            inverse_root(c, small[:, 0, :], small[:, 1, :], small[:, 2, :], small[:, 3, :])
            with v.Fori(0, NT // U) as i:
                for p in range(U):
                    t = i * U + p
                    v.wait_ge(turned, t + 1)
                    v.tensor_scalar(rows[:, p, :], src[:, ds(t, 1), :].rearrange("p o d -> p (o d)"),
                                    mv[:, ds(t, 1), 0], small[:, 2, ds(t, 1)],
                                    ALU.subtract, ALU.mult).then_inc(rows_ok, 1)

        @block.scalar
        def _(act):
            act.wait_ge(var_ready, 1)
            nc.scalar.sqrt(small[:, 1, :], small[:, 0, :]).then_inc(root_done, 1)
            act.sem_inc(copied, U)
            with act.Fori(0, NT // U) as i:
                for p in range(U):
                    t = i * U + p
                    act.wait_ge(turned, t + 1 + U)
                    nc.scalar.copy(dst_t[:, :, ds(t * CHUNK, CHUNK)],
                                   ps[:, p, 0:KC * CHUNK].rearrange("p (k t) -> p k t", k=KC)).then_inc(copied, 1)

        @block.tensor
        def _(pe):
            pe.wait_ge(ident_ready, 16)
            pe.sem_inc(turned, U)
            with pe.Fori(0, NT // U) as i:
                for p in range(U):
                    t = i * U + p
                    pe.wait_ge(rows_ok, t + 1)
                    pe.wait_ge(copied, t + 1)
                    for k in range(KC):
                        mm = pe.transpose(ps[:, p, k * CHUNK:(k + 1) * CHUNK], rows[:, p, 128 * k:128 * k + 128],
                                          ident[0:CHUNK, 0:CHUNK])
                    mm.then_inc(turned, 1)


def linear_attention(nc, io, h, h_stats, x_t, to_zero, ident, ident_ready):
    with ExitStack() as ctx:
        def sb(name, shape, dt=F32):
            return ctx.enter_context(nc.sbuf_tensor("la_" + name, shape, dt))

        sem = ctx.enter_context(cleared_semaphores(nc, "la_"))

        qv = sb("qv", [CHUNK, NT, 2 * D])
        k_t = sb("k_t", [128, KC, B, S])
        out = sb("out", [CHUNK, NT, D])
        w_qv = sb("w_qv", [128, KC, 2 * D])
        w_k = sb("w_k", [128, KC, D])
        w_o = sb("w_o", [128, KC, D])
        b_qv = sb("b_qv", [CHUNK, 2 * D])
        b_o = sb("b_o", [CHUNK, D])
        cols = sb("cols", [128, 3, KC])
        head_mask = sb("head_mask", [128, 128])
        x_s = sb("x_s", [128, 2, KC, CHUNK])
        k_max = sb("k_max", [128, KC, B])
        k_sum = sb("k_sum", [128, KC, B])
        k_inv = sb("k_inv", [128, KC, B])
        k_exp = sb("k_exp", [128, 2, S])
        k_rows = sb("k_rows", [CHUNK, 2, NCH, 128])
        q_rows = sb("q_rows", [CHUNK, 2, NCH, 128])
        q_t = sb("q_t", [128, 2, NCH, CHUNK])
        state = sb("state", [128, 2, 128])
        q_red = sb("q_red", [CHUNK, NT, HEADS])
        q_inv = sb("q_inv", [CHUNK, NT, HEADS])
        stats = sb("stats", [CHUNK, NT, 6])
        mv = sb("mv", [CHUNK, NT, 2])
        small = sb("small", [CHUNK, 4, NT])
        loaded, dve, x_copied, projected = sem("loaded"), sem("dve"), sem("x_copied"), sem("projected")
        qv_ok, k_mult, k_ok, k_max_ok = sem("qv_ok"), sem("k_mult"), sem("k_ok"), sem("k_max_ok")
        q_sub, q_exp, k_exp_ok, k_turned = sem("q_sub"), sem("q_exp"), sem("k_exp_ok"), sem("k_turned")
        k_rows_ok, q_rows_ok, q_turned, q_t_ok = sem("k_rows_ok"), sem("q_rows_ok"), sem("q_turned"), sem("q_t_ok")
        state_mult, state_ok, out_mult, out_ok = sem("state_mult"), sem("state_ok"), sem("out_mult"), sem("out_ok")
        var_ready, root_done, n_ok, n_turned = sem("var_ready"), sem("root_done"), sem("n_ok"), sem("n_turned")
        n_t_ok, o_mult, h_ok, bias_added = sem("n_t_ok"), sem("o_mult"), sem("h_ok"), sem("bias_added")
        k_inv_ok, zero_ok, zeroed = sem("k_inv_ok"), sem("zero_ok"), sem("zeroed")
        k_red, stats_ok = sem("k_red"), sem("stats_ok")
        zeros = sb("zeros", [128, D])
        ps = ctx.enter_context(nc.psum_tensor("la_ps", [128, 8, 512], F32))
        block = ctx.enter_context(nc.Block())
        QV_BANKS = (0, 1, 4, 5)
        NQ = 3
        TQ = NT // NQ

        def heads(ap):
            return ap.rearrange("p t (g e) -> p t g e", e=DH)

        def q_part(n):
            return heads(qv[:, TQ * n:TQ * n + TQ, 0:D])

        @block.sync
        def _(sp):
            sp.dma_start(w_qv[:], io["la_w_qv"]).then_inc(loaded, 16)
            sp.dma_start(w_k[:], io["la_w_k"]).then_inc(loaded, 16)
            sp.dma_start(w_o[:], io["la_w_o"]).then_inc(loaded, 16)
            sp.dma_start(b_qv[:], io["la_b_qv"].broadcast_to([CHUNK, 2 * D])).then_inc(loaded, 16)
            sp.dma_start(b_o[:], io["la_b_o"].broadcast_to([CHUNK, D])).then_inc(loaded, 16)
            sp.dma_start(cols[:], io["la_cols"]).then_inc(loaded, 16)
            sp.dma_start(head_mask[:], io["head_mask"]).then_inc(loaded, 16)
            sp.wait_ge(zero_ok, 1)
            for ap in to_zero:
                sp.dma_start(ap.rearrange("(p n) d -> p n d", p=128),
                             zeros[:].unsqueeze(1).broadcast_to([128, ap.shape[0] // 128, D])).then_inc(zeroed, 16)
            sp.wait_ge(zeroed, 16 * len(to_zero))

        @block.gpsimd
        def _(g):
            g.memset(zeros[:], 0.0).then_inc(zero_ok, 1)
            with g.Fori(0, NT // 2) as i:
                for p in range(2):
                    t = i * 2 + p
                    g.wait_ge(projected, t + 1)
                    g.tensor_copy(x_s[:, p], x_t[:, :, ds(t * CHUNK, CHUNK)]).then_inc(x_copied, 1)
            g.wait_ge(loaded, 16 * 7)
            g.tensor_tensor(h[:], h[:], b_o[:].unsqueeze(1).broadcast_to([CHUNK, NT, D]), ALU.add).then_inc(bias_added, 1)

        @block.tensor
        def _(pe):
            for s in (projected, k_turned, state_mult, q_turned, out_mult, n_turned, o_mult):
                pe.sem_inc(s, 2)
            pe.wait_ge(loaded, 16 * 7)
            pe.wait_ge(ident_ready, 16)
            with pe.Fori(0, NT // 4) as i:
                for p in range(4):
                    t = i * 4 + p
                    pe.wait_ge(x_copied, t + 1)
                    pe.wait_ge(qv_ok, t + 1)
                    for k in range(KC):
                        mm = pe.matmul(ps[0:CHUNK, QV_BANKS[p], :], x_s[:, p % 2, k, :], w_qv[:, k, :], start=(k == 0), stop=(k == KC - 1))
                    mm.then_inc(projected, 1)
            with pe.Fori(0, B) as b:
                for m in range(KC):
                    pe.wait_ge(k_ok, b * KC + m + 1)
                    for k in range(KC):
                        mm = pe.matmul(ps[:, 2 + m, 0:S], w_k[:, k, 128 * m:128 * m + 128],
                                       x_t[:, k, ds(b * S, S)], start=(k == 0), stop=(k == KC - 1))
                    mm.then_inc(k_mult, 1)
            pe.wait_ge(qv_ok, NT + 4)
            pe.wait_ge(k_ok, B * KC + 2)
            def turn_parts(b):
                for m in range(KC):
                    pe.wait_ge(k_exp_ok, b * KC + m + 1)
                    pe.wait_ge(k_rows_ok, b * KC + m + 1)
                    for j in range(NCH):
                        mm = pe.transpose(ps[0:CHUNK, m, 128 * j:128 * j + 128], k_exp[:, m, j * CHUNK:(j + 1) * CHUNK],
                                          ident[:])
                    mm.then_inc(k_turned, 1)
                for m in range(KC):
                    pe.wait_ge(q_rows_ok, b * KC + m + 1)
                    pe.wait_ge(q_t_ok, b * KC + m + 1)
                    for j in range(NCH):
                        mm = pe.transpose(ps[:, 2 + m, CHUNK * j:CHUNK * (j + 1)], q_rows[:, m, j, :],
                                          ident[0:CHUNK, 0:CHUNK])
                    mm.then_inc(q_turned, 1)

            def state_and_output(b):
                for m in range(KC):
                    pe.wait_ge(k_rows_ok, b * KC + m + 3)
                    pe.wait_ge(state_ok, b * KC + m + 1)
                    for j in range(NCH):
                        mm = pe.matmul(ps[:, 4 + m, 0:128], k_rows[:, m, j, :],
                                       qv[:, ds(b * NCH + j, 1), D + 128 * m:D + 128 * m + 128].rearrange("p o d -> p (o d)"),
                                       start=(j == 0), stop=(j == NCH - 1))
                    mm.then_inc(state_mult, 1)
                for m in range(KC):
                    pe.wait_ge(state_ok, b * KC + m + 3)
                    pe.wait_ge(q_t_ok, b * KC + m + 3)
                    pe.wait_ge(out_ok, b * KC + m + 1)
                    for j in range(NCH):
                        mm = pe.matmul(ps[0:CHUNK, 6 + m, 128 * j:128 * j + 128], q_t[:, m, j, :], state[:, m, :],
                                       start=True, stop=True)
                    mm.then_inc(out_mult, 1)

            turn_parts(0)
            with pe.Fori(0, B - 1) as b:
                turn_parts(b + 1)
                state_and_output(b)
            state_and_output(B - 1)
            def turn_pair(i):
                for p in range(2):
                    t = i * 2 + p
                    pe.wait_ge(n_ok, t + 1)
                    pe.wait_ge(n_t_ok, t + 1)
                    for k in range(KC):
                        mm = pe.transpose(ps[:, p, k * CHUNK:(k + 1) * CHUNK], q_rows[:, p, k, :],
                                          ident[0:CHUNK, 0:CHUNK])
                    mm.then_inc(n_turned, 1)

            def project_pair(i):
                for p in range(2):
                    t = i * 2 + p
                    pe.wait_ge(n_t_ok, t + 3)
                    pe.wait_ge(h_ok, t + 1)
                    for k in range(KC):
                        mm = pe.matmul(ps[0:CHUNK, 2 + p, 0:D], x_s[:, p, k, :], w_o[:, k, :],
                                       start=(k == 0), stop=(k == KC - 1))
                    mm.then_inc(o_mult, 1)

            turn_pair(0)
            with pe.Fori(0, NT // 2 - 1) as i:
                project_pair(i)
                turn_pair(i + 1)
            project_pair(NT // 2 - 1)

        @block.scalar
        def _(act):
            for s in (k_ok, q_t_ok, out_ok, n_t_ok):
                act.sem_inc(s, 2)
            act.wait_ge(loaded, 16 * 7)
            for n in range(NQ):
                act.wait_ge(q_sub, n + 1)
                nc.scalar.activation(q_part(n), q_part(n), ACT.Exp).then_inc(q_exp, 1)
            with act.Fori(0, B) as b:
                for m in range(KC):
                    act.wait_ge(k_mult, b * KC + m + 1)
                    nc.scalar.activation(k_t[:, m, ds(b, 1), :].rearrange("p o s -> p (o s)"), ps[:, 2 + m, 0:S],
                                         ACT.Identity, bias=cols[:, 0, m:m + 1]).then_inc(k_ok, 1)
            act.wait_ge(k_max_ok, 1)
            def exp_k(b):
                for m in range(KC):
                    act.wait_ge(k_turned, b * KC + m + 1)
                    nc.scalar.activation(k_exp[:, m, :], k_t[:, m, ds(b, 1), :].rearrange("p o s -> p (o s)"),
                                         ACT.Exp, bias=k_max[:, m, ds(b, 1)],
                                         accum_out=k_sum[:, m, ds(b, 1)]).then_inc(k_exp_ok, 1)

            def keep_q(b):
                for m in range(KC):
                    act.wait_ge(q_turned, b * KC + m + 3)
                    act.wait_ge(out_mult, b * KC + m + 1)
                    nc.scalar.copy(q_t[:, m].rearrange("p j t -> p (j t)"), ps[:, 2 + m, 0:S]).then_inc(q_t_ok, 1)

            def keep_out(b):
                for m in range(KC):
                    act.wait_ge(out_mult, b * KC + m + 3)
                    nc.scalar.copy(out[:, ds(b * NCH, NCH), 128 * m:128 * m + 128],
                                   ps[0:CHUNK, 6 + m, 0:NCH * 128].rearrange("p (j e) -> p j e", j=NCH)).then_inc(out_ok, 1)

            exp_k(0)
            keep_q(0)
            with act.Fori(0, B - 1) as b:
                exp_k(b + 1)
                keep_out(b)
                keep_q(b + 1)
            keep_out(B - 1)
            act.wait_ge(var_ready, 1)
            nc.scalar.sqrt(small[:, 1, :], small[:, 0, :]).then_inc(root_done, 1)
            with act.Fori(0, NT // 2) as i:
                for p in range(2):
                    t = i * 2 + p
                    act.wait_ge(n_turned, t + 3)
                    act.wait_ge(o_mult, t + 1)
                    for k in range(KC):
                        ins = nc.scalar.activation(x_s[:, p, k, :], ps[:, p, k * CHUNK:(k + 1) * CHUNK], ACT.Identity,
                                                   bias=cols[:, 2, k:k + 1], scale=cols[:, 1, k:k + 1])
                    ins.then_inc(n_t_ok, 1)

        @block.vector
        def _(v):
            c = Chain(v, dve)
            for s, n in ((qv_ok, 4), (k_rows_ok, 2), (state_ok, 2), (h_ok, 2)):
                v.sem_inc(s, n)
            v.wait_ge(loaded, 16 * 7)
            for n in range(NQ):
                with v.Fori(TQ // 4 * n, TQ // 4 * (n + 1)) as i:
                    for p in range(4):
                        t = i * 4 + p
                        v.wait_ge(projected, t + 3)
                        v.tensor_tensor(qv[:, ds(t, 1), :].rearrange("p o d -> p (o d)"), ps[0:CHUNK, QV_BANKS[p], :], b_qv[:],
                                        ALU.add).then_inc(qv_ok, 1)
                v.wait_ge(qv_ok, TQ * (n + 1) + 4)
                red = q_red[:, TQ * n:TQ * n + TQ, :]
                c.step(v.tensor_reduce(red, q_part(n), AX.X, ALU.max))
                c.wait()
                v.tensor_tensor(q_part(n), q_part(n), red.unsqueeze(3).broadcast_to([CHUNK, TQ, HEADS, DH]),
                                ALU.subtract).then_inc(q_sub, 1)
            for n in range(NQ):
                v.wait_ge(q_exp, n + 1)
                c.step(v.tensor_reduce(q_red[:, TQ * n:TQ * n + TQ, :], q_part(n), AX.X, ALU.add))
            c.wait()
            c.step(v.reciprocal(q_inv[:], q_red[:]))
            c.wait()
            with v.Fori(0, B) as b:
                v.wait_ge(k_ok, b * KC + KC + 2)
                v.tensor_reduce(k_max[:, :, ds(b, 1)], k_t[:, :, ds(b, 1), :], AX.X, ALU.max).then_inc(k_red, 1)
            v.wait_ge(k_red, B)
            v.tensor_scalar(k_max[:], k_max[:], -1.0, None, ALU.mult).then_inc(k_max_ok, 1)
            def place_q(b):
                for m in range(KC):
                    v.wait_ge(q_turned, b * KC + m + 1)
                    v.tensor_tensor(q_rows[:, m].rearrange("p j (g e) -> p j g e", e=DH),
                                    heads(qv[:, ds(b * NCH, NCH), 128 * m:128 * m + 128]),
                                    q_inv[:, ds(b * NCH, NCH), 8 * m:8 * m + 8].unsqueeze(3).broadcast_to([CHUNK, NCH, 8, DH]),
                                    ALU.mult).then_inc(q_rows_ok, 1)

            def place_k(b):
                for m in range(KC):
                    v.wait_ge(k_turned, b * KC + m + 3)
                    v.wait_ge(state_mult, b * KC + m + 1)
                    v.tensor_copy(k_rows[:, m].rearrange("p j e -> p (j e)"), ps[0:CHUNK, m, 0:NCH * 128]).then_inc(k_rows_ok, 1)
                    v.wait_ge(k_exp_ok, b * KC + m + 1)
                    v.reciprocal(k_inv[:, m, ds(b, 1)], k_sum[:, m, ds(b, 1)]).then_inc(k_inv_ok, 1)

            def place_state(b):
                for m in range(KC):
                    v.wait_ge(state_mult, b * KC + m + 3)
                    v.wait_ge(out_mult, b * KC + m + 1)
                    v.wait_ge(k_inv_ok, b * KC + m + 1)
                    v.scalar_tensor_tensor(state[:, m, :], ps[:, 4 + m, 0:128], k_inv[:, m, ds(b, 1)], head_mask[:],
                                           ALU.mult, ALU.mult).then_inc(state_ok, 1)

            place_q(0)
            place_k(0)
            with v.Fori(0, B - 1) as b:
                place_q(b + 1)
                place_state(b)
                place_k(b + 1)
            place_state(B - 1)
            v.wait_ge(out_ok, B * KC + 2)
            row_stats(c, out, stats, mv)
            v.tensor_scalar(small[:, 0, :], mv[:, :, 1], LN_EPS, None, ALU.add).then_inc(var_ready, 1)
            v.wait_ge(root_done, 1)
            inverse_root(c, small[:, 0, :], small[:, 1, :], small[:, 2, :], small[:, 3, :])
            v.wait_ge(bias_added, 1)
            def rows_pair(i):
                for p in range(2):
                    t = i * 2 + p
                    v.wait_ge(n_turned, t + 1)
                    v.tensor_scalar(q_rows[:, p, 0:KC, :].rearrange("p k e -> p (k e)"),
                                    out[:, ds(t, 1), :].rearrange("p o d -> p (o d)"),
                                    mv[:, ds(t, 1), 0], small[:, 2, ds(t, 1)],
                                    ALU.subtract, ALU.mult).then_inc(n_ok, 1)

            def add_pair(i):
                for p in range(2):
                    t = i * 2 + p
                    v.wait_ge(o_mult, t + 3)
                    row = h[:, ds(t, 1), :].rearrange("p o d -> p (o d)")
                    v.tensor_tensor(row, row, ps[0:CHUNK, 2 + p, 0:D], ALU.add).then_inc(h_ok, 1)

            def stats_pair(i):
                for p in range(2):
                    t = i * 2 + p
                    v.wait_ge(h_ok, t + 3)
                    v.bn_stats(h_stats[:, ds(t, 1), :].rearrange("p o s -> p (o s)"),
                               h[:, ds(t, 1), :].rearrange("p o d -> p (o d)")).then_inc(stats_ok, 1)

            rows_pair(0)
            with v.Fori(0, NT // 2 - 1) as i:
                rows_pair(i + 1)
                add_pair(i)
                stats_pair(i)
            add_pair(NT // 2 - 1)
            stats_pair(NT // 2 - 1)


EXPERTS, ROUNDS, FF = 4, 4, 1024
FT = FF // 128
NG2 = 2
GT = NT // NG2
MROWS = 128
MT = (2 * GT * CHUNK + EXPERTS * (MROWS - 1)) // MROWS
SORTED = MT * MROWS
W1N, W2N = EXPERTS * KC * FF, EXPERTS * FT * D
TW = 444
NP = T // TW // 2
TC = TW // CHUNK


def wait_if(eng, sem, count):
    if not isinstance(count, int) or count >= 1:
        eng.wait_ge(sem, count)


def recursive_mixture(nc, io, h, h_stats, x_sorted, y_sorted, h_dram, bias_dram, ident):
    with ExitStack() as ctx:
        def sb(name, shape, dt=F32):
            return ctx.enter_context(nc.sbuf_tensor("mo_" + name, shape, dt))

        sem = ctx.enter_context(cleared_semaphores(nc, "mo_"))
        PHASES = NG2 * ROUNDS
        BODIES = MT // 2
        GU = 3
        GB = GT // GU
        G_FIRST = 2
        CHOOSE, PLACE = G_FIRST + GB, G_FIRST + GB + 1
        HALF = FF // 2
        BN = FF + D

        w_hi, w_lo = sb("w_hi", [128, W1N + W2N], F32R), sb("w_lo", [128, W1N + W2N], F32R)
        bias = sb("bias", [2, EXPERTS, BN], F32R)
        ones_r = sb("ones_r", [2, MROWS], F32R)
        x = sb("x", [MROWS, 2, D])
        x_hi, x_lo = sb("x_hi", [128, 2, KC, MROWS], F32R), sb("x_lo", [128, 2, KC, MROWS], F32R)
        room = sb("room", [MROWS, 2 * HALF + 2 * D])
        g = room[:, 0:2 * HALF].rearrange("p (s f) -> p s f", s=2)
        y = room[:, 2 * HALF:].rearrange("p (s d) -> p s d", s=2)
        bias_raw = sb("bias_raw", [128, EXPERTS * BN // 128])
        bias_hi, bias_lo = (sb(name, [128, EXPERTS * BN // 128], F32R) for name in ("bias_hi", "bias_lo"))
        g_hi, g_lo = sb("g_hi", [128, 2, HALF], F32R), sb("g_lo", [128, 2, HALF], F32R)
        y_rows = sb("y_rows", [CHUNK, GU, 2, D])
        rows = y_rows[:, :, 1, :]
        x_f = sb("x_f", [128, GU, KC, CHUNK])
        w_g = sb("w_g", [128, KC, ROUNDS, EXPERTS])
        b_g = sb("b_g", [CHUNK, ROUNDS, EXPERTS])
        before = sb("before", [CHUNK, 2, EXPERTS, EXPERTS])
        early = sb("early", [CHUNK, CHUNK])
        ones = sb("ones", [CHUNK, CHUNK])
        numbers = sb("numbers", [CHUNK, MT])
        keep = sb("keep", [CHUNK, EXPERTS * GT])
        lg = sb("lg", [CHUNK, GT, EXPERTS])
        rank = sb("rank", [CHUNK, 4, GT, EXPERTS])
        cw = sb("cw", [CHUNK, GT, EXPERTS])
        total = sb("total", [CHUNK, GT])
        tables = sb("tables", [CHUNK, 3, EXPERTS * GT])
        ends = sb("ends", [CHUNK, 4, EXPERTS])
        ends_i = sb("ends_i", [CHUNK, EXPERTS], I32)
        place_f = sb("place_f", [CHUNK, 2, GT])
        place = sb("place", [CHUNK, NG2, 2, GT], I32)
        weight = sb("weight", [CHUNK, NG2, 2, GT])
        tile_expert = sb("tile_expert", [CHUNK, 1 + NG2 * MT], I32)
        mv = sb("mv", [CHUNK, NT, 2])
        small = sb("small", [CHUNK, 4, NT])
        cmp = y_rows[:, 0:2].rearrange("p a b d -> p a (b d)")[:, :, 0:GT * EXPERTS * EXPERTS].rearrange(
            "p a (t e f) -> p a t e f", e=EXPERTS, f=EXPERTS)
        tile_cmp = y_rows[:, 0, 0, 0:MT * EXPERTS].rearrange("p (g e) -> p g e", e=EXPERTS)
        ps = ctx.enter_context(nc.psum_tensor("mo_ps", [128, 8, 512], F32))
        HID, TURN, XT, Y, GA, GL = 0, 2, 4, 5, 6, 7

        loaded, w_loaded, h_stored, bias_loaded = sem("loaded"), [sem(f"w_loaded{n}") for n in range(4)], [sem("h_stored0"), sem("h_stored1")], sem("bias_loaded")
        ones_ok, dve, var_ready, root_done = sem("ones_ok"), sem("dve"), sem("var_ready"), sem("root_done")
        bias_split, bias_stored, kept_loaded, bias_ok, w_hi_ok, w_lo_ok = sem("bias_split"), sem("bias_stored"), [sem("kept_loaded0"), sem("kept_loaded1")], sem("bias_ok"), sem("w_hi_ok"), sem("w_lo_ok")
        half_added, row_ok, gate_turned, x_f_ok, h_ok, gate_mult = (sem("half_added"), sem("row_ok"), sem("gate_turned"),
                                                                    sem("x_f_ok"), sem("h_ok"), sem("gate_mult"))
        gate_dve, arg_ok, tanh_ok, hot_ok, counted, place_ok = (sem("gate_dve"), sem("arg_ok"), sem("tanh_ok"), sem("hot_ok"),
                                                                sem("counted"), sem("place_ok"))
        kept_added, stats_ok, last_gathered = sem("kept_added"), sem("stats_ok"), [sem(f"last_gathered{n}") for n in range(GB)]
        pool_step, weigh_dve, weight_ok = sem("pool_step"), sem("weigh_dve"), sem("weight_ok")
        scattered, gathered = sem("scattered"), [sem(f"gathered{j}") for j in range(GU)]
        x_loaded = [sem("x_loaded0"), sem("x_loaded1")]
        y_stored = [sem("y_stored0"), sem("y_stored1")]
        x_turned, x_hi_ok, x_lo_ok, hid_mult, gelu_ok = sem("x_turned"), sem("x_hi_ok"), sem("x_lo_ok"), sem("hid_mult"), sem("gelu_ok")
        g_turned, hi_ok, lo_ok, y_mult, y_ok = sem("g_turned"), sem("hi_ok"), sem("lo_ok"), sem("y_mult"), sem("y_ok")
        block = ctx.enter_context(nc.Block())
        w1 = [w[:, 0:W1N].rearrange("p (e k f) -> p e k f", e=EXPERTS, k=KC) for w in (w_hi, w_lo)]
        w2 = [w[:, W1N:].rearrange("p (e f d) -> p e f d", e=EXPERTS, f=FT) for w in (w_hi, w_lo)]
        WQ = (W1N + W2N) // 4

        last_rows = w_lo[0:CHUNK, 0:GT * 2 * D].bitcast(F32).rearrange("p (t k d) -> p t k d", k=2, d=D)

        def kept(grp):
            return w_hi[0:CHUNK, grp * GT * D:(grp + 1) * GT * D].bitcast(F32).rearrange("p (t d) -> p t d", d=D)



        def gate_slot(j):
            return ps[:, (GA, GL)[j % 2], 0:KC * CHUNK]

        LG_AT, COUNT_AT, SUM_AT = 256, 256 + EXPERTS * GT, 256 + 2 * EXPERTS * GT

        def row_of(grp, t):
            return h[:, ds(grp * GT + t, 1), :].rearrange("p o d -> p (o d)")

        def bodies(eng, body, ph, grp, rnd):
            if isinstance(ph, int) and ph == 0:
                for i in range(G_FIRST):
                    body(ph, grp, i, None)
            else:
                with eng.Fori(0, G_FIRST) as i:
                    body(ph, grp, i, None)
            with eng.Fori(0, GB) as b:
                body(ph, grp, b + G_FIRST, ("rows", b, rnd))
            body(ph, grp, CHOOSE, ("choose", None, rnd) if rnd is not None else None)
            body(ph, grp, PLACE, ("place", None, rnd) if rnd is not None else None)
            last = isinstance(ph, int) and ph == PHASES - 1
            with eng.Fori(PLACE + 1, BODIES - last) as i:
                body(ph, grp, i, None)
            if last:
                body(ph, grp, BODIES - 1, None)

        def all_phases(eng, body):
            bodies(eng, body, 0, 0, 0)
            with eng.Fori(0, ROUNDS - 1) as r:
                bodies(eng, body, r * 2 + 1, 1, r + 1)
                bodies(eng, body, r * 2 + 2, 0, r + 1)
            bodies(eng, body, PHASES - 1, 1, None)

        @block.sync
        def _(sp):
            for dst, name in ((w_g, "mo_w_g"), (b_g, "mo_b_g"), (before, "before"), (early, "early"), (numbers, "mo_numbers"),
                              (keep, "mo_keep")):
                src = io[name]
                if src.shape[0] == 1:
                    src = src.broadcast_to([CHUNK] + list(src.shape[1:]))
                sp.dma_start(dst[:], src).then_inc(loaded, 16)
            sp.dma_start(bias_raw[:], io["mo_b"]).then_inc(bias_loaded, 16)
            for grp in range(NG2):
                part = slice(grp * GT, (grp + 1) * GT)
                sp.dma_start(h_dram[:, part, :], h[:, part, :]).then_inc(h_stored[grp], 16)
            for n in range(4):
                sp.dma_start(w_lo[:, WQ * n:WQ * n + WQ].bitcast(F32), io["mo_w"][:, WQ * n:WQ * n + WQ]).then_inc(w_loaded[n], 16)
            for n, part in enumerate((bias_hi, bias_lo)):
                sp.wait_ge(bias_split, n + 1)
                sp.dma_start(bias_dram[n].rearrange("(p n) -> p n", p=128), part[:].bitcast(F32)).then_inc(bias_stored, 16)
            sp.wait_ge(bias_stored, 32)
            sp.dma_start(bias[:].bitcast(F32).rearrange("o e n -> o (e n)"), bias_dram).then_inc(bias_ok, 16)

            def tile(halves, grp, n):
                if isinstance(n, int) and not 0 <= n < MT:
                    grp, n = 1 - grp, n % MT
                return halves[grp][ds(n * MROWS, MROWS), :]

            def load(s, q, grp, n):
                sp.wait_ge(x_turned, q + 1)
                sp.dma_start(x[:, s, :], tile(x_sorted, grp, n)).then_inc(x_loaded[s], 16)

            def store(s, q, grp, n):
                sp.wait_ge(y_ok, q + 3)
                sp.dma_start(tile(y_sorted, grp, n), y[:, s, :]).then_inc(y_stored[s], 16)

            def tiles(ph, grp, i):
                for s in range(2):
                    q, n = (ph * BODIES + i) * 2 + s, i * 2 + s
                    if isinstance(i, int) and i == BODIES - 1 and s == 0 and not (isinstance(ph, int) and ph == PHASES - 1):
                        sp.wait_ge(scattered, (ph + 2) * 16 * 2 * GT)
                    if not (isinstance(q, int) and q + 2 >= PHASES * MT):
                        load(s, q + 2, grp, n + 2)
                    if not (isinstance(q, int) and q == 0):
                        store(1 - s, q - 1, grp, n - 1)

            def phase(ph, grp):
                tiles(ph, grp, 0)
                with sp.Fori(1, BODIES - 1) as i:
                    tiles(ph, grp, i)
                tiles(ph, grp, BODIES - 1)

            sp.wait_ge(scattered, 16 * 2 * GT)
            load(0, 0, 0, 0)
            load(1, 1, 0, 1)
            phase(0, 0)
            with sp.Fori(0, ROUNDS - 1) as r:
                phase(r * 2 + 1, 1)
                phase(r * 2 + 2, 0)
            phase(PHASES - 1, 1)
            store(1, PHASES * MT - 1, 1, MT - 1)
            for grp in range(NG2):
                sp.dma_start(kept(grp), h_dram[:, grp * GT:(grp + 1) * GT, :]).then_inc(kept_loaded[grp], 16)

        @block.gpsimd
        def _(gp):
            def arrived(*waits):
                for s, n in waits:
                    gp.wait_ge(s, n)
                gp.sem_inc(pool_step, 1)

            def scatter(ex, grp):
                arrived((place_ok, ex + 1), (h_ok, ex * GT + GT + GU))
                for t in range(GT):
                    for k in range(2):
                        gp.indirect_dma_start(x_sorted[grp], bass.IndirectOffsetOnAxis(ap=place[:, grp, k, t:t + 1].bitcast(U32), axis=0),
                                              h[:, grp * GT + t, :], None).then_inc(scattered, 16)

            def gather(ex, grp, to_rows=True):
                arrived(*((stored, (ex - 1) * 16 * BODIES) for stored in y_stored))
                for t in range(GT):
                    n = ex * GT + t
                    if to_rows or t < GU:
                        arrived((gate_turned, n + 1), (h_ok, n + 1))
                    else:
                        arrived((row_ok, n - GU + 1))
                    for k in range(2):
                        gp.indirect_dma_start(y_rows[:, t % GU, k, :], None, y_sorted[grp],
                                              bass.IndirectOffsetOnAxis(ap=place[:, grp, k, t:t + 1].bitcast(U32), axis=0)
                                              ).then_inc(gathered[t % GU], 16)

            scatter(0, 0)
            scatter(1, 1)
            with gp.Fori(0, ROUNDS - 1) as r:
                gather(r * 2 + 2, 0)
                scatter(r * 2 + 2, 0)
                gather(r * 2 + 3, 1)
                scatter(r * 2 + 3, 1)
            gather(PHASES, 0, False)
            arrived(*((stored, PHASES * 16 * BODIES) for stored in y_stored))
            for t in range(GT):
                for k in range(2):
                    gp.indirect_dma_start(last_rows[:, t, k, :], None, y_sorted[1],
                                          bass.IndirectOffsetOnAxis(ap=place[:, 1, k, t:t + 1].bitcast(U32), axis=0)
                                          ).then_inc(last_gathered[t // GU], 16)

        @block.tensor
        def _(pe):
            for s, n in ((x_turned, 2), (hid_mult, 4), (g_turned, 2), (y_mult, 2), (gate_turned, GU), (gate_mult, GU)):
                pe.sem_inc(s, n)
            pe.wait_ge(loaded, 16 * 6)

            def turn_rows(ex, b, js):
                for j in js:
                    t = ex * GT + b * GU + j
                    pe.wait_ge(row_ok, t + 1)
                    pe.wait_ge(x_f_ok, t + GU if j == 0 else t + GU - 1)
                    for k in range(KC):
                        mm = pe.transpose(gate_slot(j)[:, k * CHUNK:(k + 1) * CHUNK], rows[:, j, 128 * k:128 * k + 128],
                                          ident[0:CHUNK, 0:CHUNK])
                    mm.then_inc(gate_turned, 1)

            def logits(ex, b, rnd):
                for j in range(GU):
                    pe.wait_ge(x_f_ok, ex * GT + b * GU + 2 * GU)
                    for k in range(KC):
                        mm = pe.matmul(ps[0:CHUNK, GL, ds((b * GU + j) * EXPERTS + LG_AT, EXPERTS)], x_f[:, j, k, :],
                                       w_g[:, k, ds(rnd, 1), :].rearrange("p o e -> p (o e)"), start=(k == 0), stop=(k == KC - 1))
                    mm.then_inc(gate_mult, 1)

            def count(ex):
                pe.wait_ge(hot_ok, ex + 1)
                chosen = rank[:, 1].rearrange("p t e -> p (t e)")
                pe.matmul(ps[0:CHUNK, GL, COUNT_AT:COUNT_AT + EXPERTS * GT], early[:], chosen, start=True, stop=True)
                pe.matmul(ps[0:CHUNK, GL, SUM_AT:SUM_AT + EXPERTS * GT], ones[:], chosen, start=True, stop=True).then_inc(counted, 1)

            def turn_x(s, q, loads):
                pe.wait_ge(x_loaded[s], loads * 16)
                pe.wait_ge(x_lo_ok, q + 2)
                for k in range(KC):
                    mm = pe.transpose(ps[:, XT, 256 * s + MROWS * k:256 * s + MROWS * k + MROWS], x[:, s, 128 * k:128 * k + 128], ident[:])
                mm.then_inc(x_turned, 1)

            def expert(n):
                return pe.value_load(tile_expert[0:1, ds(n, 1)], min_val=0, max_val=EXPERTS - 1)

            def hidden(s, hf, q, e):
                w = q * 2 + hf
                if hf == 0:
                    pe.wait_ge(x_lo_ok, q + 3)
                pe.wait_ge(gelu_ok, w + 1)
                at = HALF * hf
                pe.matmul(ps[:, HID + hf, :], ones_r[:], bias[:, ds(e, 1), at:at + HALF].rearrange("p o f -> p (o f)"),
                          start=True, stop=False)
                for a in range(KC):
                    for part, xs in ((0, x_hi), (0, x_lo), (1, x_hi)):
                        mm = pe.matmul(ps[:, HID + hf, :], xs[:, s, a, :],
                                       w1[part][:, ds(e, 1), a, at:at + HALF].rearrange("p o f -> p (o f)"),
                                       start=False, stop=(a == KC - 1 and part == 1))
                mm.then_inc(hid_mult, 1)

            def turn_g(hf, w):
                pe.wait_ge(gelu_ok, w + 3)
                pe.wait_ge(lo_ok, w + 1)
                for f in range(FT // 2):
                    mm = pe.transpose(ps[:, TURN + hf, 128 * f:128 * f + 128], g[:, hf, 128 * f:128 * f + 128], ident[:])
                mm.then_inc(g_turned, 1)

            def down(s, hf, q, e):
                pe.wait_ge(lo_ok, q * 2 + hf + 3)
                out = ps[:, Y, 256 * s:256 * s + D]
                if hf == 0:
                    pe.wait_ge(y_ok, q + 2)
                    pe.matmul(out, ones_r[:], bias[:, ds(e, 1), FF:BN].rearrange("p o d -> p (o d)"), start=True, stop=False)
                for f in range(FT // 2):
                    for part, gs in ((0, g_hi), (0, g_lo), (1, g_hi)):
                        mm = pe.matmul(out, gs[:, hf, 128 * f:128 * f + 128],
                                       w2[part][:, ds(e, 1), f + FT // 2 * hf, :].rearrange("p o d -> p (o d)"),
                                       start=False, stop=(hf == 1 and f == FT // 2 - 1 and part == 1))
                mm.then_inc(y_mult, 1)

            def body(ph, grp, i, part):
                kind, b, rnd = part or (None, None, None)
                ex = ph + 1
                gating = kind == "rows" and not (isinstance(ph, int) and ph == PHASES - 1)
                for s in range(2):
                    q = (ph * BODIES + i) * 2 + s
                    start = isinstance(q, int) and q == 0
                    end = isinstance(q, int) and q == PHASES * MT - 1
                    n = i * 2 + s + 1 + grp * MT
                    e_prev = e if s else None
                    e = expert(n)
                    hidden(s, 0, q, e)
                    if s == 0 and not start:
                        e_prev = expert(n - 1)
                    if gating and s == 1:
                        turn_rows(ex, b, (0, 1))
                    if not end:
                        turn_x(1 - s, q + 1, ph * BODIES + i + 1 + s)
                    if not start:
                        turn_g(1, q * 2 - 1)
                        down(1 - s, 0, q - 1, e_prev)
                    hidden(s, 1, q, e)
                    if gating and s == 1:
                        turn_rows(ex, b, (2,))
                    turn_g(0, q * 2)
                    if gating and s == 1:
                        logits(ex, b, rnd)
                    if kind == "choose" and s == 1:
                        count(ex)
                    if not start:
                        down(1 - s, 1, q - 1, e_prev)

            with pe.Fori(0, GB) as b:
                turn_rows(0, b, (0, 1, 2))
                logits(0, b, 0)
            count(0)
            pe.wait_ge(bias_ok, 16)
            pe.wait_ge(w_lo_ok, 4)
            pe.wait_ge(place_ok, 1)
            turn_x(0, 0, 1)
            all_phases(pe, body)
            turn_g(1, PHASES * MT * 2 - 1)
            e = expert(NG2 * MT)
            down(1, 0, PHASES * MT - 1, e)
            down(1, 1, PHASES * MT - 1, e)

        @block.scalar
        def _(act):
            for s, n in ((gelu_ok, 2), (x_f_ok, GU), (h_ok, GU)):
                act.sem_inc(s, n)
            act.wait_ge(var_ready, 1)
            nc.scalar.sqrt(small[:, 1, :], small[:, 0, :]).then_inc(root_done, 1)

            def keep_rows(ex, grp, b, js):
                for j in js:
                    t = ex * GT + b * GU + j
                    act.wait_ge(gate_turned, t + 1 + GU)
                    act.wait_ge(gate_mult, t + 1)
                    nc.scalar.copy(x_f[:, j].rearrange("p k t -> p (k t)"), gate_slot(j)).then_inc(x_f_ok, 1)
                    nc.scalar.copy(row_of(grp, b * GU + j), rows[:, j, :]).then_inc(h_ok, 1)

            def tanh(ex):
                act.wait_ge(arg_ok, ex + 1)
                nc.scalar.activation(cw[:], cw[:], ACT.Tanh).then_inc(tanh_ok, 1)

            def part_x(s, q):
                act.wait_ge(x_turned, q + 3)
                act.wait_ge(hid_mult, q * 2 + 2)
                nc.scalar.copy(x_hi[:, s].rearrange("p k t -> p (k t)"), ps[:, XT, 256 * s:256 * s + 256]).then_inc(x_hi_ok, 1)

            def gelu(hf, w):
                act.wait_ge(hid_mult, w + 1 + 4)
                act.wait_ge(g_turned, w + 1)
                nc.scalar.activation(g[:, hf, :], ps[:, HID + hf, :], ACT.Gelu_apprx_tanh).then_inc(gelu_ok, 1)

            def part_g(hf, w):
                act.wait_ge(g_turned, w + 3)
                act.wait_ge(y_mult, w + 1)
                nc.scalar.copy(g_hi[:, hf, :], ps[:, TURN + hf, :]).then_inc(hi_ok, 1)

            def body(ph, grp, i, part):
                kind, b, rnd = part or (None, None, None)
                gating = kind == "rows" and not (isinstance(ph, int) and ph == PHASES - 1)
                for s in range(2):
                    q = (ph * BODIES + i) * 2 + s
                    gelu(0, q * 2)
                    if not (isinstance(q, int) and q == PHASES * MT - 1):
                        part_x(1 - s, q + 1)
                    if gating and s == 1:
                        keep_rows(ph + 1, 1 - grp, b, (0, 1))
                    if not (isinstance(q, int) and q == 0):
                        part_g(1, q * 2 - 1)
                    gelu(1, q * 2 + 1)
                    if gating and s == 1:
                        keep_rows(ph + 1, 1 - grp, b, (2,))
                    part_g(0, q * 2)
                    if kind == "choose" and s == 1:
                        tanh(ph + 1)

            act.wait_ge(h_stored[0], 16)
            act.wait_ge(h_stored[1], 16)
            with act.Fori(0, GB) as b:
                keep_rows(0, 0, b, (0, 1, 2))
            tanh(0)
            for n in range(4):
                act.wait_ge(w_loaded[n], 16)
                nc.scalar.copy(w_hi[:, WQ * n:WQ * n + WQ], w_lo[:, WQ * n:WQ * n + WQ].bitcast(F32)).then_inc(w_hi_ok, 1)
            part_x(0, 0)
            all_phases(act, body)
            part_g(1, PHASES * MT * 2 - 1)

        @block.vector
        def _(v):
            for s, n in ((x_lo_ok, 2), (lo_ok, 2), (y_ok, 2)):
                v.sem_inc(s, n)
            v.memset(ones[:], 1.0).then_inc(ones_ok, 1)
            c = Chain(v, dve)
            moments(c, h_stats, mv)
            v.tensor_scalar(small[:, 0, :], mv[:, :, 1], LN_EPS, None, ALU.add).then_inc(var_ready, 1)
            v.wait_ge(ones_ok, 1)
            v.tensor_copy(ones_r[:], ones[0:2, 0:1].broadcast_to([2, MROWS])).then_inc(ones_ok, 1)
            v.wait_ge(root_done, 1)
            inverse_root(c, small[:, 0, :], small[:, 1, :], small[:, 2, :], small[:, 3, :])
            v.wait_ge(loaded, 16 * 6)

            def normal_rows(ex, grp, b):
                for j in range(GU):
                    t = b * GU + j
                    v.wait_ge(gate_turned, ex * GT + t + 1)
                    v.wait_ge(h_ok, ex * GT + t + 1)
                    v.tensor_scalar(rows[:, j, :], row_of(grp, t), mv[:, ds(grp * GT + t, 1), 0], small[:, 2, ds(grp * GT + t, 1)],
                                    ALU.subtract, ALU.mult).then_inc(row_ok, 1)

            def add_first(ex, grp, b):
                for j in range(GU):
                    v.wait_ge(gathered[j], ((ex - 2) * GB + b + 1) * 32)
                    v.scalar_tensor_tensor(y_rows[:, j, 0, :], y_rows[:, j, 0, :], weight[:, grp, 0, ds(b * GU + j, 1)],
                                           row_of(grp, b * GU + j), ALU.mult, ALU.add).then_inc(half_added, 1)

            def add_second(ex, grp, b, to_rows):
                for j in range(GU):
                    v.wait_ge(half_added, (ex - 2) * GT + b * GU + j + 1)
                    v.scalar_tensor_tensor(rows[:, j, :] if to_rows else row_of(grp, b * GU + j), y_rows[:, j, 1, :],
                                           weight[:, grp, 1, ds(b * GU + j, 1)], y_rows[:, j, 0, :],
                                           ALU.mult, ALU.add).then_inc(row_ok, 1)

            CHOOSE_STEPS, PLACE_STEPS = 12, 20
            STEPS = CHOOSE_STEPS + PLACE_STEPS
            by_e = [CHUNK, GT, EXPERTS]

            def choose(ex, rnd):
                c = Chain(v, gate_dve, ex * STEPS)
                by_pair = [CHUNK, GT, EXPERTS, EXPERTS]
                v.wait_ge(gate_mult, ex * GT + GT + GU)
                v.wait_ge(h_ok, ex * GT + GT + GU)
                c.step(v.tensor_tensor(lg[:], ps[0:CHUNK, GL, LG_AT:LG_AT + GT * EXPERTS].rearrange("p (t e) -> p t e", e=EXPERTS),
                                       b_g[:, ds(rnd, 1), :].broadcast_to(by_e), ALU.add))
                c.wait()
                other = lg[:].unsqueeze(2).broadcast_to(by_pair)
                own = lg[:].unsqueeze(3).broadcast_to(by_pair)
                c.step(v.tensor_tensor(cmp[:, 0], other, own, ALU.is_ge))
                c.step(v.tensor_tensor(cmp[:, 1], other, own, ALU.is_gt))
                c.wait()
                yield
                for a in range(2):
                    c.step(v.tensor_tensor(cmp[:, a], cmp[:, a], before[:, a:a + 1].broadcast_to(by_pair), ALU.mult))
                c.wait()
                c.step(v.tensor_tensor(cmp[:, 0], cmp[:, 0], cmp[:, 1], ALU.add))
                c.wait()
                c.step(v.tensor_reduce(rank[:, 0], cmp[:, 0], AX.X, ALU.add))
                c.wait()
                v.tensor_scalar(rank[:, 1], rank[:, 0], 2.0, None, ALU.is_lt).then_inc(hot_ok, 1)
                yield
                c.step(v.tensor_scalar(rank[:, 2], rank[:, 0], 0.0, None, ALU.is_equal))
                c.step(v.tensor_scalar(rank[:, 3], rank[:, 0], 1.0, None, ALU.is_equal))
                v.wait_ge(hot_ok, ex + 1)
                c.wait()
                c.step(v.tensor_tensor(rank[:, 0], rank[:, 1], lg[:], ALU.mult))
                c.wait()
                c.step(v.tensor_reduce(total[:], rank[:, 0], AX.X, ALU.add))
                c.wait()
                v.scalar_tensor_tensor(cw[:], total[:].unsqueeze(2).broadcast_to(by_e), -0.5, lg[:],
                                       ALU.mult, ALU.add).then_inc(arg_ok, 1)
                c.step(v.memset(ends[:, 3, :], 1.0))
                assert c.n == CHOOSE_STEPS, c.n
                yield

            def set_places(ex, grp):
                c = Chain(v, gate_dve, ex * STEPS + CHOOSE_STEPS)
                v.wait_ge(counted, ex + 1)
                so_far, whole, running = tables[:, 0, :], tables[:, 1, :], tables[:, 2, :]

                def e_first(ap):
                    return ap.rearrange("p (e t) -> p e t", e=EXPERTS)

                for dst, at in ((so_far, COUNT_AT), (whole, SUM_AT)):
                    c.step(v.tensor_copy(e_first(dst), ps[0:CHUNK, GL, at:at + GT * EXPERTS].rearrange("p (t e) -> p e t", e=EXPERTS)))
                c.wait()
                c.step(v.tensor_tensor_scan(running, keep[:], whole, 0.0, ALU.mult, ALU.add))
                c.step(v.tensor_tensor(so_far, so_far, whole, ALU.subtract))
                c.wait()
                count = e_first(running)[:, :, GT - 1]
                yield
                tiles, end, first = ends[:, 0, :], ends[:, 1, :], ends[:, 2, :]
                c.step(v.tensor_scalar(ends_i[:], count, MROWS - 1, None, ALU.add))
                c.step(v.tensor_tensor(so_far, so_far, running, ALU.add))
                c.wait()
                c.step(v.tensor_scalar(ends_i[:], ends_i[:], MROWS.bit_length() - 1, None, ALU.arith_shift_right))
                c.wait()
                c.step(v.tensor_copy(tiles, ends_i[:]))
                c.wait()
                c.step(v.tensor_tensor_scan(end, ends[:, 3, :], tiles, 0.0, ALU.mult, ALU.add))
                c.wait()
                c.step(v.tensor_tensor(first, end, tiles, ALU.subtract))
                c.step(v.tensor_tensor(tile_cmp, numbers[:].unsqueeze(2).broadcast_to([CHUNK, MT, EXPERTS]),
                                       end.unsqueeze(1).broadcast_to([CHUNK, MT, EXPERTS]), ALU.is_ge))
                c.wait()
                yield
                c.step(v.tensor_scalar(first, first, float(MROWS), None, ALU.mult))
                c.step(v.tensor_reduce(running[:, 0:MT], tile_cmp, AX.X, ALU.add))
                c.wait()
                c.step(v.tensor_tensor(e_first(so_far), e_first(so_far), first.unsqueeze(2).broadcast_to([CHUNK, EXPERTS, GT]), ALU.add))
                to = tile_expert[:, 1 + grp * MT:1 + grp * MT + MT]
                c.step(v.tensor_scalar(to, running[:, 0:MT], float(EXPERTS - 1), None, ALU.min))
                c.wait()
                for k in range(2):
                    c.step(v.tensor_tensor((rank[:, 0], lg[:])[k], so_far.rearrange("p (e t) -> p t e", e=EXPERTS), rank[:, 2 + k], ALU.mult))
                c.wait()
                for k in range(2):
                    c.step(v.tensor_reduce(place_f[:, k, :], (rank[:, 0], lg[:])[k], AX.X, ALU.add))
                c.step(v.tensor_copy(tile_expert[:, 0:1], tile_expert[:, NG2 * MT:NG2 * MT + 1]) if grp else
                       v.memset(ends[:, 3, :], 1.0))
                assert c.n == PLACE_STEPS, c.n
                c.wait()
                v.tensor_copy(place[:, grp], place_f[:]).then_inc(place_ok, 1)
                yield

            WEIGH_STEPS = 3

            def weigh(ex, grp):
                c = Chain(v, weigh_dve, ex * WEIGH_STEPS)
                v.wait_ge(tanh_ok, ex + 1)
                c.step(v.tensor_scalar(cw[:], cw[:], 1.0, 0.5, ALU.add, ALU.mult))
                v.wait_ge(place_ok, ex + 1)
                c.wait()
                for k in range(2):
                    c.step(v.tensor_tensor((rank[:, 0], lg[:])[k], rank[:, 2 + k], cw[:], ALU.mult))
                c.wait()
                for k in range(2):
                    v.tensor_reduce(weight[:, grp, k, :], (rank[:, 0], lg[:])[k], AX.X, ALU.add).then_inc(weight_ok, 1)
                assert c.n == WEIGH_STEPS

            def rest_x(s, q):
                v.wait_ge(x_hi_ok, q + 1)
                v.tensor_tensor(x_lo[:, s].rearrange("p k t -> p (k t)"), ps[:, XT, 256 * s:256 * s + 256],
                                x_hi[:, s].rearrange("p k t -> p (k t)").bitcast(F32), ALU.subtract).then_inc(x_lo_ok, 1)

            def rest_g(hf, w):
                v.wait_ge(hi_ok, w + 1)
                v.tensor_tensor(g_lo[:, hf, :], ps[:, TURN + hf, :], g_hi[:, hf, :].bitcast(F32), ALU.subtract).then_inc(lo_ok, 1)

            def keep_y(s, q, stores):
                v.wait_ge(y_mult, q * 2 + 4)
                wait_if(v, y_stored[s], stores * 16)
                v.tensor_copy(y[:, s, :], ps[:, Y, 256 * s:256 * s + D]).then_inc(y_ok, 1)

            def body(ph, grp, i, part):
                kind, b, rnd = part or (None, None, None)
                ex, other = ph + 1, 1 - grp
                to_rows = not (isinstance(ph, int) and ph == PHASES - 1)
                fresh = isinstance(ph, int) and ph == 0
                parts = iter(())
                if kind == "choose":
                    parts = choose(ex, rnd)
                if kind == "place":
                    parts = set_places(ex, other)
                for s in range(2):
                    q = (ph * BODIES + i) * 2 + s
                    start = isinstance(q, int) and q == 0
                    if not (isinstance(q, int) and q == PHASES * MT - 1):
                        rest_x(1 - s, q + 1)
                    if not start:
                        rest_g(1, q * 2 - 1)
                    if kind == "rows" and s == 0:
                        if fresh:
                            normal_rows(ex, other, b)
                        else:
                            add_first(ex, other, b)
                    next(parts, None)
                    rest_g(0, q * 2)
                    if kind == "rows" and s == 0 and not fresh:
                        add_second(ex, other, b, to_rows)
                    if s == 0:
                        next(parts, None)
                    if kind == "place" and s == 1:
                        weigh(ex, other)
                    if not start:
                        keep_y(1 - s, q - 1, ph * BODIES + i - 1 + s)

            with v.Fori(0, GB) as b:
                normal_rows(0, 0, b)
            v.wait_ge(bias_loaded, 16)
            v.tensor_copy(bias_hi[:], bias_raw[:]).then_inc(bias_split, 1)
            v.wait_ge(bias_split, 1)
            v.tensor_tensor(bias_lo[:], bias_raw[:], bias_hi[:].bitcast(F32), ALU.subtract).then_inc(bias_split, 1)
            for part in (choose(0, 0), set_places(0, 0)):
                for _ in part:
                    pass
            weigh(0, 0)
            for n in range(4):
                at = slice(WQ * n, WQ * n + WQ)
                v.wait_ge(w_hi_ok, n + 1)
                v.tensor_tensor(w_lo[:, at], w_lo[:, at].bitcast(F32), w_hi[:, at].bitcast(F32), ALU.subtract).then_inc(w_lo_ok, 1)
            rest_x(0, 0)
            all_phases(v, body)
            rest_g(1, PHASES * MT * 2 - 1)
            keep_y(1, PHASES * MT - 1, PHASES * BODIES - 1)

            def one_stats(t):
                return v.bn_stats(h_stats[:, ds(t, 1), :].rearrange("p o s -> p (o s)"), row_of(0, t))

            part = h[:, 0:GT, :]
            v.wait_ge(row_ok, (PHASES + 1) * GT)
            v.wait_ge(kept_loaded[0], 16)
            v.tensor_tensor(part, part, kept(0), ALU.add).then_inc(kept_added, 1)
            v.wait_ge(kept_added, 1)
            with v.Fori(0, GT) as t:
                one_stats(t).then_inc(stats_ok, 1)
            v.wait_ge(kept_loaded[1], 16)
            for b in range(GB):
                v.wait_ge(last_gathered[b], 2 * GU * 16)
                ts = range(b * GU, (b + 1) * GU)
                for t in ts:
                    v.scalar_tensor_tensor(last_rows[:, t, 0, :], last_rows[:, t, 0, :], weight[:, 1, 0, t:t + 1],
                                           h[:, GT + t, :], ALU.mult, ALU.add).then_inc(half_added, 1)
                for t in ts:
                    v.wait_ge(half_added, PHASES * GT - GT + t + 1)
                    v.scalar_tensor_tensor(h[:, GT + t, :], last_rows[:, t, 1, :], weight[:, 1, 1, t:t + 1],
                                           last_rows[:, t, 0, :], ALU.mult, ALU.add).then_inc(row_ok, 1)
                part = slice(b * GU, (b + 1) * GU)
                v.wait_ge(row_ok, (PHASES + 1) * GT + (b + 1) * GU)
                v.tensor_tensor(h[:, GT:NT, :][:, part, :], h[:, GT:NT, :][:, part, :], kept(1)[:, part, :], ALU.add).then_inc(kept_added, 1)
                v.wait_ge(kept_added, b + 2)
                for t in ts:
                    v.bn_stats(h_stats[:, GT + t, :], h[:, GT + t, :]).then_inc(stats_ok, 1)


def retention(nc, io, h, x_t, ident):
    with ExitStack() as ctx:
        def sb(name, shape, dt=F32):
            return ctx.enter_context(nc.sbuf_tensor("re_" + name, shape, dt))

        def sem(name):
            return ctx.enter_context(nc.semaphore("re_" + name))

        U = 2 * NCH
        GH = 4
        NG = HEADS // GH
        vg = sb("vg", [CHUNK, NT, 2 * D])
        out = sb("out", [CHUNK, NT, D])
        w = sb("w", [128, KC, 4 * D])
        w_o = sb("w_o", [128, KC, D])
        bias = sb("bias", [CHUNK, 4 * D])
        b_qk = sb("b_qk", [CHUNK, NCH, 2 * D])
        rows3 = sb("rows3", [CHUNK, 3, D])
        decay = sb("decay", [CHUNK, NCH, 2])
        causal = sb("causal", [CHUNK, CHUNK])
        head_mask = sb("head_mask", [128, 128])
        head_of = sb("head_of", [128, 8])
        x_s = sb("x_s", [128, 2, KC, CHUNK])
        qk = sb("qk", [CHUNK, NCH, 2 * D])
        qk_t = sb("qk_t", [128, 2, 2 * KC, CHUNK])
        q_h = sb("q_h", [128, 2, HEADS, CHUNK])
        sc = sb("sc", [CHUNK, HEADS, CHUNK])
        state = sb("state", [128, KC, 128])
        stats = sb("stats", [CHUNK, NT, 6])
        mv = sb("mv", [CHUNK, NT, 2])
        small = sb("small", [CHUNK, 4, NT])
        rows = sb("rows", [CHUNK, 2, D])
        ps = ctx.enter_context(nc.psum_tensor("re_ps", [128, 8, 512], F32))
        QK, VG, TURN, SC, OUT, ST = 0, 1, 2, 3, 5, 7
        loaded, dve, x_copied, projected = sem("loaded"), sem("dve"), sem("x_copied"), sem("projected")
        qkvg_ok, turned, qk_t_ok, q_h_ok = sem("qkvg_ok"), sem("turned"), sem("qk_t_ok"), sem("q_h_ok")
        sc_mult, sc_ok, st_ok, out_mult, out_ok = sem("sc_mult"), sem("sc_ok"), sem("st_ok"), sem("out_mult"), sem("out_ok")
        gate_ok, gates_ready, var_ready, root_done = sem("gate_ok"), sem("gates_ready"), sem("var_ready"), sem("root_done")
        pool_step, stats_ok, n_ok, r_ok, n_turned, n_t_ok, o_mult, h_ok = sem("pool_step"), sem("stats_ok"), sem("n_ok"), sem("r_ok"), sem("n_turned"), sem("n_t_ok"), sem("o_mult"), sem("h_ok")
        block = ctx.enter_context(nc.Block())

        @block.sync
        def _(sp):
            sp.dma_start(w[:], io["re_w"]).then_inc(loaded, 16)
            sp.dma_start(w_o[:], io["re_w_o"]).then_inc(loaded, 16)
            sp.dma_start(bias[:], io["re_bias"].broadcast_to([CHUNK, 4 * D])).then_inc(loaded, 16)
            sp.dma_start(rows3[:], io["re_rows3"].broadcast_to([CHUNK, 3, D])).then_inc(loaded, 16)
            sp.dma_start(decay[:], io["decay"]).then_inc(loaded, 16)
            sp.dma_start(causal[:], io["causal"]).then_inc(loaded, 16)
            sp.dma_start(head_mask[:], io["head_mask"]).then_inc(loaded, 16)
            sp.dma_start(head_of[:], io["head_of"]).then_inc(loaded, 16)

        LOADED = 16 * 8

        def one(ap, t):
            return ap[:, ds(t, 1), :].rearrange("p o d -> p (o d)")

        def states_before(t, u):
            done = u - u // NCH - 1
            return (t - u) // NCH * (NCH - 1) + done if isinstance(t, int) else (t - u) // U * (2 * NCH - 2) + done

        def is_at(t, n):
            return isinstance(t, int) and t == n

        def all_tiles(eng, body):
            for u in range(U):
                body(0, u)
            with eng.Fori(1, NT // U - 1) as i:
                for u in range(U):
                    body(i, u)
            for u in range(U):
                body(NT // U - 1, u)

        @block.gpsimd
        def _(g):
            g.wait_ge(loaded, LOADED)

            def take_x(t, u):
                g.wait_ge(projected, t + 1)
                g.tensor_copy(x_s[:, u % 2], x_t[:, :, ds(t * CHUNK, CHUNK)]).then_inc(x_copied, 1)

            def gates(t):
                g.wait_ge(gates_ready, t + 1)
                g.wait_ge(out_mult, t + 3)
                g.sem_inc(pool_step, 1)
                v_at, g_at, row = one(vg, t)[:, 0:D], one(vg, t)[:, D:2 * D], one(h, t)
                g.tensor_tensor(v_at, g_at, rows3[:, 2, :], ALU.mult).then_inc(gate_ok, 1)
                g.tensor_tensor(row, row, rows3[:, 0, :], ALU.add).then_inc(gate_ok, 1)
                g.wait_ge(gate_ok, t * 3 + 1)
                g.sem_inc(pool_step, 1)
                g.tensor_tensor(g_at, g_at, rows3[:, 1, :], ALU.mult).then_inc(gate_ok, 1)

            def body(i, u):
                t, p = i * U + u, u % 2
                if not is_at(t, NT - 1):
                    take_x(t + 1, u + 1)
                g.wait_ge(qk_t_ok, t + 2)
                g.wait_ge(sc_mult, t * NG + NG)
                for m in range(KC):
                    ins = g.tensor_tensor(q_h[:, p, 8 * m:8 * m + 8, :],
                                          qk_t[:, p, m:m + 1, :].broadcast_to([128, 8, CHUNK]),
                                          head_of[:].unsqueeze(2).broadcast_to([128, 8, CHUNK]), ALU.mult)
                ins.then_inc(q_h_ok, 1)
                if not is_at(t, 0) and not is_at(t, 1):
                    gates(t - 2)

            take_x(0, 0)
            all_tiles(g, body)
            gates(NT - 2)
            gates(NT - 1)

        @block.tensor
        def _(pe):
            for s, n in ((projected, 2), (sc_mult, 2 * NG), (out_mult, 2), (n_turned, 2), (o_mult, 2)):
                pe.sem_inc(s, n)
            pe.wait_ge(loaded, LOADED)

            def project(t, u):
                pe.wait_ge(x_copied, t + 1)
                pe.wait_ge(qkvg_ok, t + 1)
                for bank in (QK, VG):
                    for k in range(KC):
                        mm = pe.matmul(ps[0:CHUNK, bank, :], x_s[:, u % 2, k, :], w[:, k, 512 * bank:512 * bank + 512],
                                       start=(k == 0), stop=(k == KC - 1))
                mm.then_inc(projected, 1)

            def turn(t, u):
                pe.wait_ge(qkvg_ok, t + 2)
                pe.wait_ge(qk_t_ok, t + 1)
                for k in range(2 * KC):
                    mm = pe.transpose(ps[:, TURN, k * CHUNK:(k + 1) * CHUNK], qk[:, u % NCH, 128 * k:128 * k + 128],
                                      ident[0:CHUNK, 0:CHUNK])
                mm.then_inc(turned, 1)

            def scores(t, u):
                pe.wait_ge(q_h_ok, t + 1)
                for n in range(NG):
                    pe.wait_ge(sc_ok, t * NG + n + 1)
                    pe.matmul(ps[0:CHUNK, SC + n % 2, 0:GH * CHUNK], qk_t[:, u % 2, KC + n // 2, :],
                              q_h[:, u % 2, GH * n:GH * n + GH, :], start=True, stop=True).then_inc(sc_mult, 1)

            def outputs(t, u):
                j = u % NCH
                pe.wait_ge(sc_ok, t * NG + NG + 2)
                pe.wait_ge(out_ok, t + 1)
                if j > 0:
                    pe.wait_ge(st_ok, states_before(t, u) + 1)
                    for m in range(KC):
                        pe.matmul(ps[0:CHUNK, OUT + u % 2, 128 * m:128 * m + 128], qk_t[:, u % 2, m, :], state[:, m, :],
                                  start=(m == 0), stop=False, skip_group_check=True)
                for e in range(HEADS):
                    mm = pe.matmul(ps[0:CHUNK, OUT + u % 2, DH * e:DH * e + DH], sc[:, e, :],
                                   vg[:, ds(t, 1), DH * e:DH * e + DH].rearrange("p o d -> p (o d)"),
                                   start=(j == 0 and e == 0), stop=True, skip_group_check=True)
                if j < NCH - 1:
                    for m in range(KC):
                        mm = pe.matmul(ps[:, ST, 128 * m:128 * m + 128], qk[:, u % NCH, D + 128 * m:D + 128 * m + 128],
                                       vg[:, ds(t, 1), 128 * m:128 * m + 128].rearrange("p o d -> p (o d)"),
                                       start=(j == 0 and m == 0), stop=True, skip_group_check=True)
                mm.then_inc(out_mult, 1)

            def body(i, u):
                t = i * U + u
                turn(t, u)
                if not is_at(t, 0):
                    scores(t - 1, u - 1)
                if not is_at(t, NT - 1):
                    project(t + 1, u + 1)
                if not is_at(t, 0):
                    outputs(t - 1, (u - 1) % U)

            project(0, 0)
            all_tiles(pe, body)
            scores(NT - 1, U - 1)
            outputs(NT - 1, U - 1)
            pe.wait_ge(out_ok, NT + 2)
            def turn_pair(i):
                for p in range(2):
                    t = i * 2 + p
                    pe.wait_ge(n_ok, t + 1)
                    pe.wait_ge(n_t_ok, t + 1)
                    for k in range(KC):
                        mm = pe.transpose(ps[:, p, k * CHUNK:(k + 1) * CHUNK], rows[:, p, 128 * k:128 * k + 128],
                                          ident[0:CHUNK, 0:CHUNK])
                    mm.then_inc(n_turned, 1)

            def project_pair(i):
                for p in range(2):
                    t = i * 2 + p
                    pe.wait_ge(n_t_ok, t + 3)
                    pe.wait_ge(h_ok, t + 1)
                    for k in range(KC):
                        mm = pe.matmul(ps[0:CHUNK, 2 + p, 0:D], x_s[:, p, k, :], w_o[:, k, :],
                                       start=(k == 0), stop=(k == KC - 1))
                    mm.then_inc(o_mult, 1)

            turn_pair(0)
            with pe.Fori(0, NT // 2 - 1) as i:
                project_pair(i)
                turn_pair(i + 1)
            project_pair(NT // 2 - 1)

        @block.scalar
        def _(act):
            for s, n in ((qk_t_ok, 1), (out_ok, 2), (n_t_ok, 2)):
                act.sem_inc(s, n)
            def out_rows(t, u):
                act.wait_ge(out_mult, t + 3)
                nc.scalar.copy(one(out, t), ps[0:CHUNK, OUT + u % 2, 0:D]).then_inc(out_ok, 1)
                gate = one(vg, t)[:, D:2 * D]
                nc.scalar.activation(gate, gate, ACT.Sigmoid).then_inc(gates_ready, 1)

            def body(i, u):
                t = i * U + u
                act.wait_ge(turned, t + 1)
                act.wait_ge(out_mult, t + 1)
                nc.scalar.copy(qk_t[:, u % 2].rearrange("p k t -> p (k t)"), ps[:, TURN, 0:2 * KC * CHUNK]).then_inc(qk_t_ok, 1)
                if not is_at(t, 0):
                    out_rows(t - 1, u - 1)

            all_tiles(act, body)
            out_rows(NT - 1, NT - 1)
            act.wait_ge(var_ready, 1)
            nc.scalar.sqrt(small[:, 1, :], small[:, 0, :]).then_inc(root_done, 1)
            with act.Fori(0, NT // 2) as i:
                for p in range(2):
                    t = i * 2 + p
                    act.wait_ge(n_turned, t + 3)
                    act.wait_ge(o_mult, t + 1)
                    nc.scalar.copy(x_s[:, p].rearrange("p k t -> p (k t)"), ps[:, p, 0:KC * CHUNK]).then_inc(n_t_ok, 1)

        @block.vector
        def _(v):
            for s, n in ((qkvg_ok, 1), (sc_ok, 2), (h_ok, 2)):
                v.sem_inc(s, n)
            c = Chain(v, dve)
            v.wait_ge(loaded, LOADED)
            for j in range(NCH):
                for a in range(2):
                    c.step(v.tensor_scalar(b_qk[:, j, a * D:a * D + D], bias[:, a * D:a * D + D], decay[:, j, a:a + 1],
                                           None, ALU.mult))
            c.wait()
            def take_projected(t, u):
                j = u % NCH
                v.wait_ge(projected, t + 3)
                for a in range(2):
                    v.scalar_tensor_tensor(qk[:, j, a * D:a * D + D], ps[0:CHUNK, QK, a * D:a * D + D],
                                           decay[:, j, a:a + 1], b_qk[:, j, a * D:a * D + D], ALU.mult, ALU.add)
                v.tensor_tensor(one(vg, t), ps[0:CHUNK, VG, :], bias[:, 2 * D:4 * D], ALU.add).then_inc(qkvg_ok, 1)

            def mask_scores(t, u):
                v.wait_ge(out_mult, t + 2)
                if u % NCH > 0:
                    v.tensor_tensor(state[:], ps[:, ST, 0:D].rearrange("p (m e) -> p m e", m=KC),
                                    head_mask[:].unsqueeze(1).broadcast_to([128, KC, 128]), ALU.mult).then_inc(st_ok, 1)
                for n in range(NG):
                    v.wait_ge(sc_mult, t * NG + n + 1 + 2 * NG)
                    v.tensor_tensor(sc[:, GH * n:GH * n + GH, :],
                                    ps[0:CHUNK, SC + n % 2, 0:GH * CHUNK].rearrange("p (g i) -> p g i", g=GH),
                                    causal[:].unsqueeze(1).broadcast_to([CHUNK, GH, CHUNK]), ALU.mult).then_inc(sc_ok, 1)

            def out_stats(t):
                v.wait_ge(out_ok, t + 3)
                v.bn_stats(one(stats, t), one(out, t)).then_inc(stats_ok, 1)

            def body(i, u):
                t = i * U + u
                if not is_at(t, 0):
                    mask_scores(t - 1, (u - 1) % U)
                if not is_at(t, NT - 1):
                    take_projected(t + 1, u + 1)
                if not is_at(t, 0) and not is_at(t, 1):
                    out_stats(t - 2)

            take_projected(0, 0)
            all_tiles(v, body)
            mask_scores(NT - 1, U - 1)
            out_stats(NT - 2)
            out_stats(NT - 1)
            v.wait_ge(stats_ok, NT)
            moments(c, stats, mv)
            v.tensor_scalar(small[:, 0, :], mv[:, :, 1], LN_EPS, None, ALU.add).then_inc(var_ready, 1)
            v.wait_ge(root_done, 1)
            inverse_root(c, small[:, 0, :], small[:, 1, :], small[:, 2, :], small[:, 3, :])
            v.wait_ge(gate_ok, 3 * NT)
            def rows_pair(i):
                for p in range(2):
                    t = i * 2 + p
                    v.wait_ge(n_turned, t + 1)
                    v.tensor_scalar(rows[:, p, :], one(out, t), mv[:, ds(t, 1), 0], small[:, 2, ds(t, 1)],
                                    ALU.subtract, ALU.mult).then_inc(r_ok, 1)
                for p in range(2):
                    v.wait_ge(r_ok, i * 4 + p + 1)
                    v.tensor_tensor(rows[:, p, :], rows[:, p, :], one(vg, i * 2 + p)[:, D:2 * D], ALU.mult).then_inc(r_ok, 1)
                for p in range(2):
                    v.wait_ge(r_ok, i * 4 + p + 3)
                    v.tensor_tensor(rows[:, p, :], rows[:, p, :], one(vg, i * 2 + p)[:, 0:D], ALU.add).then_inc(n_ok, 1)

            def add_pair(i):
                for p in range(2):
                    t = i * 2 + p
                    v.wait_ge(o_mult, t + 3)
                    row = h[:, ds(t, 1), :].rearrange("p o d -> p (o d)")
                    v.tensor_tensor(row, row, ps[0:CHUNK, 2 + p, 0:D], ALU.add).then_inc(h_ok, 1)

            rows_pair(0)
            with v.Fori(0, NT // 2 - 1) as i:
                rows_pair(i + 1)
                add_pair(i)
            add_pair(NT // 2 - 1)


NEXP, EF, SF = 16, 256, 1024
ST = SF // 128
ROWS = 128
G_TILES = (T + NEXP * (ROWS - 1)) // ROWS
SHW = ST * (2 * KC * 128 + D)


def route_and_share(nc, io, h, x_sorted, place, tile_expert, w_gu, ident):
    with ExitStack() as ctx:
        def sb(name, shape, dt=F32):
            return ctx.enter_context(nc.sbuf_tensor("sh_" + name, shape, dt))

        def sem(name):
            return ctx.enter_context(nc.semaphore("sh_" + name))

        w_hi, w_lo = sb("w_hi", [128, SHW], F32R), sb("w_lo", [128, SHW], F32R)
        stats = sb("stats", [CHUNK, NT, 6])
        mv = sb("mv", [CHUNK, NT, 2])
        small = sb("small", [CHUNK, 6, NT])
        x_rows = sb("x_rows", [CHUNK, NT, D])
        x_f = sb("x_f", [128, KC, TW])
        x_hi, x_lo = sb("x_hi", [128, 2, KC, TW], F32R), sb("x_lo", [128, 2, KC, TW], F32R)
        router = sb("router", [128, KC, NEXP])
        lg = sb("lg", [CHUNK, NT, NEXP])
        hot = sb("hot", [CHUNK, NT, NEXP])
        early = sb("early", [CHUNK, CHUNK])
        ones = sb("ones", [CHUNK, CHUNK])
        numbers = sb("numbers", [CHUNK, NEXP + G_TILES])
        keep = sb("keep", [CHUNK, NEXP * NT])
        ends = sb("ends", [CHUNK, 4, NEXP])
        ends_i = sb("ends_i", [CHUNK, NEXP], I32)
        big = sb("big", [128, 6 * TW])
        g = big[:, 0:2 * TW].rearrange("p (s t) -> p s t", s=2)
        pr = big[:, 2 * TW:4 * TW].rearrange("p (s t) -> p s t", s=2)
        g_hi, g_lo = sb("g_hi", [128, 2, TW], F32R), sb("g_lo", [128, 2, TW], F32R)
        rows = sb("rows", [CHUNK, 2, D])
        y_f = big[:, 4 * TW:6 * TW].rearrange("p (m t) -> p m t", m=KC)
        ps = ctx.enter_context(nc.psum_tensor("sh_ps", [128, 8, 512], F32))
        GATE, UP, Y, XT = 0, 2, 4, 6
        loaded, gu_loaded, lo_ok_w, hi_ok_w = (sem("loaded"), sem("gu_loaded"),
                                                                sem("lo_ok_w"), sem("hi_ok_w"))
        staged = [sem("staged0"), sem("staged1")]
        dve, var_ready, root_done, rows_ok, r_turned, r_t_ok = (sem("dve"), sem("var_ready"), sem("root_done"), sem("rows_ok"),
                                                                sem("r_turned"), sem("r_t_ok"))
        lg_mult, lg_ok, hot_ok, counted, score_arg, score_ok = (sem("lg_mult"), sem("lg_ok"), sem("hot_ok"), sem("counted"),
                                                                sem("score_arg"), sem("score_ok"))
        scale_ok, x_rows_ok, scattered = sem("scale_ok"), sem("x_rows_ok"), sem("scattered")
        rows2_ok, turned, x_f_ok, x_hi_ok, x_lo_ok = sem("rows2_ok"), sem("turned"), sem("x_f_ok"), sem("x_hi_ok"), sem("x_lo_ok")
        hid_mult, silu_ok, prod_ok, hi_ok, lo_ok = sem("hid_mult"), sem("silu_ok"), sem("prod_ok"), sem("hi_ok"), sem("lo_ok")
        y_mult, y_f_ok, back_turned, h_ok = sem("y_mult"), sem("y_f_ok"), sem("back_turned"), sem("h_ok")
        block = ctx.enter_context(nc.Block())
        WH = SHW // 2
        raw = w_gu[:].rearrange("p e k f -> p (e k f)")[:, 0:SHW]
        Y_FREE = ST + 1
        w1 = [w[:, 0:ST * 2 * KC * 128].rearrange("p (f u k c) -> p f u k c", f=ST, u=2, k=KC) for w in (w_hi, w_lo)]
        w2 = [w[:, ST * 2 * KC * 128:].rearrange("p (f d) -> p f d", f=ST) for w in (w_hi, w_lo)]

        def is_at(j, n):
            return isinstance(j, int) and j == n

        def all_tiles(eng, tile):
            tile(0, 0)
            with eng.Fori(0, NP - 1) as i:
                tile(i * 2 + 1, 1)
                tile(i * 2 + 2, 0)
            tile(2 * NP - 1, 1)

        @block.sync
        def _(sp):
            for dst, name in ((router, "router"), (early, "early"), (keep, "keep"), (numbers, "numbers")):
                src = io[name]
                sp.dma_start(dst[:], src if src.shape[0] > 1 else src.broadcast_to([CHUNK, src.shape[1]])).then_inc(loaded, 16)
            for n in range(2):
                sp.dma_start(raw[:, WH * n:WH * n + WH], io["sh_w"][:, WH * n:WH * n + WH]).then_inc(staged[n], 16)
            sp.wait_ge(lo_ok_w, 2)
            sp.dma_start(w_gu[:], io["ex_gu"]).then_inc(gu_loaded, 16)
            sp.wait_ge(gu_loaded, 16)

        @block.gpsimd
        def _(gp):
            for n in range(2):
                at = slice(WH * n, WH * n + WH)
                gp.wait_ge(hi_ok_w, n + 1)
                gp.tensor_tensor(w_lo[:, at], raw[:, at], w_hi[:, at].bitcast(F32), ALU.subtract).then_inc(lo_ok_w, 1)
            gp.wait_ge(scale_ok, 2)
            for t in range(NT):
                gp.wait_ge(x_rows_ok, t + 1)
                gp.indirect_dma_start(x_sorted, bass.IndirectOffsetOnAxis(ap=place[:, t:t + 1].bitcast(U32), axis=0),
                                      x_rows[:, t, :], None).then_inc(scattered, 16)
            gp.wait_ge(scattered, 16 * NT)

        @block.tensor
        def _(pe):
            for s, n in ((r_turned, 2), (lg_mult, 2), (turned, 2), (y_mult, Y_FREE), (back_turned, 1)):
                pe.sem_inc(s, n)
            pe.wait_ge(loaded, 16 * 4)
            def turn_pair(i):
                for p in range(2):
                    t = i * 2 + p
                    pe.wait_ge(rows_ok, t + 1)
                    pe.wait_ge(r_t_ok, t + 1)
                    for k in range(KC):
                        mm = pe.transpose(ps[:, p, k * CHUNK:(k + 1) * CHUNK], rows[:, p, 128 * k:128 * k + 128],
                                          ident[0:CHUNK, 0:CHUNK])
                    mm.then_inc(r_turned, 1)

            def logits_pair(i):
                for p in range(2):
                    t = i * 2 + p
                    pe.wait_ge(r_t_ok, t + 3)
                    pe.wait_ge(lg_ok, t + 1)
                    for k in range(KC):
                        mm = pe.matmul(ps[0:CHUNK, 2 + p, 0:NEXP], x_f[:, p, k * CHUNK:(k + 1) * CHUNK], router[:, k, :],
                                       start=(k == 0), stop=(k == KC - 1))
                    mm.then_inc(lg_mult, 1)

            turn_pair(0)
            with pe.Fori(0, NT // 2 - 1) as i:
                logits_pair(i)
                turn_pair(i + 1)
            logits_pair(NT // 2 - 1)
            pe.wait_ge(hot_ok, 1)
            all_hot = hot[:].rearrange("p t e -> p (t e)")
            pe.matmul(ps[0:CHUNK, 4, 0:NT * NEXP], early[:], all_hot, start=True, stop=True)
            pe.matmul(ps[0:CHUNK, 5, 0:NT * NEXP], ones[:], all_hot, start=True, stop=True).then_inc(counted, 1)
            pe.wait_ge(scale_ok, 2)
            pe.wait_ge(lo_ok_w, 2)

            def back(j):
                pe.wait_ge(y_f_ok, j + 2)
                pe.wait_ge(h_ok, j + 1)
                pe.wait_ge(x_f_ok, (2 * NP if is_at(j, 2 * NP - 1) else j + 2) * TC + 2)
                for c in range(TC):
                    for m in range(KC):
                        at = 256 * (c % 2) + 128 * m
                        mm = pe.transpose(ps[0:CHUNK, XT + c // 2, at:at + 128], y_f[:, m, c * CHUNK:(c + 1) * CHUNK], ident[:])
                mm.then_inc(back_turned, 1)

            def turn(j, c):
                pe.wait_ge(rows2_ok, j * TC + c + 1)
                pe.wait_ge(x_f_ok, j * TC + c + 1)
                wait_if(pe, h_ok, j)
                for k in range(KC):
                    mm = pe.transpose(ps[:, XT + c % 2, k * CHUNK:(k + 1) * CHUNK], rows[:, c % 2, 128 * k:128 * k + 128],
                                      ident[0:CHUNK, 0:CHUNK])
                mm.then_inc(turned, 1)

            def tile(j, p):
                pe.wait_ge(x_lo_ok, j + 2)
                for k in range(ST + 2):
                    if k < ST:
                        q = j * ST + k
                        pe.wait_ge(prod_ok, q + 1)
                        for u, bank in ((0, GATE), (1, UP)):
                            for a in range(KC):
                                for part, xs in ((0, x_hi), (0, x_lo), (1, x_hi)):
                                    mm = pe.matmul(ps[:, bank + k % 2, 0:TW], w1[part][:, k, u, a, :], xs[:, p, a, :],
                                                   start=(a == 0 and part == 0 and xs is x_hi), stop=(a == KC - 1 and part == 1))
                        mm.then_inc(hid_mult, 1)
                    if k == 2:
                        pe.wait_ge(y_f_ok, j + 1)
                    if k >= 2:
                        f = k - 2
                        pe.wait_ge(lo_ok, j * ST + f + 3)
                        for m in range(KC):
                            for part, gs in ((0, g_hi), (0, g_lo), (1, g_hi)):
                                mm = pe.matmul(ps[:, Y + m, 0:TW], w2[part][:, f, 128 * m:128 * m + 128], gs[:, f % 2, :],
                                               start=(f == 0 and part == 0 and gs is g_hi), stop=(f == ST - 1 and part == 1))
                        mm.then_inc(y_mult, 1)
                    if k == 1 and not is_at(j, 0):
                        back(j - 1)
                    if 3 <= k < 3 + TC and not is_at(j, 2 * NP - 1):
                        turn(j + 1, k - 3)

            for c in range(TC):
                turn(0, c)
            all_tiles(pe, tile)
            back(2 * NP - 1)

        @block.scalar
        def _(act):
            for s, n in ((r_t_ok, 2), (x_f_ok, 2), (y_f_ok, 1)):
                act.sem_inc(s, n)
            act.wait_ge(var_ready, 1)
            nc.scalar.sqrt(small[:, 1, :], small[:, 0, :]).then_inc(root_done, 1)
            for n in range(2):
                act.wait_ge(staged[n], 16)
                nc.scalar.copy(w_hi[:, WH * n:WH * n + WH], raw[:, WH * n:WH * n + WH]).then_inc(hi_ok_w, 1)
            with act.Fori(0, NT // 2) as i:
                for p in range(2):
                    t = i * 2 + p
                    act.wait_ge(r_turned, t + 3)
                    act.wait_ge(lg_mult, t + 1)
                    nc.scalar.copy(x_f[:, p, 0:KC * CHUNK], ps[:, p, 0:KC * CHUNK]).then_inc(r_t_ok, 1)
            act.wait_ge(score_arg, 1)
            nc.scalar.activation(small[:, 4, :], small[:, 3, :], ACT.Sigmoid).then_inc(score_ok, 1)

            def scaled_rows(t):
                nc.scalar.activation(x_rows[:, t, :], h[:, t, :], ACT.Identity,
                                     bias=small[:, 5, t:t + 1], scale=small[:, 4, t:t + 1]).then_inc(x_rows_ok, 1)

            def silu(j, k):
                q = j * ST + k
                act.wait_ge(hid_mult, q + 1)
                nc.scalar.activation(g[:, k % 2, :], ps[:, GATE + k % 2, 0:TW], ACT.Silu).then_inc(silu_ok, 1)
                act.wait_ge(prod_ok, q + 3)
                act.wait_ge(y_mult, q + ST)
                nc.scalar.copy(g_hi[:, k % 2, :], pr[:, k % 2, :]).then_inc(hi_ok, 1)

            def keep_x(j, c):
                act.wait_ge(x_lo_ok, j + 1)
                act.wait_ge(turned, j * TC + c + 3)
                nc.scalar.copy(x_f[:, :, c * CHUNK:(c + 1) * CHUNK],
                               ps[:, XT + c % 2, 0:KC * CHUNK].rearrange("p (k t) -> p k t", k=KC)).then_inc(x_f_ok, 1)

            def part_x(j, p):
                act.wait_ge(x_f_ok, j * TC + TC + 2)
                act.wait_ge(y_mult, j * ST + 1)
                nc.scalar.copy(x_hi[:, p], x_f[:]).then_inc(x_hi_ok, 1)

            def tile(j, p):
                for k in range(ST):
                    silu(j, k)
                    if is_at(j, 0):
                        for t in range(k * NT // ST, (k + 1) * NT // ST):
                            scaled_rows(t)
                    if 3 <= k < 3 + TC and not is_at(j, 2 * NP - 1):
                        keep_x(j + 1, k - 3)
                    if k == 2 + TC and not is_at(j, 2 * NP - 1):
                        part_x(j + 1, 1 - p)
                act.wait_ge(y_mult, j * ST + ST + Y_FREE)
                act.wait_ge(back_turned, j + 1)
                nc.scalar.copy(y_f[:], ps[:, Y:Y + KC, 0:TW]).then_inc(y_f_ok, 1)

            for c in range(TC):
                keep_x(0, c)
            part_x(0, 0)
            act.wait_ge(scale_ok, 2)
            all_tiles(act, tile)

        @block.vector
        def _(v):
            for s, n in ((lg_ok, 2), (x_lo_ok, 1), (prod_ok, 2), (lo_ok, 2), (h_ok, 1)):
                v.sem_inc(s, n)
            c = Chain(v, dve)
            c.step(v.memset(ones[:], 1.0))
            row_stats(c, h, stats, mv)
            v.tensor_scalar(small[:, 0, :], mv[:, :, 1], LN_EPS, None, ALU.add).then_inc(var_ready, 1)
            v.wait_ge(root_done, 1)
            inverse_root(c, small[:, 0, :], small[:, 1, :], small[:, 2, :], small[:, 3, :])

            def row_tile(t, slot):
                return v.tensor_scalar(rows[:, slot, :], h[:, ds(t, 1), :].rearrange("p o d -> p (o d)"),
                                       mv[:, ds(t, 1), 0], small[:, 2, ds(t, 1)], ALU.subtract, ALU.mult)

            def rows_pair(i):
                for p in range(2):
                    v.wait_ge(r_turned, i * 2 + p + 1)
                    row_tile(i * 2 + p, p).then_inc(rows_ok, 1)

            def keep_logits(i):
                for p in range(2):
                    v.wait_ge(lg_mult, i * 2 + p + 3)
                    v.tensor_copy(lg[:, ds(i * 2 + p, 1), :].rearrange("p o e -> p (o e)"),
                                  ps[0:CHUNK, 2 + p, 0:NEXP]).then_inc(lg_ok, 1)

            rows_pair(0)
            with v.Fori(0, NT // 2 - 1) as i:
                rows_pair(i + 1)
                keep_logits(i)
            keep_logits(NT // 2 - 1)
            v.wait_ge(lg_ok, NT + 2)
            v.wait_ge(loaded, 16 * 4)
            by_e = [CHUNK, NT, NEXP]
            tables = big[0:CHUNK, 0:4 * NT * NEXP].rearrange("p (a n) -> p a n", a=4)
            v.tensor_reduce(small[:, 3, :], lg[:], AX.X, ALU.max).then_inc(score_arg, 1)
            v.wait_ge(score_arg, 1)
            number = numbers[:, 0:NEXP].unsqueeze(1).broadcast_to(by_e)
            c.step(v.tensor_tensor(hot[:], lg[:], small[:, 3, :].unsqueeze(2).broadcast_to(by_e), ALU.is_ge))
            c.wait()
            c.step(v.tensor_tensor(lg[:], hot[:], number, ALU.mult))
            c.wait()
            c.step(v.tensor_reduce(small[:, 5, :], lg[:], AX.X, ALU.min))
            c.wait()
            v.tensor_tensor(hot[:], number, small[:, 5, :].unsqueeze(2).broadcast_to(by_e), ALU.is_equal).then_inc(hot_ok, 1)
            v.wait_ge(counted, 1)
            before, total, running = tables[:, 0, :], tables[:, 1, :], tables[:, 2, :]

            def expert_first(ap):
                return ap.rearrange("p (t e) -> p e t", e=NEXP)

            c.step(v.tensor_copy(before.rearrange("p (e t) -> p e t", e=NEXP), expert_first(ps[0:CHUNK, 4, 0:NT * NEXP])))
            c.step(v.tensor_copy(total.rearrange("p (e t) -> p e t", e=NEXP), expert_first(ps[0:CHUNK, 5, 0:NT * NEXP])))
            c.wait()
            c.step(v.tensor_tensor_scan(running, keep[:], total, 0.0, ALU.mult, ALU.add))
            c.wait()
            count = running.rearrange("p (e t) -> p e t", e=NEXP)[:, :, NT - 1]
            tiles, end = ends[:, 0, :], ends[:, 1, :]
            c.step(v.tensor_scalar(ends_i[:], count, ROWS - 1, None, ALU.add))
            c.step(v.memset(ends[:, 3, :], 1.0))
            c.wait()
            c.step(v.tensor_scalar(ends_i[:], ends_i[:], 7, None, ALU.arith_shift_right))
            c.wait()
            c.step(v.tensor_copy(tiles, ends_i[:]))
            c.wait()
            c.step(v.tensor_tensor_scan(end, ends[:, 3, :], tiles, 0.0, ALU.mult, ALU.add))
            c.step(v.tensor_tensor(before, before, running, ALU.add))
            c.wait()
            c.step(v.tensor_tensor(ends[:, 2, :], end, tiles, ALU.subtract))
            c.step(v.tensor_tensor(before, before, total, ALU.subtract))
            c.wait()
            c.step(v.tensor_scalar(ends[:, 2, :], ends[:, 2, :], float(ROWS), None, ALU.mult))
            c.wait()
            c.step(v.tensor_tensor(before.rearrange("p (e t) -> p e t", e=NEXP), before.rearrange("p (e t) -> p e t", e=NEXP),
                                   ends[:, 2, :].unsqueeze(2).broadcast_to([CHUNK, NEXP, NT]), ALU.add))
            c.wait()
            c.step(v.tensor_tensor(lg[:], before.rearrange("p (e t) -> p t e", e=NEXP), hot[:], ALU.mult))
            c.wait()
            v.wait_ge(score_ok, 1)
            c.step(v.tensor_reduce(small[:, 3, :], lg[:], AX.X, ALU.add))
            c.wait()
            v.tensor_copy(place[:], small[:, 3, :]).then_inc(scale_ok, 1)
            cmp = big[0:CHUNK, 4 * NT * NEXP:4 * NT * NEXP + G_TILES * NEXP].rearrange("p (g e) -> p g e", e=NEXP)
            c.step(v.tensor_tensor(cmp, numbers[:, NEXP:].unsqueeze(2).broadcast_to([CHUNK, G_TILES, NEXP]),
                                   end.unsqueeze(1).broadcast_to([CHUNK, G_TILES, NEXP]), ALU.is_ge))
            c.wait()
            c.step(v.tensor_reduce(tables[:, 3, 0:G_TILES], cmp, AX.X, ALU.add))
            c.wait()
            c.step(v.tensor_scalar(tile_expert[:], tables[:, 3, 0:G_TILES], float(NEXP - 1), None, ALU.min))
            c.step(v.tensor_tensor(small[:, 4, :], small[:, 4, :], small[:, 2, :], ALU.mult))
            c.wait()
            v.scalar_tensor_tensor(small[:, 5, :], mv[:, :, 0], -1.0, small[:, 4, :], ALU.mult, ALU.mult).then_inc(scale_ok, 1)
            def place_row(j, c):
                v.wait_ge(turned, j * TC + c + 1)
                row_tile(j * TC + c, c % 2).then_inc(rows2_ok, 1)

            def rest_x(j, p):
                v.wait_ge(x_hi_ok, j + 1)
                v.tensor_tensor(x_lo[:, p], x_f[:], x_hi[:, p].bitcast(F32), ALU.subtract).then_inc(x_lo_ok, 1)

            def add_back(j):
                v.wait_ge(back_turned, j + 2)
                v.wait_ge(x_rows_ok, NT)
                out = h[:, ds(j * TC, TC), :].rearrange("p (a b) d -> p a (b d)", a=2)
                v.tensor_tensor(out, out, ps[0:CHUNK, XT:XT + 2, :], ALU.add).then_inc(h_ok, 1)

            def tile(j, p):
                for k in range(ST + 1):
                    if k < ST:
                        q = j * ST + k
                        v.wait_ge(silu_ok, q + 1)
                        v.wait_ge(lo_ok, q + 1)
                        v.tensor_tensor(pr[:, k % 2, :], g[:, k % 2, :], ps[:, UP + k % 2, 0:TW], ALU.mult).then_inc(prod_ok, 1)
                    if k >= 1:
                        q = j * ST + k - 1
                        v.wait_ge(hi_ok, q + 1)
                        v.wait_ge(y_mult, q + ST)
                        v.tensor_tensor(g_lo[:, (k - 1) % 2, :], pr[:, (k - 1) % 2, :], g_hi[:, (k - 1) % 2, :].bitcast(F32),
                                        ALU.subtract).then_inc(lo_ok, 1)
                    if k == 2 and not is_at(j, 0):
                        add_back(j - 1)
                    if 2 <= k < 2 + TC and not is_at(j, 2 * NP - 1):
                        place_row(j + 1, k - 2)
                    if k == 3 + TC and not is_at(j, 2 * NP - 1):
                        rest_x(j + 1, 1 - p)

            for c in range(TC):
                place_row(0, c)
            rest_x(0, 0)
            all_tiles(v, tile)
            add_back(2 * NP - 1)


def routed_experts(nc, io, h, out, x_sorted, y_sorted, place, tile_expert, w_gu, ident):
    with ExitStack() as ctx:
        def sb(name, shape, dt=F32):
            return ctx.enter_context(nc.sbuf_tensor("ex_" + name, shape, dt))

        def sem(name):
            return ctx.enter_context(nc.semaphore("ex_" + name))

        U = 6
        XS = 3
        NGATHER = 6
        TG = NT // NGATHER
        w_d = sb("w_d", [128, NEXP, EF // 128, D])
        x = sb("x", [ROWS, XS, D])
        x_t = sb("x_t", [128, 2, KC, ROWS])
        g = sb("g", [ROWS, 2, EF])
        pr = sb("pr", [ROWS, 2, EF])
        pr_t = sb("pr_t", [128, 2, EF // 128, ROWS])
        y = sb("y", [ROWS, G_TILES, D])
        y_rows = sb("y_rows", [CHUNK, NT, D])
        ps = ctx.enter_context(nc.psum_tensor("ex_ps", [128, 8, 512], F32))
        XT, GU, PT, Y = 0, 2, 4, 6
        w_loaded, x_turned, x_t_ok, gu_mult, silu_ok = sem("w_loaded"), sem("x_turned"), sem("x_t_ok"), sem("gu_mult"), sem("silu_ok")
        x_loaded = [sem(f"x_loaded{u}") for u in range(XS)]
        prod_ok, p_turned, p_t_ok, y_mult, y_ok, y_stored = (sem("prod_ok"), sem("p_turned"), sem("p_t_ok"), sem("y_mult"),
                                                             sem("y_ok"), sem("y_stored"))
        gathered = [sem(f"gathered{n}") for n in range(NGATHER)]
        h_ok, out_stored = sem("h_ok"), sem("out_stored")
        block = ctx.enter_context(nc.Block())

        def is_at(q, n):
            return isinstance(q, int) and q == n

        def all_tiles(eng, body):
            for u in range(U):
                body(0, u)
            with eng.Fori(1, G_TILES // U - 1) as i:
                for u in range(U):
                    body(i, u)
            for u in range(U):
                body(G_TILES // U - 1, u)

        @block.sync
        def _(sp):
            with sp.Fori(0, G_TILES // U) as i:
                for u in range(U):
                    q = i * U + u
                    sp.wait_ge(x_turned, q + 1)
                    sp.dma_start(x[:, u % XS, :], x_sorted[ds(q * ROWS, ROWS), :]).then_inc(x_loaded[u % XS], 16)
            for n in range(NGATHER):
                sp.wait_ge(h_ok, n + 1)
                sp.dma_start(out.rearrange("c (j p) d -> p (c j) d", p=CHUNK)[:, TG * n:TG * n + TG, :],
                             h[:, TG * n:TG * n + TG, :]).then_inc(out_stored, 16)
            sp.wait_ge(out_stored, 16 * NGATHER)

        @block.gpsimd
        def _(gp):
            gp.dma_start(w_d[:], io["ex_d"]).then_inc(w_loaded, 16)
            with gp.Fori(0, G_TILES // U) as i:
                for u in range(U):
                    q = i * U + u
                    gp.wait_ge(y_ok, q + 3)
                    gp.dma_start(y_sorted[ds(q * ROWS, ROWS), :], y[:, ds(q, 1), :].rearrange("p o d -> p (o d)")).then_inc(y_stored, 16)
            gp.wait_ge(y_stored, 16 * G_TILES)
            for t in range(NT):
                gp.indirect_dma_start(y_rows[:, t, :], None, y_sorted,
                                      bass.IndirectOffsetOnAxis(ap=place[:, t:t + 1].bitcast(U32), axis=0)).then_inc(gathered[t // TG], 16)

        @block.tensor
        def _(pe):
            for s, n in ((x_turned, XS), (gu_mult, 2), (p_turned, 2), (y_mult, 2)):
                pe.sem_inc(s, n)

            def expert(q):
                return pe.value_load(tile_expert[0:1, ds(q, 1)], min_val=0, max_val=NEXP - 1)

            def turn_x(q, u, loads):
                pe.wait_ge(x_loaded[u % XS], loads * 16)
                pe.wait_ge(x_t_ok, q + 1)
                for k in range(KC):
                    mm = pe.transpose(ps[:, XT + u % 2, ROWS * k:ROWS * k + ROWS], x[:, u % XS, 128 * k:128 * k + 128], ident[:])
                mm.then_inc(x_turned, 1)

            def gate_up(q, u, e):
                pe.wait_ge(x_t_ok, q + 3)
                pe.wait_ge(prod_ok, q + 1)
                for k in range(KC):
                    mm = pe.matmul(ps[0:ROWS, GU + u % 2, :], x_t[:, u % 2, k, :],
                                   w_gu[:, ds(e, 1), k, :].rearrange("p o f -> p (o f)"), start=(k == 0), stop=(k == KC - 1))
                mm.then_inc(gu_mult, 1)

            def turn_prod(q, u):
                pe.wait_ge(prod_ok, q + 3)
                pe.wait_ge(p_t_ok, q + 1)
                for k in range(EF // 128):
                    mm = pe.transpose(ps[:, PT + u % 2, ROWS * k:ROWS * k + ROWS], pr[:, u % 2, 128 * k:128 * k + 128], ident[:])
                mm.then_inc(p_turned, 1)

            def down(q, u, e):
                pe.wait_ge(p_t_ok, q + 3)
                pe.wait_ge(y_ok, q + 1)
                for k in range(EF // 128):
                    mm = pe.matmul(ps[0:ROWS, Y + u % 2, 0:D], pr_t[:, u % 2, k, :],
                                   w_d[:, ds(e, 1), k, :].rearrange("p o d -> p (o d)"), start=(k == 0), stop=(k == EF // 128 - 1))
                mm.then_inc(y_mult, 1)

            fetched = {}

            def body(i, u):
                q = i * U + u
                if u == 0:
                    fetched.clear()
                    fetched[0] = expert(q)
                if not is_at(q, 0):
                    turn_prod(q - 1, u - 1)
                gate_up(q, u, fetched[u])
                if u == 0 and not is_at(q, 0):
                    fetched[-1] = expert(q - 1)
                if u < U - 1:
                    fetched[u + 1] = expert(q + 1)
                if not is_at(q, G_TILES - 1):
                    turn_x(q + 1, u + 1, i * (U // XS) + (u + 1) // XS + 1)
                if not is_at(q, 0):
                    down(q - 1, u - 1, fetched[u - 1])

            turn_x(0, 0, 1)
            pe.wait_ge(w_loaded, 16)
            all_tiles(pe, body)
            turn_prod(G_TILES - 1, U - 1)
            down(G_TILES - 1, U - 1, fetched[U - 1])

        @block.scalar
        def _(act):
            for s, n in ((x_t_ok, 2), (p_t_ok, 2)):
                act.sem_inc(s, n)

            def keep_x(q, u):
                act.wait_ge(x_turned, q + 1 + XS)
                act.wait_ge(gu_mult, q + 1)
                nc.scalar.copy(x_t[:, u % 2].rearrange("p k t -> p (k t)"), ps[:, XT + u % 2, 0:KC * ROWS]).then_inc(x_t_ok, 1)

            def keep_prod(q, u):
                act.wait_ge(p_turned, q + 3)
                act.wait_ge(y_mult, q + 1)
                nc.scalar.copy(pr_t[:, u % 2].rearrange("p k t -> p (k t)"), ps[:, PT + u % 2, 0:EF]).then_inc(p_t_ok, 1)

            def body(i, u):
                q = i * U + u
                if not is_at(q, 0):
                    keep_prod(q - 1, u - 1)
                act.wait_ge(gu_mult, q + 3)
                act.wait_ge(prod_ok, q + 1)
                nc.scalar.activation(g[:, u % 2, :], ps[0:ROWS, GU + u % 2, 0:EF], ACT.Silu).then_inc(silu_ok, 1)
                if not is_at(q, G_TILES - 1):
                    keep_x(q + 1, u + 1)

            keep_x(0, 0)
            all_tiles(act, body)
            keep_prod(G_TILES - 1, U - 1)

        @block.vector
        def _(v):
            for s, n in ((prod_ok, 2), (y_ok, 2)):
                v.sem_inc(s, n)

            def keep_y(q, u):
                v.wait_ge(y_mult, q + 3)
                v.tensor_copy(y[:, ds(q, 1), :].rearrange("p o d -> p (o d)"), ps[0:ROWS, Y + u % 2, 0:D]).then_inc(y_ok, 1)

            def body(i, u):
                q = i * U + u
                v.wait_ge(silu_ok, q + 1)
                v.wait_ge(p_turned, q + 1)
                v.tensor_tensor(pr[:, u % 2, :], g[:, u % 2, :], ps[0:ROWS, GU + u % 2, EF:2 * EF], ALU.mult).then_inc(prod_ok, 1)
                if not is_at(q, 0):
                    keep_y(q - 1, u - 1)

            all_tiles(v, body)
            keep_y(G_TILES - 1, U - 1)
            for n in range(NGATHER):
                v.wait_ge(gathered[n], 16 * TG)
                part = h[:, TG * n:TG * n + TG, :]
                v.tensor_tensor(part, part, y_rows[:, TG * n:TG * n + TG, :], ALU.add).then_inc(h_ok, 1)


def build(nc, io, out):
    with ExitStack() as ctx:
        h = ctx.enter_context(nc.sbuf_tensor("h", [CHUNK, NT, D], F32))
        h_stats = ctx.enter_context(nc.sbuf_tensor("h_stats", [CHUNK, NT, 6], F32))
        ident = ctx.enter_context(nc.sbuf_tensor("ident", [128, 128], F32))
        ident_ready = ctx.enter_context(nc.semaphore("ident_ready"))
        mx_sorted, my_sorted = ([nc.dram_tensor(f"m{n}_sorted{grp}", (SORTED, D), F32, kind="Internal").ap()
                                 for grp in range(NG2)] for n in "xy")
        x_sorted = nc.dram_tensor("x_sorted", (G_TILES * ROWS, D), F32, kind="Internal").ap()
        y_sorted = nc.dram_tensor("y_sorted", (G_TILES * ROWS, D), F32, kind="Internal").ap()
        embed(nc, io, h, ident, ident_ready)
        with nc.sbuf_tensor("x0_t", [128, KC, T], F32) as x_t:
            normalise(nc, "n0", h, x_t, ident, ident_ready)
            linear_attention(nc, io, h, h_stats, x_t, mx_sorted + [x_sorted], ident, ident_ready)
        h_dram = nc.dram_tensor("h_rows", (CHUNK, NT, D), F32, kind="Internal").ap()
        bias_dram = nc.dram_tensor("bias_parts", (2, EXPERTS * (FF + D)), F32, kind="Internal").ap()
        recursive_mixture(nc, io, h, h_stats, mx_sorted, my_sorted, h_dram, bias_dram, ident)
        with nc.sbuf_tensor("x2_t", [128, KC, T], F32) as x_t:
            normalise(nc, "n2", h, x_t, ident, ident_ready, h_stats)
            retention(nc, io, h, x_t, ident)
        place = ctx.enter_context(nc.sbuf_tensor("place", [CHUNK, NT], I32))
        tile_expert = ctx.enter_context(nc.sbuf_tensor("tile_expert", [CHUNK, G_TILES], I32))
        w_gu = ctx.enter_context(nc.sbuf_tensor("ex_w_gu", [128, NEXP, KC, 2 * EF], F32))
        route_and_share(nc, io, h, x_sorted, place, tile_expert, w_gu, ident)
        routed_experts(nc, io, h, out, x_sorted, y_sorted, place, tile_expert, w_gu, ident)


def host_arrays(inputs):
    import numpy as np
    f = lambda n: np.asarray(inputs[n])

    def pairs(w):
        return w.reshape(w.shape[0] // 128, 128, -1).transpose(1, 0, 2)

    io = {
        "x": f("x").transpose(3, 2, 0, 1), "log_dt": f("L0_tok_log_dt"), "inv_A_real": f("L0_tok_inv_A_real").T,
        "A_imag": f("L0_tok_A_imag").T, "B_ri": f("L0_tok_B_ri").transpose(2, 1, 0),
        "sign": np.repeat(np.array([[1.0], [-1.0]], np.float32), MODES, axis=0),
        "x_txt": f("x_txt").T, "W_txt": np.concatenate([f("L0_txt_W0"), f("L0_txt_W1"), f("L0_txt_W2")]).reshape(3, 128, D).transpose(1, 0, 2),
        "E0": f("L0_txt_E0"), "E1": f("L0_txt_E1"), "E2": f("L0_txt_E2"),
        "la_w_qv": pairs(np.concatenate([f("L0_attn_Wq").T, f("L0_attn_Wv").T], axis=1)),
        "la_w_k": pairs(f("L0_attn_Wk").T), "la_w_o": pairs(f("L0_attn_Wo").T),
        "la_b_qv": np.concatenate([f("L0_attn_bq"), f("L0_attn_bv")])[None], "la_b_o": f("L0_attn_bo")[None],
        "la_cols": np.stack([f("L0_attn_bk"), f("L0_attn_ln_g"), f("L0_attn_ln_b")]).reshape(3, KC, 128).transpose(2, 0, 1),
        "head_mask": np.kron(np.eye(8, dtype=np.float32), np.ones((16, 16), np.float32)),
        "mo_w": np.concatenate([
            f("L0_ffn_W1").reshape(EXPERTS, KC, 128, FF).transpose(2, 0, 1, 3).reshape(128, -1),
            f("L0_ffn_W2").reshape(EXPERTS, FT, 128, D).transpose(2, 0, 1, 3).reshape(128, -1)], axis=1),
        "mo_w_g": f("L0_ffn_Wg").reshape(ROUNDS, KC, 128, EXPERTS).transpose(2, 1, 0, 3), "mo_b_g": f("L0_ffn_bg")[None],
        "mo_b": np.concatenate([f("L0_ffn_b1"), f("L0_ffn_b2")], axis=1).reshape(128, -1),
        "mo_numbers": np.arange(MT, dtype=np.float32)[None],
        "mo_keep": (np.arange(EXPERTS * GT) % GT != 0).astype(np.float32)[None],
        "before": np.stack([np.tri(EXPERTS, k=-1), np.tri(EXPERTS, k=-1).T]).astype(np.float32)[None],
        "re_w": pairs(np.concatenate([f("L1_attn_W" + n) for n in "qkvg"], axis=1)), "re_w_o": pairs(f("L1_attn_Wo")),
        "re_bias": np.concatenate([f("L1_attn_b" + n) for n in "qkvg"])[None],
        "re_rows3": np.stack([f("L1_attn_bo"), f("L1_attn_gamma"), f("L1_attn_beta")])[None],
        "decay": np.stack([0.25 * 0.99 ** np.arange(S), 0.99 ** -np.arange(S).astype(np.float64)], axis=1)
        .astype(np.float32).reshape(NCH, CHUNK, 2).transpose(1, 0, 2),
        "causal": np.tri(CHUNK, dtype=np.float32).T, "head_of": np.kron(np.eye(8, dtype=np.float32), np.ones((16, 1), np.float32)),
        "router": pairs(f("L1_ffn_router_w").T), "early": np.tri(CHUNK, k=-1, dtype=np.float32).T,
        "keep": (np.arange(NEXP * NT) % NT != 0).astype(np.float32)[None],
        "numbers": np.concatenate([np.arange(NEXP) - NEXP, np.arange(G_TILES)]).astype(np.float32)[None],
        "sh_w": np.concatenate([
            np.stack([f("L1_ffn_shared_gate_w"), f("L1_ffn_shared_up_w")]).reshape(2, ST, 128, KC, 128)
            .transpose(4, 1, 0, 3, 2).reshape(128, -1),
            f("L1_ffn_shared_down_w").T.reshape(ST, 128, D).transpose(1, 0, 2).reshape(128, -1)], axis=1),
        "ex_gu": f("L1_ffn_gate_up_proj").reshape(NEXP, KC, 128, 2 * EF).transpose(2, 0, 1, 3),
        "ex_d": f("L1_ffn_down_proj").reshape(NEXP, EF // 128, 128, D).transpose(2, 0, 1, 3),
        "ident": np.eye(128, dtype=np.float32),
    }
    return {k: np.ascontiguousarray(v) for k, v in io.items()}


def kernel(**inputs):
    import concourse.bacc as _bacc
    from concourse.bass_utils import run_bass_kernel_spmd as _run

    nc = _bacc.Bacc("TRN2", target_bir_lowering=False, num_devices=1)
    arrays, io = {}, {}
    for name, a in host_arrays(inputs).items():
        arrays[f"in_{name}_dram"] = a
        io[name] = nc.dram_tensor(f"in_{name}_dram", a.shape, mybir.dt.from_np(a.dtype), kind="ExternalInput").ap()
    out = nc.dram_tensor("out_0_dram", (B, S, D), F32, kind="ExternalOutput").ap()
    build(nc, io, out)
    r = _run(nc, [arrays], core_ids=[0])
    return r.results[0]["out_0_dram"]
```
